# Optimizing a Trainium2 kernel written in Bass

```python
import numpy as np
import jax
import jax.numpy as jnp

def _softmax(x, axis=-1):
    return jax.nn.softmax(x, axis=axis)

def _gelu(x):
    return jax.nn.gelu(x, approximate=True)

def _silu(x):
    return jax.nn.silu(x)

def _sigmoid(x):
    return jax.nn.sigmoid(x)

def _layernorm(x, axis=-1, eps=1e-05):
    m = jnp.mean(x, axis=axis, keepdims=True)
    v = jnp.var(x, axis=axis, keepdims=True)
    return (x - m) / jnp.sqrt(v + eps)

def _scatter_add(tgt, idx, src, axis=0):
    return tgt.at[idx].add(src)

def _segment_sum(src, seg, n):
    return jax.ops.segment_sum(src, seg, n)
kernel_name = 'mk_seq_preln_d2_jaxref_r8_fc35a2'

def setup_inputs(seed: int=0):
    np.random.seed(seed)
    _w = jnp.asarray

    def _L0_attn_setup():
        import jax, jax.numpy as jnp
        import numpy as np
        import math
        EMBED_DIM = 256
        NUM_HEADS = 16
        HEAD_DIM = EMBED_DIM // NUM_HEADS
        ROPE_BASE = 10000.0

        def apply_rope(x):
            B, S, H, D = x.shape
            half = D // 2
            positions = jnp.arange(S, dtype=x.dtype)
            inv_freq = 1.0 / ROPE_BASE ** (jnp.arange(0, D, 2, dtype=x.dtype) / D)
            angles = positions[:, None] * inv_freq[None, :]
            sin = jnp.sin(angles)[None, :, None, :]
            cos = jnp.cos(angles)[None, :, None, :]
            x1, x2 = (x[..., :half], x[..., half:])
            return jnp.concatenate([x1 * cos - x2 * sin, x1 * sin + x2 * cos], axis=-1)
        key = jax.random.key(seed)
        ks = jax.random.split(key, 5)
        B, S, E = (2, 256, EMBED_DIM)
        scale = 1.0 / math.sqrt(E)
        return {'x': jax.random.normal(ks[0], (B, S, E), dtype=jnp.float32), 'wq': jax.random.normal(ks[1], (E, E), dtype=jnp.float32) * scale, 'wk': jax.random.normal(ks[2], (E, E), dtype=jnp.float32) * scale, 'wv': jax.random.normal(ks[3], (E, E), dtype=jnp.float32) * scale, 'wo': jax.random.normal(ks[4], (E, E), dtype=jnp.float32) * scale}
    _L0_attn_in = _L0_attn_setup()

    def _L0_ffn_setup():
        import jax, jax.numpy as jnp
        import numpy as np
        HIDDEN = 256
        INTER = 1024
        BATCH, LOCAL_SEQ = (2, 512)
        key = jax.random.key(seed)
        k1, k2, k3 = jax.random.split(key, 3)
        h_shard = jax.random.normal(k1, (BATCH, LOCAL_SEQ, HIDDEN), dtype=jnp.float32)
        w_gate_up = jax.random.normal(k2, (2 * INTER, HIDDEN), dtype=jnp.float32) * 0.02
        w_down = jax.random.normal(k3, (HIDDEN, INTER), dtype=jnp.float32) * 0.02
        return {'h_shard': h_shard, 'w_gate_up': w_gate_up, 'w_down': w_down}
    _L0_ffn_in = _L0_ffn_setup()

    def _L1_attn_setup():
        import jax, jax.numpy as jnp
        import numpy as np
        N_Q, N_KV = (16, 4)

        def _rope(x):
            d = x.shape[-1]
            T = x.shape[-2]
            inv_freq = 1.0 / 10000.0 ** (jnp.arange(d // 2, dtype=jnp.float32) * 2.0 / d)
            emb = jnp.arange(T, dtype=jnp.float32)[:, None] * inv_freq[None, :]
            cos, sin = (jnp.cos(emb), jnp.sin(emb))
            x1, x2 = (x[..., 0::2], x[..., 1::2])
            return jnp.concatenate([x1 * cos - x2 * sin, x1 * sin + x2 * cos], axis=-1)
        key = jax.random.key(seed)
        ks = jax.random.split(key, 5)
        B, T, C = (4, 256, 256)
        g = N_Q // N_KV
        Ckv = C // g
        s = 0.02
        return {'x': jax.random.normal(ks[0], (B, T, C), dtype=jnp.float32), 'Wq': jax.random.normal(ks[1], (C, C), dtype=jnp.float32) * s, 'bq': jnp.zeros((C,), dtype=jnp.float32), 'Wk': jax.random.normal(ks[2], (C, Ckv), dtype=jnp.float32) * s, 'bk': jnp.zeros((Ckv,), dtype=jnp.float32), 'Wv': jax.random.normal(ks[3], (C, Ckv), dtype=jnp.float32) * s, 'bv': jnp.zeros((Ckv,), dtype=jnp.float32), 'Wo': jax.random.normal(ks[4], (Ckv, C), dtype=jnp.float32) * s, 'bo': jnp.zeros((C,), dtype=jnp.float32)}
    _L1_attn_in = _L1_attn_setup()

    def _L1_ffn_setup():
        import jax, jax.numpy as jnp
        import numpy as np
        TOP_K = 2
        key = jax.random.key(seed)
        ks = jax.random.split(key, 5)
        B, T, D, E, H = (4, 256, 256, 8, 176)
        s = 1.0 / np.sqrt(D)
        sh = 1.0 / np.sqrt(H)
        return {'x': jax.random.normal(ks[0], (B, T, D), dtype=jnp.float32), 'Wg': jax.random.normal(ks[1], (E, D), dtype=jnp.float32) * s, 'W1': jax.random.normal(ks[2], (E, H, D), dtype=jnp.float32) * s, 'W2': jax.random.normal(ks[3], (E, H, D), dtype=jnp.float32) * s, 'W3': jax.random.normal(ks[4], (E, D, H), dtype=jnp.float32) * sh}
    _L1_ffn_in = _L1_ffn_setup()
    _d = {'L0_attn_x': _L0_attn_in['x'], 'L0_attn_wq': _L0_attn_in['wq'], 'L0_attn_wk': _L0_attn_in['wk'], 'L0_attn_wv': _L0_attn_in['wv'], 'L0_attn_wo': _L0_attn_in['wo'], 'L0_ffn_w_gate_up': _L0_ffn_in['w_gate_up'], 'L0_ffn_w_down': _L0_ffn_in['w_down'], 'L1_attn_Wq': _L1_attn_in['Wq'], 'L1_attn_bq': _L1_attn_in['bq'], 'L1_attn_Wk': _L1_attn_in['Wk'], 'L1_attn_bk': _L1_attn_in['bk'], 'L1_attn_Wv': _L1_attn_in['Wv'], 'L1_attn_bv': _L1_attn_in['bv'], 'L1_attn_Wo': _L1_attn_in['Wo'], 'L1_attn_bo': _L1_attn_in['bo'], 'L1_ffn_Wg': _L1_ffn_in['Wg'], 'L1_ffn_W1': _L1_ffn_in['W1'], 'L1_ffn_W2': _L1_ffn_in['W2'], 'L1_ffn_W3': _L1_ffn_in['W3']}
    _x0 = _d['L0_attn_x']
    _d['L0_attn_x'] = jax.random.normal(jax.random.fold_in(jax.random.key(seed), 1), (16, 256, 256), dtype=_x0.dtype)
    del _x0
    return _d

def reference(L0_attn_x, L0_attn_wq, L0_attn_wk, L0_attn_wv, L0_attn_wo, L0_ffn_w_gate_up, L0_ffn_w_down, L1_attn_Wq, L1_attn_bq, L1_attn_Wk, L1_attn_bk, L1_attn_Wv, L1_attn_bv, L1_attn_Wo, L1_attn_bo, L1_ffn_Wg, L1_ffn_W1, L1_ffn_W2, L1_ffn_W3):

    def _L0_attn_ref(x, wq, wk, wv, wo):
        import jax, jax.numpy as jnp
        import numpy as np
        import math
        EMBED_DIM = 256
        NUM_HEADS = 16
        HEAD_DIM = EMBED_DIM // NUM_HEADS
        ROPE_BASE = 10000.0

        def apply_rope(x):
            B, S, H, D = x.shape
            half = D // 2
            positions = jnp.arange(S, dtype=x.dtype)
            inv_freq = 1.0 / ROPE_BASE ** (jnp.arange(0, D, 2, dtype=x.dtype) / D)
            angles = positions[:, None] * inv_freq[None, :]
            sin = jnp.sin(angles)[None, :, None, :]
            cos = jnp.cos(angles)[None, :, None, :]
            x1, x2 = (x[..., :half], x[..., half:])
            return jnp.concatenate([x1 * cos - x2 * sin, x1 * sin + x2 * cos], axis=-1)
        B, S, E = x.shape
        H, D = (NUM_HEADS, HEAD_DIM)
        q = (x @ wq).reshape(B, S, H, D)
        k = (x @ wk).reshape(B, S, H, D)
        v = (x @ wv).reshape(B, S, H, D)
        q = apply_rope(q)
        k = apply_rope(k)
        scores = jnp.einsum('bqhd,bkhd->bhqk', q, k) / math.sqrt(D)
        causal = jnp.triu(jnp.full((S, S), -jnp.inf, dtype=x.dtype), k=1)
        scores = scores + causal[None, None, :, :]
        attn = jax.nn.softmax(scores, axis=-1)
        out = jnp.einsum('bhqk,bkhd->bqhd', attn, v).reshape(B, S, E)
        return out @ wo

    def _L0_ffn_ref(h_shard, w_gate_up, w_down):
        import jax, jax.numpy as jnp
        import numpy as np
        HIDDEN = 256
        INTER = 1024
        BATCH, LOCAL_SEQ = (2, 512)
        batch, local_seq, hidden = h_shard.shape
        gate_up = jnp.einsum('bsh,oh->bso', h_shard, w_gate_up)
        gate, up = jnp.split(gate_up, 2, axis=-1)
        h = jax.nn.silu(gate) * up
        out = jnp.einsum('bsi,hi->bsh', h, w_down)
        return out

    def _L1_attn_ref(x, Wq, bq, Wk, bk, Wv, bv, Wo, bo):
        import jax, jax.numpy as jnp
        import numpy as np
        N_Q, N_KV = (16, 4)

        def _rope(x):
            d = x.shape[-1]
            T = x.shape[-2]
            inv_freq = 1.0 / 10000.0 ** (jnp.arange(d // 2, dtype=jnp.float32) * 2.0 / d)
            emb = jnp.arange(T, dtype=jnp.float32)[:, None] * inv_freq[None, :]
            cos, sin = (jnp.cos(emb), jnp.sin(emb))
            x1, x2 = (x[..., 0::2], x[..., 1::2])
            return jnp.concatenate([x1 * cos - x2 * sin, x1 * sin + x2 * cos], axis=-1)
        B, T, C = x.shape
        g = N_Q // N_KV
        d = C // N_Q
        q = (x @ Wq + bq).reshape(B, T, N_Q, d).transpose(0, 2, 1, 3)
        k = (x @ Wk + bk).reshape(B, T, N_KV, d).transpose(0, 2, 1, 3)
        v = (x @ Wv + bv).reshape(B, T, N_KV, d).transpose(0, 2, 1, 3)
        q = _rope(q)
        k = _rope(k)
        qg = q.reshape(B, N_KV, g, T, d)
        scores = jnp.einsum('bhgnd,bhsd->bhns', qg, k) * (1.0 / jnp.sqrt(jnp.float32(d)))
        mask = jnp.tril(jnp.ones((T, T), dtype=bool))
        att = jax.nn.softmax(jnp.where(mask, scores, -jnp.inf), axis=-1)
        y = jnp.einsum('bhns,bhsd->bhnd', att, v)
        y = y.transpose(0, 2, 1, 3).reshape(B, T, C // g)
        return y @ Wo + bo

    def _L1_ffn_ref(x, Wg, W1, W2, W3):
        import jax, jax.numpy as jnp
        import numpy as np
        TOP_K = 2
        E = Wg.shape[0]
        scores = jnp.einsum('btd,ed->bte', x, Wg)
        topk_s, topk_i = jax.lax.top_k(scores, TOP_K)
        probs = jax.nn.softmax(topk_s, axis=-1)
        onehot = (topk_i[..., None] == jnp.arange(E)).astype(x.dtype)
        w = jnp.einsum('btk,btke->bte', probs, onehot)
        y = jnp.zeros_like(x)
        for e in range(E):
            h = jax.nn.silu(jnp.einsum('btd,hd->bth', x, W1[e])) * jnp.einsum('btd,hd->bth', x, W2[e])
            y = y + w[..., e:e + 1] * jnp.einsum('bth,dh->btd', h, W3[e])
        return y
    x = L0_attn_x
    x = x + _L0_attn_ref(_layernorm(x, axis=-1), L0_attn_wq, L0_attn_wk, L0_attn_wv, L0_attn_wo)
    x = x + _L0_ffn_ref(_layernorm(x, axis=-1), L0_ffn_w_gate_up, L0_ffn_w_down)
    x = x + _L1_attn_ref(_layernorm(x, axis=-1), L1_attn_Wq, L1_attn_bq, L1_attn_Wk, L1_attn_bk, L1_attn_Wv, L1_attn_bv, L1_attn_Wo, L1_attn_bo)
    x = x + _L1_ffn_ref(_layernorm(x, axis=-1), L1_ffn_Wg, L1_ffn_W1, L1_ffn_W2, L1_ffn_W3)
    return x

_drawn_inputs = setup_inputs


def setup_inputs(seed=0):
    import zlib

    import numpy as np

    out = dict(_drawn_inputs(seed))
    spreads = {'L1_attn_bq': (0.0, 0.8),
     'L1_attn_bk': (0.0, 0.8),
     'L1_attn_bv': (0.0, 0.1),
     'L1_attn_bo': (0.0, 0.1)}
    factors = {'L1_attn_Wq': 8.0, 'L1_attn_Wk': 7.202}
    for name, (base, spread) in spreads.items():
        noise = np.random.default_rng([zlib.crc32(name.encode()), seed]).standard_normal(out[name].shape)
        drawn = base * np.exp(spread * noise) if base else spread * noise
        out[name] = jnp.asarray(drawn.astype(out[name].dtype))
    for name, factor in factors.items():
        out[name] = (out[name] * factor).astype(out[name].dtype)
    return out
```

```python
from contextlib import ExitStack

import numpy as np

import concourse.bass as bass
from concourse import mybir

F32 = mybir.dt.float32
F32R = mybir.dt.float32r
BF16 = mybir.dt.bfloat16
ALU = mybir.AluOpType
ACT = mybir.ActivationFunctionType
AX = mybir.AxisListType

P = 128
NSEQ, T, E = 16, 256, 256
NT = T // P
NC = E // P
HD = 16
EPS = 1e-5
MASK = -1e30
INTER0 = 1024
NEXP, HID = 8, 176
INTER1 = NEXP * HID
NB = 8
BT = 4
BN = BT * P
W0 = 3 * E
WB_CHUNK = (2 * INTER0 * NC + INTER0 // P * E) // NSEQ
WD_CHUNK = (2 * INTER1 * NC + INTER1 // P * E) // NSEQ
WMAX = WD_CHUNK * NSEQ


def cols(start, size):
    return bass.ds(start, size)


class Names:
    pass


def live(seq):
    return not isinstance(seq, int) or 0 <= seq < NSEQ


class Attn:

    def __init__(self, layer):
        self.layer = layer
        self.H = 16 if layer == 0 else 4
        self.NG = self.H // 4
        self.HB = min(8, self.H)
        self.NH = self.H // self.HB
        self.U = 3 * self.NG
        self.QC = self.H * HD
        self.RB = 2 if layer == 0 else 1
        self.RH = 16 if layer == 0 else 8
        self.RC = self.RH * HD
        self.NCH = self.RC // P
        self.OE = max(1, self.NG // 2)

    def stack(self, h):
        return 64 * (h // self.HB), h % self.HB

    def unit(self, u):
        g, r = divmod(u, 3)
        return (g, "A", [4 * g + 2 * r, 4 * g + 2 * r + 1]) if r < 2 else (g, "B", [4 * g + i for i in range(4)])


def build(nc, x_in, wqkv0, wo0, w_ff0, wq1, wkv1, bq1, bkv1, wo1, bo1, w_moe, w_gate,
          c_cos, c_sin, c_ident, c_mask, c_tri, c_sel, out):
    ctx = ExitStack()
    with ctx:
        def sb(name, shape, dt=F32):
            return ctx.enter_context(nc.sbuf_tensor(name, shape, dt))

        x = sb("x_res", [P, NSEQ * NT, E])
        wff_hi = sb("wff_hi", [P, WMAX], F32R)
        wff_lo = sb("wff_lo", [P, WMAX], F32R)
        wat_hi = sb("wat_hi", [P, NC * (W0 + E)], F32R)
        wat_lo = sb("wat_lo", [P, NC * (W0 + E)], F32R)
        wstage = sb("wstage", [P, WD_CHUNK])
        cos = sb("cos", [P, NT, HD])
        sin = sb("sin", [P, NT, HD])
        ident = sb("ident", [P, P])
        identb = sb("identb", [P, P], BF16)
        maskb = sb("maskb", [P, 4, P], BF16)
        half = sb("minus_half", [P, BT])
        bias = sb("bias_rows", [64, 2 * E], F32R)
        ones = sb("ones_rows", [64, P], F32R)
        wg_hi = sb("wg_hi", [P, NC * NEXP], F32R)
        wg_lo = sb("wg_lo", [P, NC * NEXP], F32R)
        tri = sb("tri", [P, NEXP, NEXP])
        mv = sb("mv", [P, BT, 2])
        st = sb("st", [P, BT, 6])
        rs = sb("rs", [P, 2, BT])
        nmr = sb("nmr", [P, BT])

        ps = [ctx.enter_context(nc.psum_tensor(f"bank{i}", [P, 512], F32)) for i in range(8)]

        setup = Names()
        setup.tick = ctx.enter_context(nc.semaphore("su_tick"))
        setup.x_first = ctx.enter_context(nc.semaphore("su_x_first"))
        setup.x_rest = ctx.enter_context(nc.semaphore("su_x_rest"))
        setup.w_raw = ctx.enter_context(nc.semaphore("su_w_raw"))
        setup.w_hi = ctx.enter_context(nc.semaphore("su_w_hi"))
        setup.w_lo = ctx.enter_context(nc.semaphore("su_w_lo"))
        setup.const = ctx.enter_context(nc.semaphore("su_const"))
        setup.const_cp = ctx.enter_context(nc.semaphore("su_const_cp"))
        setup.raw1 = ctx.enter_context(nc.semaphore("su_raw1"))
        setup.sum1 = ctx.enter_context(nc.semaphore("su_sum1"))
        setup.hi1 = ctx.enter_context(nc.semaphore("su_hi1"))
        setup.lo1 = ctx.enter_context(nc.semaphore("su_lo1"))
        setup.wg = ctx.enter_context(nc.semaphore("su_wg"))
        phase = Names()
        phase.done = ctx.enter_context(nc.semaphore("ph_done"))
        wf = Names()
        wf.in0 = ctx.enter_context(nc.semaphore("wf_in0"))
        wf.hi0 = ctx.enter_context(nc.semaphore("wf_hi0"))
        wf.lo0 = ctx.enter_context(nc.semaphore("wf_lo0"))
        wf.in1 = ctx.enter_context(nc.semaphore("wf_in1"))
        wf.hi1 = ctx.enter_context(nc.semaphore("wf_hi1"))
        wf.lo1 = ctx.enter_context(nc.semaphore("wf_lo1"))
        dram = [nc.dram_tensor(f"scr{b}{p}", [2, 2 * P, T], F32, kind="Internal").ap() for b in range(2) for p in range(2)]
        dram_m = [nc.dram_tensor(f"scrm{p}", [16, 2, T], F32, kind="Internal").ap() for p in range(2)]

        def wqkv_at(w, layer, c, c0, n):
            base = c * W0 if layer == 0 else c * E
            return w[:, base + c0:base + c0 + n]

        def wo_at(w, layer, c):
            base = NC * W0 + c * E if layer == 0 else NC * E
            return w[0:P if layer == 0 else 64, base:base + E]

        def end_of_phase(eng, n):
            eng.drain().then_inc(phase.done, 1)
            eng.wait_ge(phase.done, 5 * n)

        def plain(eng):
            eng.sem_inc(setup.tick, 1)

        def attention(L, region, block_no):
            A = Attn(L)
            H, NG, HB, U, QC = A.H, A.NG, A.HB, A.U, A.QC
            R = region
            S = Names()
            S.ln_st = ctx.enter_context(nc.semaphore(f"a{L}_ln_st"))
            S.ln_mv = ctx.enter_context(nc.semaphore(f"a{L}_ln_mv"))
            S.ln_rs = ctx.enter_context(nc.semaphore(f"a{L}_ln_rs"))
            S.xn = ctx.enter_context(nc.semaphore(f"a{L}_xn"))
            S.xT_ps = ctx.enter_context(nc.semaphore(f"a{L}_xT_ps"))
            S.xT_hi = ctx.enter_context(nc.semaphore(f"a{L}_xT_hi"))
            S.xT_lo = ctx.enter_context(nc.semaphore(f"a{L}_xT_lo"))
            S.qk_ps = ctx.enter_context(nc.semaphore(f"a{L}_qk_ps"))
            S.v_ps = ctx.enter_context(nc.semaphore(f"a{L}_v_ps"))
            S.v_sb = ctx.enter_context(nc.semaphore(f"a{L}_v_sb"))
            S.rope_t = ctx.enter_context(nc.semaphore(f"a{L}_rope_t"))
            S.r_ok = ctx.enter_context(nc.semaphore(f"a{L}_r_ok"))
            S.qkT_ps = ctx.enter_context(nc.semaphore(f"a{L}_qkT_ps"))
            S.qkT_hi = ctx.enter_context(nc.semaphore(f"a{L}_qkT_hi"))
            S.qkT_lo = ctx.enter_context(nc.semaphore(f"a{L}_qkT_lo"))
            S.q_out = ctx.enter_context(nc.semaphore(f"a{L}_q_out"))
            S.k_out = ctx.enter_context(nc.semaphore(f"a{L}_k_out"))
            S.half0 = ctx.enter_context(nc.semaphore(f"a{L}_half0"))
            S.half1 = ctx.enter_context(nc.semaphore(f"a{L}_half1"))
            S.rows_ps = ctx.enter_context(nc.semaphore(f"a{L}_rows_ps"))
            S.mx = ctx.enter_context(nc.semaphore(f"a{L}_mx"))
            S.m_ps = ctx.enter_context(nc.semaphore(f"a{L}_m_ps"))
            S.m_hi = ctx.enter_context(nc.semaphore(f"a{L}_m_hi"))
            S.m_lo = ctx.enter_context(nc.semaphore(f"a{L}_m_lo"))
            S.m_out = ctx.enter_context(nc.semaphore(f"a{L}_m_out"))
            S.m_in = ctx.enter_context(nc.semaphore(f"a{L}_m_in"))
            S.main_ps = ctx.enter_context(nc.semaphore(f"a{L}_main_ps"))
            S.ex = ctx.enter_context(nc.semaphore(f"a{L}_ex"))
            S.cz = ctx.enter_context(nc.semaphore(f"a{L}_cz"))
            S.av = ctx.enter_context(nc.semaphore(f"a{L}_av"))
            S.o_sb = ctx.enter_context(nc.semaphore(f"a{L}_o_sb"))
            S.oN_ps = ctx.enter_context(nc.semaphore(f"a{L}_oN_ps"))
            S.rinv = ctx.enter_context(nc.semaphore(f"a{L}_rinv"))
            S.on_sb = ctx.enter_context(nc.semaphore(f"a{L}_on_sb"))
            S.oT_ps = ctx.enter_context(nc.semaphore(f"a{L}_oT_ps"))
            S.oT_hi = ctx.enter_context(nc.semaphore(f"a{L}_oT_hi"))
            S.oT_lo = ctx.enter_context(nc.semaphore(f"a{L}_oT_lo"))
            S.o_ps = ctx.enter_context(nc.semaphore(f"a{L}_o_ps"))
            S.xr = ctx.enter_context(nc.semaphore(f"a{L}_xr"))
            scrq, scrk = dram[0:2], dram[2:4]

            def split_mm(pe, out_, lhs, rhs, start, stop):
                pe.matmul(out_, lhs[0], rhs[0], start=start, stop=False)
                pe.matmul(out_, lhs[0], rhs[1], start=False, stop=False)
                return pe.matmul(out_, lhs[1], rhs[0], start=False, stop=stop)

            def pe_xT(pe, s, bank):
                pe.wait_ge(S.xn, s * 2 + 2)
                for c in range(NC):
                    for j in range(NT):
                        mm = pe.transpose(ps[bank][:, c * T + j * P:c * T + (j + 1) * P],
                                          R.xn[:, j, c * P:(c + 1) * P], ident[:, :])
                mm.then_inc(S.xT_ps, 1)

            def pe_proj(pe, s, p, bank, c0, n, signal):
                pe.wait_ge(S.xT_lo, s + 1)
                for j in range(NT):
                    o = ps[bank][:, j * T:j * T + n]
                    if L == 1:
                        pe.matmul(o, ones[:, :], bias[:, 0:n], start=True, stop=False)
                    for c in range(NC):
                        xs = [t[:, p, c * T + j * P:c * T + (j + 1) * P] for t in (R.xT_hi, R.xT_lo)]
                        ws = [wqkv_at(w, L, c, c0, n) for w in (wat_hi, wat_lo)]
                        mm = split_mm(pe, o, xs, ws, start=(c == 0 and L == 0), stop=(c == NC - 1))
                mm.then_inc(signal, 1)

            def pe_qkT(pe, s, b, bank):
                pe.wait_ge(S.r_ok, s * A.RB + b + 1)
                for c in range(A.NCH):
                    for j in range(NT):
                        mm = pe.transpose(ps[bank][:, c * T + j * P:c * T + (j + 1) * P],
                                          R.rot[:, b, j, c * P:(c + 1) * P], ident[:, :])
                mm.then_inc(S.qkT_ps, 1)

            def pe_rows(pe, s, p, u):
                g, kind, heads = A.unit(u)
                bank = (U * p + u) % 2
                if heads[0] < HB:
                    pe.wait_ge(S.half0, s * 96 + 96)
                if heads[-1] >= HB:
                    pe.wait_ge(S.half1, s * 96 + 96)
                if not (isinstance(s, int) and U * s + u < 2):
                    pe.wait_ge(S.mx, s * U + (u - 1))
                if kind == "A":
                    o = ps[bank][:, :].rearrange("p (h k) -> p h k", h=2)
                    pe.matmul(o[:, :, P:T], identb[:, :], maskb[:, 0:2, :], start=True, stop=False,
                              skip_group_check=True)
                    for i, h in enumerate(heads):
                        b, sl = A.stack(h)
                        mm = pe.matmul(o[:, i, :], R.Q[b:b + 48, p, sl, P:T], R.K[b:b + 48, p, sl, :],
                                       start=False, stop=True, skip_group_check=True)
                else:
                    o = ps[bank][:, :].rearrange("p (h k) -> p h k", h=4)
                    pe.matmul(o, identb[:, :], maskb[:, :, :], start=True, stop=False,
                              skip_group_check=True)
                    for i, h in enumerate(heads):
                        b, sl = A.stack(h)
                        mm = pe.matmul(o[:, i, :], R.Q[b:b + 48, p, sl, 0:P], R.K[b:b + 48, p, sl, 0:P],
                                       start=False, stop=True, skip_group_check=True)
                mm.then_inc(S.rows_ps, 1)

            def pe_mT(pe, s, p, bank):
                pe.wait_ge(S.mx, s * U + U)
                for j in range(NT):
                    mm = pe.transpose(ps[bank][0:H, j * P:(j + 1) * P], R.negm[:, p, j, 0:H], ident[:, :])
                mm.then_inc(S.m_ps, 1)

            def pe_main(pe, s, p, u):
                g, kind, heads = A.unit(u)
                bank = 2 + (U * p + u) % 2
                if u == 0:
                    pe.wait_ge(S.m_in, s * (16 * A.NH) + 16 * A.NH)
                if not (isinstance(s, int) and U * s + u < 2):
                    pe.wait_ge(S.ex, s * U + (u - 1))
                for i, h in enumerate(heads):
                    b, sl = A.stack(h)
                    if kind == "A":
                        mm = pe.matmul(ps[bank][:, i * T:(i + 1) * T], R.K[b:b + 50, p, sl, 0:P],
                                       R.Q[b:b + 50, p, sl, :], start=True, stop=True)
                    else:
                        mm = pe.matmul(ps[bank][:, i * P:(i + 1) * P], R.K[b:b + 50, p, sl, P:T],
                                       R.Q[b:b + 50, p, sl, P:T], start=True, stop=True)
                mm.then_inc(S.main_ps, 1)

            def pe_av(pe, s, p, g):
                pg = (NG * p + g) % 2
                pe.wait_ge(S.cz, s * NG + g + 1)
                if g == 0:
                    pe.wait_ge(S.v_sb, s + 1)
                if g % 2 == 0 and not (isinstance(s, int) and A.OE * s + g // 2 < 1):
                    pe.wait_ge(S.o_sb, s * A.OE + g // 2)
                c0 = (g % 2) * T if NG > 1 else 0
                for kt in range(2):
                    for i in range(4):
                        h = 4 * g + i
                        o = ps[4][32 * i:32 * i + 32, c0 + kt * P:c0 + T]
                        rhs = R.prob[:, pg, 0:3:2, i, :] if kt == 0 else R.prob[:, pg, 1, i, :]
                        mm = pe.matmul(o, R.v[:, p, kt, h, :], rhs, start=(kt == 0), stop=(kt == 1),
                                       skip_group_check=True)
                mm.then_inc(S.av, 1)

            def pe_oN(pe, s, bank, tiles):
                pe.wait_ge(S.o_sb, s * A.OE + A.OE)
                for n, j in enumerate(tiles):
                    for g in range(NG):
                        mm = pe.transpose(ps[bank][:, (n * NG + g) * P:(n * NG + g + 1) * P],
                                          R.o[:, g, j * P:(j + 1) * P], ident[:, :])
                mm.then_inc(S.oN_ps, 1)

            def pe_oT(pe, s, bank):
                pe.wait_ge(S.on_sb, s * 2 + 2)
                plain(pe)
                w = min(QC, P)
                for c in range(max(1, QC // P)):
                    for j in range(NT):
                        mm = pe.transpose(ps[bank][0:w, c * T + j * P:c * T + (j + 1) * P],
                                          R.on[:, j, c * w:(c + 1) * w], ident[:, :])
                mm.then_inc(S.oT_ps, 1)

            def pe_out(pe, s, bank):
                pe.wait_ge(S.oT_lo, s + 1)
                w, nch = min(QC, P), max(1, QC // P)
                for j in range(NT):
                    o = ps[bank][:, j * E:(j + 1) * E]
                    if L == 1:
                        pe.matmul(o, ones[:, :], bias[:, E:2 * E], start=True, stop=False)
                    for c in range(nch):
                        xs = [t[0:w, c * T + j * P:c * T + (j + 1) * P] for t in (R.oT_hi, R.oT_lo)]
                        mm = split_mm(pe, o, xs, [wo_at(t, L, c) for t in (wat_hi, wat_lo)],
                                      start=(c == 0 and L == 0), stop=(c == nch - 1))
                mm.then_inc(S.o_ps, 1)

            def pe_step0(pe, t, p):
                q = 1 - p
                if live(t + 1):
                    if live(t + 1):
                        pe.wait_ge(S.qkT_lo, (t + 1) * 2 + 2)
                    pe_proj(pe, t + 1, q, 5, 2 * E, E, S.v_ps)
                if live(t - 1):
                    pe_av(pe, t - 1, q, 3)
                    if live(t):
                        pe.wait_ge(S.m_lo, t + 1)
                    if live(t - 2):
                        pe.wait_ge(S.xr, t - 1)
                    pe_oN(pe, t - 1, 6, [0])
                    if live(t + 1):
                        pe.wait_ge(S.qkT_lo, (t + 1) * 2 + 1)
                    pe_oN(pe, t - 1, 7, [1])
                for u in range(3):
                    if live(t + 1):
                        pe_rows(pe, t + 1, q, u)
                for u in range(3):
                    if live(t):
                        pe_main(pe, t, p, u)
                if live(t + 2):
                    if live(t + 1):
                        pe.wait_ge(S.v_sb, t + 2)
                    pe_xT(pe, t + 2, 5)
                if live(t - 1):
                    pe_oT(pe, t - 1, 6)
                for g in range(1, 4):
                    for u in range(3 * g, 3 * g + 3):
                        if live(t + 1):
                            pe_rows(pe, t + 1, q, u)
                        if live(t):
                            pe_main(pe, t, p, u)
                    if g == 3 and live(t + 1):
                        if live(t - 1):
                            pe.wait_ge(S.xr, t)
                        if live(t):
                            pe.wait_ge(S.m_lo, t + 1)
                        pe_mT(pe, t + 1, q, 6)
                    if live(t):
                        pe_av(pe, t, p, g - 1)
                    if g == 1:
                        if live(t + 2):
                            if live(t + 1):
                                pe.wait_ge(S.qkT_lo, (t + 1) * 2 + 1)
                            pe_proj(pe, t + 2, p, 7, 0, E, S.qk_ps)
                            pe_proj(pe, t + 2, p, 5, E, E, S.qk_ps)
                        if live(t - 1):
                            pe_out(pe, t - 1, 6)
                    if g == 2 and live(t + 2):
                        pe_qkT(pe, t + 2, 0, 7)
                        pe_qkT(pe, t + 2, 1, 5)

            def pe_step1(pe, t, p):
                q = 1 - p
                if live(t - 1):
                    if live(t):
                        pe.wait_ge(S.m_lo, t + 1)
                    pe_oN(pe, t - 1, 5, [0, 1])
                for u in range(3):
                    if live(t + 1):
                        pe_rows(pe, t + 1, q, u)
                for u in range(3):
                    if live(t):
                        pe_main(pe, t, p, u)
                if live(t + 2):
                    if live(t - 2):
                        pe.wait_ge(S.xr, t - 1)
                    pe_xT(pe, t + 2, 6)
                if live(t - 1):
                    if live(t + 1):
                        pe.wait_ge(S.qkT_lo, t + 2)
                    pe_oT(pe, t - 1, 7)
                if live(t):
                    pe_av(pe, t, p, 0)
                if live(t + 2):
                    if live(t):
                        pe.wait_ge(S.m_lo, t + 1)
                    pe_proj(pe, t + 2, p, 5, 0, E, S.qk_ps)
                if live(t - 1):
                    if live(t - 2):
                        pe.wait_ge(S.xr, t - 1)
                    pe_out(pe, t - 1, 6)
                if live(t + 2):
                    pe_qkT(pe, t + 2, 0, 7)
                if live(t + 1):
                    pe_mT(pe, t + 1, q, 5)

            def act_xn(act, s):
                act.wait_ge(S.ln_rs, s * 4 + 4)
                if live(s - 1):
                    act.wait_ge(S.r_ok, (s - 1) * A.RB + A.RB)
                for j in range(NT):
                    nc.scalar.activation(R.xn[:, j:j + 1, :], x[:, cols(2 * s + j, 1), :], ACT.Identity,
                                         bias=nmr[:, j:j + 1], scale=rs[:, 1, j:j + 1]).then_inc(S.xn, 1)

            def act_xT(act, s, p, bank):
                act.wait_ge(S.xT_ps, s + 1)
                if live(s - 2):
                    act.wait_ge(S.v_ps if L == 0 else S.qk_ps, s - 1)
                nc.scalar.copy(R.xT_hi[:, p, :], ps[bank][:, :]).then_inc(S.xT_hi, 1)

            def act_v(act, s, p, bank, c0):
                act.wait_ge(S.v_ps if L == 0 else S.qk_ps, s + 1)
                if live(s - 2):
                    act.wait_ge(S.av, (s - 2) * NG + NG)
                src = ps[bank][:, :].rearrange("p (j n) -> p j n", j=NT)[:, :, c0:c0 + QC]
                nc.scalar.copy(R.v[:, p, :, 0:H, 0:HD], src.rearrange("p j (h d) -> p j h d", h=H))\
                    .then_inc(S.v_sb, 1)

            def act_qkT(act, s, b, bank):
                act.wait_ge(S.qkT_ps, s * A.RB + b + 1)
                if live(s - 1):
                    act.wait_ge(S.k_out if b else S.q_out, s * 32)
                n = A.NCH * T
                nc.scalar.copy(R.split[:, b, 0, 0:n], ps[bank][:, 0:n]).then_inc(S.qkT_hi, 1)

            def act_m(act, s, bank):
                act.wait_ge(S.m_ps, s + 1)
                if live(s - 1):
                    act.wait_ge(S.m_out, (s - 1) * 16 + 16)
                nc.scalar.copy(R.msplit[0:H, 0, :], ps[bank][0:H, 0:T]).then_inc(S.m_hi, 1)

            def act_exp(act, s, p, u):
                g, kind, heads = A.unit(u)
                bank, pg = 2 + (U * p + u) % 2, (NG * p + g) % 2
                act.wait_ge(S.main_ps, s * U + u + 1)
                if u % 3 == 0 and not (isinstance(s, int) and NG * s + g < 2):
                    act.wait_ge(S.av, s * NG + (g - 1))
                if kind == "A":
                    i = heads[0] % 4
                    o = R.prob[:, pg, 0:3:2, i:i + 2, :]
                    src = ps[bank][:, :].rearrange("p (h a q) -> p a h q", h=2, a=2)
                else:
                    o = R.prob[:, pg, 1, :, :]
                    src = ps[bank][:, :].rearrange("p (h k) -> p h k", h=4)
                nc.scalar.activation(o, src, ACT.Exp, scale=float(HD) ** -0.5).then_inc(S.ex, 1)

            def act_o(act, s, e):
                n = min(NG, 2)
                act.wait_ge(S.av, s * NG + n * (e + 1))
                if live(s - 1):
                    act.wait_ge(S.oN_ps, s * (2 if L == 0 else 1))
                nc.scalar.copy(R.o[:, n * e:n * (e + 1), :], ps[4][:, 0:n * T]
                               .rearrange("p (g q) -> p g q", g=n)).then_inc(S.o_sb, 1)

            def act_oT(act, s, bank):
                act.wait_ge(S.oT_ps, s + 1)
                if live(s - 1):
                    act.wait_ge(S.o_ps, s)
                w, n = min(QC, P), max(1, QC // P) * T
                nc.scalar.copy(R.oT_hi[0:w, 0:n], ps[bank][0:w, 0:n]).then_inc(S.oT_hi, 1)

            def act_step0(act, t, p):
                q = 1 - p
                if live(t + 1):
                    act_v(act, t + 1, q, 5, 0)
                if live(t - 1):
                    act_o(act, t - 1, 1)
                if live(t + 2):
                    act_xn(act, t + 2)
                for g in range(4):
                    if g == 3 and live(t + 2):
                        act_qkT(act, t + 2, 0, 7)
                        act_qkT(act, t + 2, 1, 5)
                    for u in range(3 * g, 3 * g + 3):
                        if live(t):
                            act_exp(act, t, p, u)
                    if g == 0:
                        if live(t + 2):
                            act_xT(act, t + 2, p, 5)
                        if live(t - 1):
                            act_oT(act, t - 1, 6)
                    if g == 2 and live(t):
                        act_o(act, t, 0)
                if live(t + 1):
                    act_m(act, t + 1, 6)

            def act_step1(act, t, p):
                if live(t + 2):
                    act_xn(act, t + 2)
                for u in range(3):
                    if live(t):
                        act_exp(act, t, p, u)
                if live(t + 2):
                    act_xT(act, t + 2, p, 6)
                if live(t - 1):
                    act_oT(act, t - 1, 7)
                if live(t):
                    act_o(act, t, 0)
                if live(t + 2):
                    act_v(act, t + 2, p, 5, 2 * QC)
                    act_qkT(act, t + 2, 0, 7)
                if live(t + 1):
                    act_m(act, t + 1, 5)

            def v_ln(dve, s):
                if L == 0:
                    if isinstance(s, int) and s < 2:
                        dve.wait_ge(setup.x_first, 16)
                    else:
                        dve.wait_ge(setup.x_rest, 16)
                for j in range(NT):
                    nc.vector.bn_stats(st[:, j, :], x[:, cols(2 * s + j, 1), :].rearrange("p a e -> p (a e)"))\
                        .then_inc(S.ln_st, 1)
                dve.wait_ge(S.ln_st, s * 2 + 2)
                if live(s - 1):
                    dve.wait_ge(S.ln_rs, (s - 1) * 4 + 4)
                plain(dve)
                for j in range(NT):
                    nc.vector.bn_aggr(mv[:, j, :], st[:, j, :]).then_inc(S.ln_mv, 1)

            def v_xT(dve, s, p, bank):
                dve.wait_ge(S.xT_hi, s + 1)
                nc.vector.tensor_tensor(R.xT_lo[:, p, :], ps[bank][:, :], R.xT_hi[:, p, :].bitcast(F32),
                                        ALU.subtract).then_inc(S.xT_lo, 1)

            def v_rope(dve, s, b, bank):
                dve.wait_ge(S.qk_ps, s * A.RB + b + 1)
                if L == 1:
                    dve.wait_ge(S.v_sb, s + 1)
                if live(s - 1):
                    dve.wait_ge(S.qkT_ps, (s - 1) * A.RB + b + 1)
                if live(s - 3):
                    dve.wait_ge(S.oT_ps, s - 2)
                n = A.RC
                src = ps[bank][:, :].rearrange("p (j n) -> p j n", j=NT)[:, :, 0:n]\
                    .rearrange("p j (h d) -> p j h d", h=A.RH)
                o1 = R.rot[:, b, :, 0:n].rearrange("p j (h d) -> p j h d", h=A.RH)
                o2 = R.rot2[:, b, :, 0:n].rearrange("p j (h d) -> p j h d", h=A.RH)
                hd = HD // 2
                for j in range(NT):
                    c_b = cos[:, j:j + 1, :].to_broadcast([P, A.RH, HD])
                    nc.vector.tensor_tensor(o1[:, j], src[:, j], c_b, ALU.mult).then_inc(S.rope_t, 1)
                for a, z in ((0, hd), (hd, 0)):
                    for j in range(NT):
                        s_b = sin[:, j:j + 1, a:a + hd].to_broadcast([P, A.RH, hd])
                        nc.vector.tensor_tensor(o2[:, j, :, a:a + hd], src[:, j, :, z:z + hd], s_b,
                                                ALU.mult).then_inc(S.rope_t, 1)

            def v_qkT(dve, s, b, bank):
                dve.wait_ge(S.qkT_hi, s * A.RB + b + 1)
                n = A.NCH * T
                nc.vector.tensor_tensor(R.split[:, b, 1, 0:n], ps[bank][:, 0:n],
                                        R.split[:, b, 0, 0:n].bitcast(F32),
                                        ALU.subtract).then_inc(S.qkT_lo, 1)

            def v_max(dve, s, p, u):
                g, kind, heads = A.unit(u)
                bank = (U * p + u) % 2
                dve.wait_ge(S.rows_ps, s * U + u + 1)
                if u == 0:
                    if live(s - 2):
                        dve.wait_ge(S.m_ps, s - 1)
                j, n = (1, 2) if kind == "A" else (0, 4)
                nc.vector.tensor_reduce(R.negm[:, p, j, heads[0]:heads[0] + n],
                                        ps[bank][:, :].rearrange("p (h k) -> p h k", h=n),
                                        axis=AX.X, op=ALU.max, negate=True).then_inc(S.mx, 1)

            def v_m(dve, s, bank):
                dve.wait_ge(S.m_hi, s + 1)
                nc.vector.tensor_tensor(R.msplit[0:H, 1, :], ps[bank][0:H, 0:T],
                                        R.msplit[0:H, 0, :].bitcast(F32), ALU.subtract).then_inc(S.m_lo, 1)

            def v_on(dve, s, bank, tiles):
                dve.wait_ge(S.oN_ps, s * (2 // len(tiles)) + tiles[0] + 1)
                if live(s + 2):
                    dve.wait_ge(S.r_ok, (s + 2) * A.RB + A.RB)
                for n, j in enumerate(tiles):
                    src = ps[bank][:, n * NG * P:(n + 1) * NG * P].rearrange("p (h d) -> p h d", h=H)
                    nc.vector.reciprocal(R.rinv[:, j, 0:H].rearrange("p (h o) -> p h o", o=1),
                                         src[:, :, HD:HD + 1]).then_inc(S.rinv, 1)
                for n, j in enumerate(tiles):
                    src = ps[bank][:, n * NG * P:(n + 1) * NG * P].rearrange("p (h d) -> p h d", h=H)
                    dve.wait_ge(S.rinv, s * 2 + j + 1)
                    r_b = R.rinv[:, j, 0:H].rearrange("p (h o) -> p h o", o=1).to_broadcast([P, H, HD])
                    nc.vector.tensor_tensor(R.on[:, j, 0:QC].rearrange("p (h d) -> p h d", h=H),
                                            src[:, :, 0:HD], r_b, ALU.mult).then_inc(S.on_sb, 1)

            def v_oT(dve, s, bank):
                dve.wait_ge(S.oT_hi, s + 1)
                w, n = min(QC, P), max(1, QC // P) * T
                nc.vector.tensor_tensor(R.oT_lo[0:w, 0:n], ps[bank][0:w, 0:n],
                                        R.oT_hi[0:w, 0:n].bitcast(F32), ALU.subtract).then_inc(S.oT_lo, 1)

            def v_res(dve, s, bank):
                dve.wait_ge(S.o_ps, s + 1)
                xs = x[:, cols(2 * s, 2), :]
                nc.vector.tensor_tensor(xs, ps[bank][:, :].rearrange("p (j e) -> p j e", j=NT), xs,
                                        ALU.add).then_inc(S.xr, 1)

            def v_step0(dve, t, p):
                q = 1 - p
                if live(t + 2):
                    v_ln(dve, t + 2)
                if live(t - 1):
                    v_on(dve, t - 1, 6, [0])
                    v_on(dve, t - 1, 7, [1])
                for g in range(4):
                    for u in range(3 * g, 3 * g + 3):
                        if live(t + 1):
                            v_max(dve, t + 1, q, u)
                    if g == 0:
                        if live(t + 2):
                            v_xT(dve, t + 2, p, 5)
                        if live(t - 1):
                            v_oT(dve, t - 1, 6)
                    if g == 1:
                        if live(t + 2):
                            v_rope(dve, t + 2, 0, 7)
                            v_rope(dve, t + 2, 1, 5)
                        if live(t - 1):
                            v_res(dve, t - 1, 6)
                    if g == 2 and live(t + 2):
                        v_qkT(dve, t + 2, 0, 7)
                        v_qkT(dve, t + 2, 1, 5)
                if live(t + 1):
                    v_m(dve, t + 1, 6)

            def v_step1(dve, t, p):
                q = 1 - p
                if live(t + 2):
                    v_ln(dve, t + 2)
                if live(t - 1):
                    v_on(dve, t - 1, 5, [0, 1])
                for u in range(3):
                    if live(t + 1):
                        v_max(dve, t + 1, q, u)
                if live(t + 2):
                    v_xT(dve, t + 2, p, 6)
                if live(t - 1):
                    v_oT(dve, t - 1, 7)
                if live(t + 2):
                    v_rope(dve, t + 2, 0, 5)
                if live(t - 1):
                    v_res(dve, t - 1, 6)
                if live(t + 2):
                    v_qkT(dve, t + 2, 0, 7)
                if live(t + 1):
                    v_m(dve, t + 1, 5)

            def p_ln(pool, s):
                pool.wait_ge(S.ln_mv, s * 2 + 2)
                if live(s - 1):
                    pool.wait_ge(S.xn, (s - 1) * 2 + 2)
                plain(pool)
                nc.gpsimd.tensor_scalar(rs[:, 0, 0:NT], mv[:, 0:NT, 1], EPS, None, ALU.add).then_inc(S.ln_rs, 1)
                pool.wait_ge(S.ln_rs, s * 4 + 1)
                nc.gpsimd.tensor_tensor(rs[:, 1, 0:NT], rs[:, 0, 0:NT], half[:, 0:NT], ALU.pow).then_inc(S.ln_rs, 1)
                pool.wait_ge(S.ln_rs, s * 4 + 2)
                plain(pool)
                for j in range(NT):
                    nc.gpsimd.tensor_scalar(nmr[:, j:j + 1], mv[:, j, 0:1], rs[:, 1, j:j + 1], -1.0,
                                            ALU.mult, ALU.mult).then_inc(S.ln_rs, 1)

            def p_rope(pool, s, b):
                pool.wait_ge(S.rope_t, s * (6 * A.RB) + 6 * (b + 1))
                nc.gpsimd.tensor_tensor(R.rot[:, b, :, 0:A.RC], R.rot[:, b, :, 0:A.RC],
                                        R.rot2[:, b, :, 0:A.RC], ALU.add).then_inc(S.r_ok, 1)

            def p_causal(pool, s, p, g):
                pg = (NG * p + g) % 2
                pool.wait_ge(S.ex, s * U + 3 * (g + 1))
                v = R.prob[:, pg, 0:2, :, :].rearrange("p a h q -> p (a h) q")
                plain(pool)
                nc.gpsimd.affine_select(out=v, in_=v, compare_op=ALU.is_ge, fill=0.0, base=0,
                                        pattern=[[0, 8], [1, P]], channel_multiplier=-1)\
                    .then_inc(S.cz, 1)

            def p_weights(pool, n):
                chunk = WB_CHUNK if L == 0 else WD_CHUNK
                w_in, w_hi, w_lo = (wf.in0, wf.hi0, wf.lo0) if L == 0 else (wf.in1, wf.hi1, wf.lo1)
                pool.wait_ge(w_in, n * 16 + 16)
                hi, lo = (w[:, cols(n * chunk, chunk)] for w in (wff_hi, wff_lo))
                nc.gpsimd.tensor_copy(hi, wstage[:, 0:chunk]).then_inc(w_hi, 1)
                pool.wait_ge(w_hi, n + 1)
                nc.gpsimd.tensor_tensor(lo, wstage[:, 0:chunk], hi.bitcast(F32), ALU.subtract).then_inc(w_lo, 1)

            def p_step(pool, t, p):
                if live(t + 2):
                    p_ln(pool, t + 2)
                for g in range(NG):
                    if g == min(2, NG - 1) and L == 0 and live(t + 2):
                        p_rope(pool, t + 2, 0)
                        p_rope(pool, t + 2, 1)
                    if live(t):
                        p_causal(pool, t, p, g)
                if L == 1 and live(t + 2):
                    p_rope(pool, t + 2, 0)
                if live(t + 2):
                    p_weights(pool, t + 2)

            def sp_weights(sp, n):
                chunk = WB_CHUNK if L == 0 else WD_CHUNK
                src, w_in, w_lo = (w_ff0, wf.in0, wf.lo0) if L == 0 else (w_moe, wf.in1, wf.lo1)
                if live(n - 1):
                    sp.wait_ge(w_lo, n)
                sp.dma_start(wstage[:, 0:chunk], src[:, cols(n * chunk, chunk)]).then_inc(w_in, 16)

            def sp_out(sp, s, b, p):
                sp.wait_ge(S.qkT_lo, s * A.RB + b + 1)
                n = A.NCH * T
                for r in range(2):
                    sp.dma_start((scrk if b else scrq)[p][r].rearrange("(c p) t -> p c t", p=P)[:, 0:A.NCH, :],
                                 R.split[:, b, r, 0:n].bitcast(F32).rearrange("p (c t) -> p c t", t=T))\
                        .then_inc((S.k_out if b else S.q_out), 16)

            def sp_half(sp, s, hf, p):
                done = S.half1 if hf else S.half0
                for stack, srcs, lay in ((R.Q, scrq, (0, 1, 0)), (R.K, scrk, (0, 0, 1))):
                    if L == 1:
                        srcs = scrq
                    row0 = hf * HB * HD + (QC if L == 1 and stack is R.K else 0)
                    for i, r in enumerate(lay):
                        src = srcs[p][r, row0:row0 + HB * HD, :].rearrange("(h d) t -> d h t", h=HB)
                        b0 = 64 * hf + HD * i
                        sp.dma_start(stack[b0:b0 + HD, p, 0:HB, :].bitcast(F32), src).then_inc(done, 16)

            def sp_step(sp, t, p):
                q = 1 - p
                if live(t + 2):
                    sp_weights(sp, t + 2)
                    sp_out(sp, t + 2, 0, p)
                    if L == 0:
                        sp_out(sp, t + 2, 1, p)
                    if live(t + 2):
                        sp.wait_ge(S.q_out, (t + 2) * 32 + 32)
                    if L == 0:
                        if live(t + 2):
                            sp.wait_ge(S.k_out, (t + 2) * 32 + 32)
                    if live(t):
                        sp.wait_ge(S.main_ps, t * U + (U // 2) if L == 0 else U)
                    sp_half(sp, t + 2, 0, p)
                if live(t + 1):
                    if live(t + 1):
                        sp.wait_ge(S.m_lo, t + 2)
                    sp.dma_start(dram_m[q][0:H], R.msplit[0:H, :, :].bitcast(F32)).then_inc(S.m_out, 16)
                    if live(t + 1):
                        sp.wait_ge(S.m_out, (t + 1) * 16 + 16)
                    for hf in range(A.NH):
                        src = dram_m[q][hf * HB:(hf + 1) * HB].rearrange("h r t -> r h t")
                        sp.dma_start(R.Q[64 * hf + 48:64 * hf + 50, q, 0:HB, :].bitcast(F32), src)\
                            .then_inc(S.m_in, 16)
                if live(t + 2) and A.NH == 2:
                    if live(t):
                        sp.wait_ge(S.main_ps, t * U + U)
                    sp_half(sp, t + 2, 1, p)

            return dict(pe=pe_step0 if L == 0 else pe_step1, act=act_step0 if L == 0 else act_step1,
                        dve=v_step0 if L == 0 else v_step1, pool=p_step, sp=sp_step)

        def run_attention(eng, step):
            for t in range(-2, 2):
                step(eng, t, t % 2)
            with eng.Fori(1, NSEQ // 2 - 1) as i:
                step(eng, i * 2, 0)
                step(eng, i * 2 + 1, 1)
            step(eng, NSEQ - 2, 0)
            step(eng, NSEQ - 1, 1)
            step(eng, NSEQ, 0)

        def feed_forward(L, region):
            R = region
            NM = (INTER0 if L == 0 else INTER1) // P
            W1 = 2 * NM * P
            moe = L == 1
            S = Names()
            S.ln_st = ctx.enter_context(nc.semaphore(f"f{L}_ln_st"))
            S.ln_mv = ctx.enter_context(nc.semaphore(f"f{L}_ln_mv"))
            S.ln_rs = ctx.enter_context(nc.semaphore(f"f{L}_ln_rs"))
            S.xn = ctx.enter_context(nc.semaphore(f"f{L}_xn"))
            S.xT_ps = ctx.enter_context(nc.semaphore(f"f{L}_xT_ps"))
            S.xT_hi = ctx.enter_context(nc.semaphore(f"f{L}_xT_hi"))
            S.xT_lo = ctx.enter_context(nc.semaphore(f"f{L}_xT_lo"))
            S.g_ps = ctx.enter_context(nc.semaphore(f"f{L}_g_ps"))
            S.u_ps = ctx.enter_context(nc.semaphore(f"f{L}_u_ps"))
            S.silu = ctx.enter_context(nc.semaphore(f"f{L}_silu"))
            S.hh = ctx.enter_context(nc.semaphore(f"f{L}_hh"))
            S.h_hi = ctx.enter_context(nc.semaphore(f"f{L}_h_hi"))
            S.h_lo = ctx.enter_context(nc.semaphore(f"f{L}_h_lo"))
            S.dn = ctx.enter_context(nc.semaphore(f"f{L}_dn"))
            S.o_ps = ctx.enter_context(nc.semaphore(f"f{L}_o_ps"))
            S.xr = ctx.enter_context(nc.semaphore(f"f{L}_xr"))
            S.stored = ctx.enter_context(nc.semaphore(f"f{L}_stored"))
            S.sc_ps = ctx.enter_context(nc.semaphore(f"f{L}_sc_ps"))
            S.gate = ctx.enter_context(nc.semaphore(f"f{L}_gate"))
            S.tanh = ctx.enter_context(nc.semaphore(f"f{L}_tanh"))
            S.w_ok = ctx.enter_context(nc.semaphore(f"f{L}_w_ok"))
            S.wT_ps = ctx.enter_context(nc.semaphore(f"f{L}_wT_ps"))
            S.wT_hi = ctx.enter_context(nc.semaphore(f"f{L}_wT_hi"))
            S.wT_lo = ctx.enter_context(nc.semaphore(f"f{L}_wT_lo"))
            S.wb_ps = ctx.enter_context(nc.semaphore(f"f{L}_wb_ps"))
            HH = 2 if moe else 1

            def last_user(n, m, depth):
                if m >= depth:
                    return n * NM + m - depth + 1
                return n * NM + 1 - NM + max(k for k in range(NM) if k % depth == m % depth)

            def used_before(n, m, depth):
                return not isinstance(n, int) or last_user(n, m, depth) > 0

            def w_up(w, c, col):
                return w[:, c * W1 + col:c * W1 + col + P]

            def w_down(w, m):
                return w[:, NC * W1 + m * E:NC * W1 + (m + 1) * E]

            def blk_live(n):
                return not isinstance(n, int) or 0 <= n < NB

            def pe_xT(pe, n):
                for c in range(NC):
                    if c == 0:
                        pe.wait_ge(S.xn, n * BT + BT)
                        if moe:
                            if blk_live(n - 1):
                                pe.wait_ge(S.wT_lo, n)
                        else:
                            if blk_live(n - 1):
                                pe.wait_ge(S.xT_lo, (n - 1) * NC + NC)
                    else:
                        pe.wait_ge(S.xT_lo, n * NC + c)
                    for j in range(BT):
                        mm = pe.transpose(ps[6][:, j * P:(j + 1) * P], R.xnF[:, j, c * P:(c + 1) * P], ident[:, :])
                    mm.then_inc(S.xT_ps, 1)

            def pe_scores(pe, n, p):
                pe.wait_ge(S.xT_lo, n * NC + NC)
                for j in range(BT):
                    o = ps[6][:, j * NEXP:(j + 1) * NEXP]
                    for c in range(NC):
                        hi, lo = (t[:, p, c, j * P:(j + 1) * P] for t in (R.xF_hi, R.xF_lo))
                        gh, gl = (w[:, c * NEXP:(c + 1) * NEXP] for w in (wg_hi, wg_lo))
                        pe.matmul(o, hi, gh, start=(c == 0), stop=False)
                        pe.matmul(o, hi, gl, start=False, stop=False)
                        mm = pe.matmul(o, lo, gh, start=False, stop=(c == NC - 1))
                mm.then_inc(S.sc_ps, 1)

            def pe_wT(pe, n):
                pe.wait_ge(S.w_ok, n + 1)
                for j in range(BT):
                    mm = pe.transpose(ps[6][0:NEXP, j * P:(j + 1) * P], R.wexp[:, j, :], ident[:, :])
                mm.then_inc(S.wT_ps, 1)

            def act_xn(act, n):
                act.wait_ge(S.ln_rs, n * (BT + 2) + BT + 2)
                if blk_live(n - 1):
                    act.wait_ge(S.xT_ps, (n - 1) * NC + NC)
                for j in range(BT):
                    nc.scalar.activation(R.xnF[:, j:j + 1, :], x[:, cols(BT * n + j, 1), :], ACT.Identity,
                                         bias=nmr[:, j:j + 1], scale=rs[:, 1, j:j + 1]).then_inc(S.xn, 1)

            def act_xT(act, n, p):
                for c in range(NC):
                    act.wait_ge(S.xT_ps, n * NC + c + 1)
                    if c == 0:
                        if blk_live(n - 2):
                            act.wait_ge(S.u_ps, (n - 2) * NM + NM)
                    nc.scalar.copy(R.xF_hi[:, p, c, :], ps[6][:, :]).then_inc(S.xT_hi, 1)

            def act_wT(act, n, p):
                act.wait_ge(S.wT_ps, n + 1)
                if blk_live(n - 2):
                    act.wait_ge(S.wb_ps, (n - 2) * NM + NM)
                nc.scalar.copy(R.wT[0:NEXP, p, :], ps[6][0:NEXP, :]).then_inc(S.wT_hi, 1)

            def v_ln(dve, n):
                for j in range(BT):
                    nc.vector.bn_stats(st[:, j, :], x[:, cols(BT * n + j, 1), :].rearrange("p a e -> p (a e)"))\
                        .then_inc(S.ln_st, 1)
                dve.wait_ge(S.ln_st, n * BT + BT)
                if blk_live(n - 1):
                    dve.wait_ge(S.ln_rs, (n - 1) * (BT + 2) + BT + 2)
                plain(dve)
                for j in range(BT):
                    nc.vector.bn_aggr(mv[:, j, :], st[:, j, :]).then_inc(S.ln_mv, 1)

            def v_xT(dve, n, p):
                for c in range(NC):
                    dve.wait_ge(S.xT_hi, n * NC + c + 1)
                    nc.vector.tensor_tensor(R.xF_lo[:, p, c, :], ps[6][:, :], R.xF_hi[:, p, c, :].bitcast(F32),
                                            ALU.subtract).then_inc(S.xT_lo, 1)

            NGATE = 9

            def v_gate(dve, n):
                k = [0]

                def link(ins):
                    ins.then_inc(S.gate, 1)
                    k[0] += 1
                    dve.wait_ge(S.gate, n * NGATE + k[0])

                dve.wait_ge(S.sc_ps, n + 1)
                if blk_live(n - 1):
                    if blk_live(n - 1):
                        dve.wait_ge(S.tanh, n)
                sc = R.sc[:, :, :]
                link(nc.vector.tensor_copy(sc, ps[6][:, 0:BT * NEXP].rearrange("p (j e) -> p j e", j=BT)))
                for j in range(BT):
                    mine = R.sc[:, j, :].rearrange("p (e o) -> p e o", o=1).to_broadcast([P, NEXP, NEXP])
                    other = R.sc[:, j:j + 1, :].to_broadcast([P, NEXP, NEXP])
                    ins = nc.vector.tensor_tensor(R.gt[:, j], other, mine, ALU.is_gt)
                    ins2 = nc.vector.tensor_tensor(R.eq[:, j], other, mine, ALU.is_equal)
                link(ins2)
                tri_b = tri[:, :, :].rearrange("p e f -> p (e f)").rearrange("p (o n) -> p o n", o=1)\
                    .to_broadcast([P, BT, NEXP * NEXP])
                gt = R.gt[:, :, :, :].rearrange("p j e f -> p j (e f)")
                eq = R.eq[:, :, :, :].rearrange("p j e f -> p j (e f)")
                link(nc.vector.tensor_tensor(eq, eq, tri_b, ALU.mult))
                link(nc.vector.tensor_tensor(gt, gt, eq, ALU.add))
                link(nc.vector.tensor_reduce(R.rank[:, :, :], R.gt[:, :, :, :], axis=AX.X, op=ALU.add))
                link(nc.vector.tensor_scalar(R.halfsel[:, :, :], R.rank[:, :, :], 2.0, 0.5, ALU.is_lt, ALU.mult))
                link(nc.vector.tensor_tensor(R.tz[:, :, :], R.halfsel[:, :, :], sc, ALU.mult))
                link(nc.vector.tensor_reduce(R.mid[:, :], R.tz[:, :, :], axis=AX.X, op=ALU.add))
                mid_b = R.mid[:, :].rearrange("p (j o) -> p j o", o=1).to_broadcast([P, BT, NEXP])
                link(nc.vector.tensor_tensor(R.tz[:, :, :], sc, mid_b, ALU.subtract))
                dve.wait_ge(S.tanh, n + 1)
                if blk_live(n - 1):
                    dve.wait_ge(S.wT_ps, n)
                nc.vector.scalar_tensor_tensor(out=R.wexp[:, :, :], in0=R.th[:, :, :], scalar=1.0,
                                               in1=R.halfsel[:, :, :], op0=ALU.add, op1=ALU.mult)\
                    .then_inc(S.w_ok, 1)

            def act_tanh(act, n):
                act.wait_ge(S.gate, n * NGATE + NGATE)
                if blk_live(n - 1):
                    act.wait_ge(S.w_ok, n)
                nc.scalar.activation(R.th[:, :, :], R.tz[:, :, :], ACT.Tanh).then_inc(S.tanh, 1)

            def v_wT(dve, n, p):
                dve.wait_ge(S.wT_hi, n + 1)
                nc.vector.tensor_tensor(R.wT[32:32 + NEXP, p, :], ps[6][0:NEXP, :],
                                        R.wT[0:NEXP, p, :].bitcast(F32), ALU.subtract).then_inc(S.wT_lo, 1)

            def p_ln(pool, n):
                k = BT + 2
                pool.wait_ge(S.ln_mv, n * BT + BT)
                if blk_live(n - 1):
                    pool.wait_ge(S.xn, (n - 1) * BT + BT)
                plain(pool)
                nc.gpsimd.tensor_scalar(rs[:, 0, :], mv[:, :, 1], EPS, None, ALU.add).then_inc(S.ln_rs, 1)
                pool.wait_ge(S.ln_rs, n * k + 1)
                nc.gpsimd.tensor_tensor(rs[:, 1, :], rs[:, 0, :], half[:, :], ALU.pow).then_inc(S.ln_rs, 1)
                pool.wait_ge(S.ln_rs, n * k + 2)
                plain(pool)
                for j in range(BT):
                    nc.gpsimd.tensor_scalar(nmr[:, j:j + 1], mv[:, j, 0:1], rs[:, 1, j:j + 1], -1.0,
                                            ALU.mult, ALU.mult).then_inc(S.ln_rs, 1)

            def banks(n_par, m):
                b = 2 * (m % 2)
                return ps[b], ps[b + 1]

            def pe_up(pe, n, p, m):
                if m == 0:
                    pe.wait_ge(S.xT_lo, n * NC + NC)
                    if moe:
                        pe.wait_ge(S.wT_lo, n + 1)
                if used_before(n, m, 2):
                    pe.wait_ge(S.hh, last_user(n, m, 2) * HH)
                g_bank, u_bank = banks(p, m)
                for o, off, signal in ((g_bank, 0, S.g_ps), (u_bank, NM * P, S.u_ps)):
                    for c in range(NC):
                        wh, wl = (w_up(w, c, off + m * P) for w in (wff_hi, wff_lo))
                        xh, xl = R.xF_hi[:, p, c, :], R.xF_lo[:, p, c, :]
                        pe.matmul(o[:, :], wh, xh, start=(c == 0), stop=False)
                        pe.matmul(o[:, :], wh, xl, start=False, stop=False)
                        mm = pe.matmul(o[:, :], wl, xh, start=False, stop=(c == NC - 1))
                    mm.then_inc(signal, 1)
                if moe:
                    if used_before(n, m, 1):
                        pe.wait_ge(S.hh, last_user(n, m, 1) * HH)
                    pe.matmul(ps[7][:, :], R.sel[:, m, :], R.wT[:, p, :], start=True, stop=True)\
                        .then_inc(S.wb_ps, 1)

            def act_silu(act, n, p, m):
                act.wait_ge(S.g_ps, n * NM + m + 1)
                if used_before(n, m, 2):
                    act.wait_ge(S.hh, last_user(n, m, 2) * HH)
                nc.scalar.activation(R.sg[:, m % 2, :], banks(p, m)[0][:, :], ACT.Silu).then_inc(S.silu, 1)

            def act_hi(act, n, m):
                act.wait_ge(S.hh, n * (NM * HH) + HH * (m + 1))
                if used_before(n, m, 4):
                    act.wait_ge(S.dn, last_user(n, m, 4))
                nc.scalar.copy(R.h_hi[:, m % 4, :], R.hf[:, m % 2, :]).then_inc(S.h_hi, 1)

            def v_h(dve, n, p, m):
                dve.wait_ge(S.u_ps, n * NM + m + 1)
                dve.wait_ge(S.silu, n * NM + m + 1)
                if used_before(n, m, 2):
                    dve.wait_ge(S.h_lo, last_user(n, m, 2))
                h = R.hf[:, m % 2, :]
                nc.vector.tensor_tensor(h, banks(p, m)[1][:, :], R.sg[:, m % 2, :], ALU.mult).then_inc(S.hh, 1)
                if moe:
                    dve.wait_ge(S.wb_ps, n * NM + m + 1)
                    dve.wait_ge(S.hh, n * (NM * HH) + HH * m + 1)
                    nc.vector.tensor_tensor(h, ps[7][:, :], h, ALU.mult).then_inc(S.hh, 1)

            def v_lo(dve, n, m):
                dve.wait_ge(S.h_hi, n * NM + m + 1)
                nc.vector.tensor_tensor(R.h_lo[:, m % 4, :], R.hf[:, m % 2, :], R.h_hi[:, m % 4, :].bitcast(F32),
                                        ALU.subtract).then_inc(S.h_lo, 1)

            LAG = 2

            def pe_step(pe, n, p):
                for m in range(NM):
                    if blk_live(n):
                        pe_up(pe, n, p, m)
                    if m < LAG:
                        if blk_live(n - 1):
                            pe_down(pe, n - 1, NM - LAG + m)
                    elif blk_live(n):
                        pe_down(pe, n, m - LAG)
                    if blk_live(n + 1) and m == PREP:
                        pe_xT(pe, n + 1)
                    if moe and blk_live(n + 1):
                        if m == PREP + 1:
                            pe_scores(pe, n + 1, 1 - p)
                        if m == PREP + 3:
                            pe_wT(pe, n + 1)
                    if not blk_live(n) and m == LAG - 1:
                        break

            def pe_down(pe, n, m):
                pe.wait_ge(S.h_lo, n * NM + m + 1)
                if m == 0:
                    if blk_live(n - 1):
                        pe.wait_ge(S.xr, (n - 1) * 2 + 2)
                b = m % 4
                order = [0, 2, 1, 3]
                for j in order:
                    o = ps[4 + j // 2][:, (j % 2) * E:(j % 2 + 1) * E]
                    hi, lo = (t[:, b, j * P:(j + 1) * P] for t in (R.h_hi, R.h_lo))
                    pe.matmul(o, hi, w_down(wff_hi, m), start=(m == 0 and j % 2 == 0), stop=False,
                              skip_group_check=True)
                    pe.matmul(o, hi, w_down(wff_lo, m), start=False, stop=False, skip_group_check=True)
                    mm = pe.matmul(o, lo, w_down(wff_hi, m), start=False, stop=(m == NM - 1 and j % 2 == 1),
                                   skip_group_check=True)
                mm.then_inc(S.dn, 1)

            PREP = 3

            def act_step(act, n, p):
                if not blk_live(n):
                    return
                for m in range(NM):
                    act_silu(act, n, p, m)
                    act_hi(act, n, m)
                    if blk_live(n + 1):
                        if m == PREP - 2:
                            act_xn(act, n + 1)
                        if m == PREP:
                            act_xT(act, n + 1, 1 - p)
                        if moe and m == PREP + 2:
                            act_tanh(act, n + 1)
                        if moe and m == PREP + 3:
                            act_wT(act, n + 1, 1 - p)

            def v_step(dve, n, p):
                for m in range(NM):
                    if blk_live(n):
                        v_h(dve, n, p, m)
                        v_lo(dve, n, m)
                    if blk_live(n + 1) and blk_live(n):
                        if m == PREP - 3:
                            v_ln(dve, n + 1)
                        if m == PREP:
                            v_xT(dve, n + 1, 1 - p)
                        if moe and m == PREP + 2:
                            v_gate(dve, n + 1)
                        if moe and m == PREP + 3:
                            v_wT(dve, n + 1, 1 - p)
                    if m == LAG - 1 and blk_live(n - 1):
                        v_res(dve, n - 1)
                    if not blk_live(n) and m == LAG - 1:
                        break

            def v_res(dve, n):
                dve.wait_ge(S.dn, n * NM + NM)
                for r in range(2):
                    xs = x[:, cols(BT * n + 2 * r, 2), :]
                    nc.vector.tensor_tensor(xs, ps[4 + r][:, :].rearrange("p (j e) -> p j e", j=2), xs,
                                            ALU.add).then_inc(S.xr, 1)

            def p_step(pool, n, p):
                if blk_live(n + 1) and blk_live(n):
                    p_ln(pool, n + 1)

            def sp_step(sp, n, p):
                if moe and blk_live(n - 1):
                    if blk_live(n - 1):
                        sp.wait_ge(S.xr, (n - 1) * 2 + 2)
                    dst = out.rearrange("b (j p) e -> p (b j) e", p=P)
                    sp.dma_start(dst[:, cols(BT * (n - 1), BT), :], x[:, cols(BT * (n - 1), BT), :])\
                        .then_inc(S.stored, 16)

            def prep_first(engine, eng):
                if engine == "dve":
                    v_ln(eng, 0)
                    v_xT(eng, 0, 0)
                    if moe:
                        v_gate(eng, 0)
                        v_wT(eng, 0, 0)
                elif engine == "pool":
                    p_ln(eng, 0)
                elif engine == "act":
                    act_xn(eng, 0)
                    act_xT(eng, 0, 0)
                    if moe:
                        act_tanh(eng, 0)
                        act_wT(eng, 0, 0)
                elif engine == "pe":
                    pe_xT(eng, 0)
                    if moe:
                        pe_scores(eng, 0, 0)
                        pe_wT(eng, 0)

            return dict(pe=pe_step, act=act_step, dve=v_step, pool=p_step, sp=sp_step, first=prep_first,
                        stored=S.stored)

        def run_feed_forward(eng, F, engine):
            step = F[engine]
            F["first"](engine, eng)
            step(eng, 0, 0)
            step(eng, 1, 1)
            with eng.Fori(1, NB // 2 - 1) as i:
                step(eng, i * 2, 0)
                step(eng, i * 2 + 1, 1)
            step(eng, NB - 2, 0)
            step(eng, NB - 1, 1)
            step(eng, NB, 0)

        attn_buffers = ExitStack()

        def ra(name, shape, dt=F32):
            return attn_buffers.enter_context(nc.sbuf_tensor("a_" + name, shape, dt))

        RA = Names()
        RA.xT_hi = ra("xT_hi", [P, 2, NC * T], F32R)
        RA.xT_lo = ra("xT_lo", [P, 2, NC * T], F32R)
        RA.rot = ra("rot", [P, 2, NT, E])
        RA.rot2 = ra("rot2", [P, 2, NT, E])
        RA.split = ra("split", [P, 2, 2, NC * T], F32R)
        RA.Q = ra("Q", [P, 2, 8, T], F32R)
        RA.K = ra("K", [P, 2, 8, T], F32R)
        RA.prob = ra("prob", [P, 2, 3, 4, P])
        RA.v = ra("v", [P, 2, NT, 16, 2 * HD])
        RA.o = ra("o", [P, 4, T])
        RA.oT_hi = ra("oT_hi", [P, NC * T], F32R)
        RA.oT_lo = ra("oT_lo", [P, NC * T], F32R)
        RA.negm = ra("negm", [P, 2, NT, 16])
        RA.msplit = ra("msplit", [16, 2, T], F32R)
        RA.rinv = ra("rinv", [P, NT, 16])
        attn_buffers.close()
        RA.xn, RA.on = RA.rot2[:, 0], RA.rot2[:, 1]

        def rf(name, shape, dt=F32):
            return ctx.enter_context(nc.sbuf_tensor("f_" + name, shape, dt))

        RF = Names()
        RF.xnF = rf("xnF", [P, BT, E])
        RF.xF_hi = rf("xF_hi", [P, 2, NC, BN], F32R)
        RF.xF_lo = rf("xF_lo", [P, 2, NC, BN], F32R)
        RF.sg = rf("sg", [P, 2, BN])
        RF.hf = rf("hf", [P, 2, BN])
        RF.h_hi = rf("h_hi", [P, 4, BN], F32R)
        RF.h_lo = rf("h_lo", [P, 4, BN], F32R)
        RF.sel = rf("sel", [64, INTER1 // P, P], F32R)
        RF.wT = rf("wT", [64, 2, BN], F32R)
        RF.selraw = rf("selraw", [64, INTER1 // P, P])
        RF.sc = rf("sc", [P, BT, NEXP])
        RF.gt = rf("gt", [P, BT, NEXP, NEXP])
        RF.eq = rf("eq", [P, BT, NEXP, NEXP])
        RF.rank = rf("rank", [P, BT, NEXP])
        RF.halfsel = rf("halfsel", [P, BT, NEXP])
        RF.tz = rf("tz", [P, BT, NEXP])
        RF.th = rf("th", [P, BT, NEXP])
        RF.mid = rf("mid", [P, BT])
        RF.wexp = rf("wexp", [P, BT, NEXP])

        A0 = attention(0, RA, 0)
        F0 = feed_forward(0, RF)
        A1 = attention(1, RA, 1)
        F1 = feed_forward(1, RF)

        raw0 = RA.v[:, :, :, :, :].rearrange("p a j h d -> p (a j h d)")
        NW0 = NC * (W0 + E)
        NQ1 = NC * E
        rawm = RA.rot[:, :, :, :].rearrange("p a j e -> p (a j e)")
        rawo = RA.rot2[:, :, :, :].rearrange("p a j e -> p (a j e)")
        sum1 = RA.o[:, 0:2, :].rearrange("p j e -> p (j e)")
        sumb = RA.o[:, 2:4, :].rearrange("p j e -> p (j e)")
        rawg = RA.prob[:, 0, 0, 0, :]

        block = ctx.enter_context(nc.Block())

        @block.sync
        def _(sp):
            x_v = x_in.rearrange("b (j p) e -> p (b j) e", p=P)
            for dst, src in ((cos, c_cos), (sin, c_sin)):
                sp.dma_start(dst[:, :, :], src).then_inc(setup.const, 16)
            sp.dma_start(ident[:, :], c_ident).then_inc(setup.const, 16)
            sp.dma_start(tri[:, :, :], c_tri).then_inc(setup.const, 16)
            sp.dma_start(wstage[:, 0:P], c_mask).then_inc(setup.const, 16)
            sp.dma_start(x[:, 0:2 * NT, :], x_v[:, 0:2 * NT, :]).then_inc(setup.x_first, 16)
            sp.dma_start(raw0[:, 0:NC * W0].rearrange("p (c n) -> p c n", c=NC),
                         wqkv0.rearrange("(c p) n -> p c n", p=P)).then_inc(setup.w_raw, 16)
            sp.dma_start(raw0[:, NC * W0:NW0].rearrange("p (c n) -> p c n", c=NC),
                         wo0.rearrange("(c p) n -> p c n", p=P)).then_inc(setup.w_raw, 16)
            sp.dma_start(x[:, 2 * NT:, :], x_v[:, 2 * NT:, :]).then_inc(setup.x_rest, 16)
            sp.wait_ge(setup.const_cp, 3)
            sp.wait_ge(setup.w_lo, 1)
            run_attention(sp, A0["sp"])
            end_of_phase(sp, 1)
            run_feed_forward(sp, F0, "sp")
            end_of_phase(sp, 2)
            sp.dma_start(rawm[:, 0:2 * E].rearrange("p (c n) -> p c n", c=NC),
                         wq1.rearrange("(c p) n -> p c n", p=P)).then_inc(setup.raw1, 16)
            sp.dma_start(rawm[:, 2 * E:2 * E + 2 * P].rearrange("p (c n) -> p c n", c=NC),
                         wkv1.rearrange("(c p) n -> p c n", p=P)).then_inc(setup.raw1, 16)
            sp.dma_start(rawo[0:64, 0:E], wo1).then_inc(setup.raw1, 16)
            sp.dma_start(rawg[:, 0:NC * NEXP].rearrange("p (c n) -> p c n", c=NC),
                         w_gate.rearrange("(c p) n -> p c n", p=P)).then_inc(setup.raw1, 16)
            sp.wait_ge(setup.sum1, 2)
            for row in (0, 32):
                sp.dma_start(rawo[row:row + 1, E:2 * E], bq1).then_inc(setup.raw1, 16)
                sp.dma_start(rawo[row:row + 1, 2 * E:2 * E + P], bkv1).then_inc(setup.raw1, 16)
                sp.dma_start(rawo[row:row + 1, 3 * E:4 * E], bo1).then_inc(setup.raw1, 16)
            sp.wait_ge(setup.lo1, 4)
            run_attention(sp, A1["sp"])
            end_of_phase(sp, 3)
            sp.dma_start(RF.selraw[:, :, :], c_sel).then_inc(setup.wg, 16)
            run_feed_forward(sp, F1, "sp")
            sp.wait_ge(F1["stored"], 16 * NB)
            end_of_phase(sp, 4)

        @block.gpsimd
        def _(pool):
            nc.gpsimd.memset(half[:, :], -0.5)
            pool.wait_ge(setup.w_lo, 1)
            nc.gpsimd.memset(RA.v[:, :, :, :, HD:2 * HD], 1.0)
            pool.drain().then_inc(setup.hi1, 1)
            pool.wait_ge(setup.const_cp, 3)
            run_attention(pool, A0["pool"])
            end_of_phase(pool, 1)
            run_feed_forward(pool, F0, "pool")
            end_of_phase(pool, 2)
            nc.gpsimd.memset(RA.v[:, :, :, :, HD:2 * HD], 1.0)
            pool.drain().then_inc(setup.hi1, 1)
            run_attention(pool, A1["pool"])
            end_of_phase(pool, 3)
            run_feed_forward(pool, F1, "pool")
            end_of_phase(pool, 4)

        @block.scalar
        def _(act):
            act.wait_ge(setup.w_raw, 32)
            nc.scalar.copy(wat_hi[:, 0:NW0], raw0[:, 0:NW0]).then_inc(setup.w_hi, 1)
            act.wait_ge(setup.hi1, 1)
            run_attention(act, A0["act"])
            end_of_phase(act, 1)
            run_feed_forward(act, F0, "act")
            end_of_phase(act, 2)
            act.wait_ge(setup.hi1, 2)
            run_attention(act, A1["act"])
            end_of_phase(act, 3)
            run_feed_forward(act, F1, "act")
            end_of_phase(act, 4)

        @block.vector
        def _(dve):
            dve.wait_ge(setup.const, 80)
            nc.vector.tensor_copy(identb[:, :], ident[:, :]).then_inc(setup.const_cp, 1)
            nc.vector.tensor_copy(maskb[:, :, :], wstage[:, 0:P].rearrange("p (o n) -> p o n", o=1)
                                  .to_broadcast([P, 4, P])).then_inc(setup.const_cp, 1)
            nc.vector.memset(ones[:, :].bitcast(F32), 1.0).then_inc(setup.const_cp, 1)
            dve.wait_ge(setup.w_hi, 1)
            nc.vector.tensor_tensor(wat_lo[:, 0:NW0], raw0[:, 0:NW0], wat_hi[:, 0:NW0].bitcast(F32),
                                    ALU.subtract)
            for b in (32, 96):
                nc.vector.memset(RA.K[b:b + 32, :, :, :].bitcast(F32), 1.0)
            dve.drain().then_inc(setup.w_lo, 1)
            run_attention(dve, A0["dve"])
            end_of_phase(dve, 1)
            run_feed_forward(dve, F0, "dve")
            end_of_phase(dve, 2)
            nc.vector.memset(rawo[0:64, E:4 * E], 0.0).then_inc(setup.sum1, 1)
            for b in (32,):
                nc.vector.memset(RA.K[b:b + 32, :, :, :].bitcast(F32), 1.0)
            dve.drain().then_inc(setup.sum1, 1)
            dve.wait_ge(setup.raw1, 16 * 10)
            nc.vector.memset(sum1[:, :], 0.0)
            nc.vector.memset(sumb[0:64, :], 0.0)
            dve.drain().then_inc(setup.sum1, 1)
            dve.wait_ge(setup.sum1, 3)
            for c in range(NC):
                nc.vector.tensor_reduce(
                    sum1[:, c * E:c * E + 64].rearrange("p (k d) -> p k d", k=4),
                    rawm[:, c * E:(c + 1) * E].rearrange("p (k g d) -> p k d g", k=4, g=4), axis=AX.X, op=ALU.add)
                nc.vector.tensor_copy(sum1[:, c * E + 64:c * E + 192], rawm[:, 2 * E + c * P:2 * E + (c + 1) * P])
            nc.vector.tensor_reduce(sumb[0:64, 0:64].rearrange("p (k d) -> p k d", k=4),
                                    rawo[0:64, E:2 * E].rearrange("p (k g d) -> p k d g", k=4, g=4),
                                    axis=AX.X, op=ALU.add)
            nc.vector.tensor_copy(sumb[0:64, 64:192], rawo[0:64, 2 * E:2 * E + P])
            nc.vector.tensor_copy(sumb[0:64, E:2 * E], rawo[0:64, 3 * E:4 * E])
            dve.drain().then_inc(setup.sum1, 1)
            dve.wait_ge(setup.sum1, 4)
            nc.vector.tensor_copy(wat_hi[:, 0:NQ1], sum1[:, :])
            nc.vector.tensor_copy(wat_hi[0:64, NQ1:NQ1 + E], rawo[0:64, 0:E])
            nc.vector.tensor_copy(wg_hi[:, :], rawg[:, 0:NC * NEXP])
            nc.vector.tensor_copy(bias[:, :], sumb[0:64, :])
            dve.drain().then_inc(setup.lo1, 1)
            dve.wait_ge(setup.lo1, 1)
            nc.vector.tensor_tensor(wat_lo[:, 0:NQ1], sum1[:, :], wat_hi[:, 0:NQ1].bitcast(F32), ALU.subtract)
            nc.vector.tensor_tensor(wat_lo[0:64, NQ1:NQ1 + E], rawo[0:64, 0:E],
                                    wat_hi[0:64, NQ1:NQ1 + E].bitcast(F32), ALU.subtract)
            nc.vector.tensor_tensor(wg_lo[:, :], rawg[:, 0:NC * NEXP], wg_hi[:, :].bitcast(F32), ALU.subtract)
            nc.vector.tensor_tensor(bias[32:64, :], sumb[32:64, :], bias[32:64, :].bitcast(F32), ALU.subtract)
            dve.drain().then_inc(setup.lo1, 3)
            dve.wait_ge(setup.lo1, 4)
            run_attention(dve, A1["dve"])
            end_of_phase(dve, 3)
            dve.wait_ge(setup.wg, 16)
            nc.vector.tensor_copy(RF.sel[:, :, :], RF.selraw[:, :, :])
            nc.vector.memset(RF.wT[:, :, :].bitcast(F32), 0.0)
            dve.drain().then_inc(setup.wg, 1)
            dve.wait_ge(setup.wg, 17)
            run_feed_forward(dve, F1, "dve")
            end_of_phase(dve, 4)

        @block.tensor
        def _(pe):
            pe.wait_ge(setup.const_cp, 3)
            pe.wait_ge(setup.w_lo, 1)
            run_attention(pe, A0["pe"])
            end_of_phase(pe, 1)
            run_feed_forward(pe, F0, "pe")
            end_of_phase(pe, 2)
            pe.wait_ge(setup.lo1, 4)
            run_attention(pe, A1["pe"])
            end_of_phase(pe, 3)
            pe.wait_ge(setup.wg, 17)
            run_feed_forward(pe, F1, "pe")
            end_of_phase(pe, 4)


def constants():
    f = np.float32
    inv = (f(1.0) / np.power(f(10000.0), np.arange(0, HD, 2, dtype=f) / f(HD))).astype(f)
    ang = (np.arange(T, dtype=f)[:, None] * inv[None, :]).astype(f)
    c, s = np.cos(ang).astype(f), np.sin(ang).astype(f)
    cos = np.concatenate([c, c], 1).reshape(NT, P, HD).transpose(1, 0, 2)
    sin = np.concatenate([-s, s], 1).reshape(NT, P, HD).transpose(1, 0, 2)
    ident = np.eye(P, dtype=f)
    mask = np.where(np.arange(P)[None, :] > np.arange(P)[:, None], f(MASK), f(0.0)).astype(f)
    tri = np.broadcast_to(np.tril(np.ones((NEXP, NEXP), f), -1), (P, NEXP, NEXP))
    sel = np.zeros((64, INTER1), f)
    for e in range(NEXP):
        sel[e, e * HID:(e + 1) * HID] = 1.0
        sel[32 + e, e * HID:(e + 1) * HID] = 1.0
    sel = sel.reshape(64, INTER1 // P, P)
    return {k: np.ascontiguousarray(v) for k, v in
            dict(c_cos=cos, c_sin=sin, c_ident=ident, c_mask=mask, c_tri=tri, c_sel=sel).items()}


def kernel(**inputs):
    import concourse.bacc as bacc
    from concourse.bass_utils import run_bass_kernel_spmd as run

    i = {k: np.asarray(v) for k, v in inputs.items()}
    perm = np.concatenate([np.arange(0, HD, 2), np.arange(1, HD, 2)])

    def heads(w):
        return w.reshape(w.shape[0], -1, HD)[:, :, perm].reshape(w.shape[0], -1)

    def by_partition(w):
        k, n = w.shape
        return w.reshape(k // P, P, n).transpose(1, 0, 2).reshape(P, -1)

    w1 = i["L1_ffn_W1"].reshape(INTER1, E).T
    w2 = i["L1_ffn_W2"].reshape(INTER1, E).T
    w3 = i["L1_ffn_W3"].transpose(0, 2, 1).reshape(INTER1, E)
    arrays = dict(
        x_in=i["L0_attn_x"],
        wqkv0=np.concatenate([i["L0_attn_wq"], i["L0_attn_wk"], i["L0_attn_wv"]], 1),
        wo0=i["L0_attn_wo"],
        w_ff0=np.concatenate([by_partition(i["L0_ffn_w_gate_up"].T), by_partition(i["L0_ffn_w_down"].T)], 1),
        wq1=heads(i["L1_attn_Wq"]),
        wkv1=np.concatenate([heads(i["L1_attn_Wk"]), i["L1_attn_Wv"]], 1),
        bq1=heads(i["L1_attn_bq"][None, :]),
        bkv1=np.concatenate([heads(i["L1_attn_bk"][None, :]), i["L1_attn_bv"][None, :]], 1),
        wo1=i["L1_attn_Wo"],
        bo1=i["L1_attn_bo"][None, :],
        w_moe=np.concatenate([by_partition(np.concatenate([w1, w2], 1)), by_partition(w3)], 1),
        w_gate=i["L1_ffn_Wg"].T,
        **constants(),
    )
    arrays = {k: np.ascontiguousarray(v) for k, v in arrays.items()}
    nc = bacc.Bacc("TRN2", target_bir_lowering=False, num_devices=1)
    args = [nc.dram_tensor(k, v.shape, mybir.dt.from_np(v.dtype), kind="ExternalInput").ap()
            for k, v in arrays.items()]
    out = nc.dram_tensor("out", (NSEQ, T, E), F32, kind="ExternalOutput").ap()
    build(nc, *args, out)
    r = run(nc, [arrays], core_ids=[0])
    return r.results[0]["out"]
```

```python
from contextlib import ExitStack

import numpy as np

import concourse.bass as bass
from concourse import mybir

F32 = mybir.dt.float32
F32R = mybir.dt.float32r
BF16 = mybir.dt.bfloat16
ALU = mybir.AluOpType
ACT = mybir.ActivationFunctionType
AX = mybir.AxisListType

P = 128
NSEQ, T, E = 16, 256, 256
NT = T // P
NC = E // P
HD = 16
EPS = 1e-5
MASK = -1e30
INTER0 = 1024
NEXP, HID = 8, 176
INTER1 = NEXP * HID
NB = 8
BT = 4
BN = BT * P
W0 = 3 * E
WB_CHUNK = (2 * INTER0 * NC + INTER0 // P * E) // NSEQ
WD_CHUNK = (2 * INTER1 * NC + INTER1 // P * E) // NSEQ
WMAX = WD_CHUNK * NSEQ


def cols(start, size):
    return bass.ds(start, size)


class Names:
    pass


def live(seq):
    return not isinstance(seq, int) or 0 <= seq < NSEQ


class Attn:

    def __init__(self, layer):
        self.layer = layer
        self.H = 16 if layer == 0 else 4
        self.NG = self.H // 4
        self.HB = min(8, self.H)
        self.NH = self.H // self.HB
        self.U = 3 * self.NG
        self.QC = self.H * HD
        self.RB = 2 if layer == 0 else 1
        self.RH = 16 if layer == 0 else 8
        self.RC = self.RH * HD
        self.NCH = self.RC // P
        self.DEPTH = 50 if layer == 0 else 48
        self.OE = max(1, self.NG // 2)

    def stack(self, h):
        return 64 * (h // self.HB), h % self.HB

    def unit(self, u):
        g, r = divmod(u, 3)
        return (g, "A", [4 * g + 2 * r, 4 * g + 2 * r + 1]) if r < 2 else (g, "B", [4 * g + i for i in range(4)])


def build(nc, x_in, wqkv0, wo0, w_ff0, wq1, wkv1, bq1, bkv1, wo1, bo1, w_moe, w_gate,
          c_cos, c_sin, c_ident, c_mask, c_tri, c_sel, c_pick, out):
    ctx = ExitStack()
    with ctx:
        def sb(name, shape, dt=F32):
            return ctx.enter_context(nc.sbuf_tensor(name, shape, dt))

        x = sb("x_res", [P, NSEQ * NT, E])
        wff_hi = sb("wff_hi", [P, WMAX], F32R)
        wff_lo = sb("wff_lo", [P, WMAX], F32R)
        wat_hi = sb("wat_hi", [P, NC * (W0 + E)], F32R)
        wat_lo = sb("wat_lo", [P, NC * (W0 + E)], F32R)
        wstage = sb("wstage", [P, WD_CHUNK])
        cos = sb("cos", [P, NT, HD])
        sin = sb("sin", [P, NT, HD])
        ident = sb("ident", [P, P])
        identb = sb("identb", [P, P], BF16)
        maskb = sb("maskb", [P, 4, P], BF16)
        half = sb("minus_half", [P, BT])
        bias = sb("bias_rows", [64, 2 * E], F32R)
        ones = sb("ones_rows", [64, P], F32R)
        wg_hi = sb("wg_hi", [P, NC * NEXP], F32R)
        wg_lo = sb("wg_lo", [P, NC * NEXP], F32R)
        tri = sb("tri", [P, NEXP, NEXP])
        mv = sb("mv", [P, BT, 2])
        st = sb("st", [P, BT, 6])
        rs = sb("rs", [P, 2, BT])
        nmr = sb("nmr", [P, BT])

        ps = [ctx.enter_context(nc.psum_tensor(f"bank{i}", [P, 512], F32)) for i in range(8)]

        setup = Names()
        setup.tick = ctx.enter_context(nc.semaphore("su_tick"))
        setup.x_first = ctx.enter_context(nc.semaphore("su_x_first"))
        setup.x_rest = ctx.enter_context(nc.semaphore("su_x_rest"))
        setup.w_raw = ctx.enter_context(nc.semaphore("su_w_raw"))
        setup.w_hi = ctx.enter_context(nc.semaphore("su_w_hi"))
        setup.w_lo = ctx.enter_context(nc.semaphore("su_w_lo"))
        setup.const = ctx.enter_context(nc.semaphore("su_const"))
        setup.const_cp = ctx.enter_context(nc.semaphore("su_const_cp"))
        setup.raw1 = ctx.enter_context(nc.semaphore("su_raw1"))
        setup.sum1 = ctx.enter_context(nc.semaphore("su_sum1"))
        setup.hi1 = ctx.enter_context(nc.semaphore("su_hi1"))
        setup.lo1 = ctx.enter_context(nc.semaphore("su_lo1"))
        setup.wg = ctx.enter_context(nc.semaphore("su_wg"))
        phase = Names()
        phase.done = ctx.enter_context(nc.semaphore("ph_done"))
        wf = Names()
        wf.in0 = ctx.enter_context(nc.semaphore("wf_in0"))
        wf.hi0 = ctx.enter_context(nc.semaphore("wf_hi0"))
        wf.lo0 = ctx.enter_context(nc.semaphore("wf_lo0"))
        wf.in1 = ctx.enter_context(nc.semaphore("wf_in1"))
        wf.hi1 = ctx.enter_context(nc.semaphore("wf_hi1"))
        wf.lo1 = ctx.enter_context(nc.semaphore("wf_lo1"))
        dram = [nc.dram_tensor(f"scr{b}{p}", [2, 2 * P, T], F32, kind="Internal").ap() for b in range(2) for p in range(2)]
        dram_m = [nc.dram_tensor(f"scrm{p}", [16, 2, T], F32, kind="Internal").ap() for p in range(2)]

        def wqkv_at(w, layer, c, c0, n):
            base = c * W0 if layer == 0 else c * E
            return w[:, base + c0:base + c0 + n]

        def wo_at(w, layer, c):
            base = NC * W0 + c * E if layer == 0 else NC * E
            return w[0:P if layer == 0 else 64, base:base + E]

        def end_of_phase(eng, n):
            eng.drain().then_inc(phase.done, 1)
            eng.wait_ge(phase.done, 5 * n)

        def plain(eng):
            eng.sem_inc(setup.tick, 1)

        def attention(L, region, block_no):
            A = Attn(L)
            H, NG, HB, U, QC = A.H, A.NG, A.HB, A.U, A.QC
            R = region
            S = Names()
            S.ln_st = ctx.enter_context(nc.semaphore(f"a{L}_ln_st"))
            S.ln_mv = ctx.enter_context(nc.semaphore(f"a{L}_ln_mv"))
            S.ln_rs = ctx.enter_context(nc.semaphore(f"a{L}_ln_rs"))
            S.xn = ctx.enter_context(nc.semaphore(f"a{L}_xn"))
            S.xT_ps = ctx.enter_context(nc.semaphore(f"a{L}_xT_ps"))
            S.xT_hi = ctx.enter_context(nc.semaphore(f"a{L}_xT_hi"))
            S.xT_lo = ctx.enter_context(nc.semaphore(f"a{L}_xT_lo"))
            S.qk_ps = ctx.enter_context(nc.semaphore(f"a{L}_qk_ps"))
            S.v_ps = ctx.enter_context(nc.semaphore(f"a{L}_v_ps"))
            S.v_sb = ctx.enter_context(nc.semaphore(f"a{L}_v_sb"))
            S.rope_t = ctx.enter_context(nc.semaphore(f"a{L}_rope_t"))
            S.hold = ctx.enter_context(nc.semaphore(f"a{L}_hold"))
            S.r_ok = ctx.enter_context(nc.semaphore(f"a{L}_r_ok"))
            S.qkT_ps = ctx.enter_context(nc.semaphore(f"a{L}_qkT_ps"))
            S.qkT_hi = ctx.enter_context(nc.semaphore(f"a{L}_qkT_hi"))
            S.qkT_lo = ctx.enter_context(nc.semaphore(f"a{L}_qkT_lo"))
            S.q_out = ctx.enter_context(nc.semaphore(f"a{L}_q_out"))
            S.k_out = ctx.enter_context(nc.semaphore(f"a{L}_k_out"))
            S.half0 = ctx.enter_context(nc.semaphore(f"a{L}_half0"))
            S.half1 = ctx.enter_context(nc.semaphore(f"a{L}_half1"))
            S.rows_ps = ctx.enter_context(nc.semaphore(f"a{L}_rows_ps"))
            S.mx = ctx.enter_context(nc.semaphore(f"a{L}_mx"))
            S.m_ps = ctx.enter_context(nc.semaphore(f"a{L}_m_ps"))
            S.m_hi = ctx.enter_context(nc.semaphore(f"a{L}_m_hi"))
            S.m_lo = ctx.enter_context(nc.semaphore(f"a{L}_m_lo"))
            S.m_out = ctx.enter_context(nc.semaphore(f"a{L}_m_out"))
            S.m_in = ctx.enter_context(nc.semaphore(f"a{L}_m_in"))
            S.main_ps = ctx.enter_context(nc.semaphore(f"a{L}_main_ps"))
            S.ex = ctx.enter_context(nc.semaphore(f"a{L}_ex"))
            S.cz = ctx.enter_context(nc.semaphore(f"a{L}_cz"))
            S.av = ctx.enter_context(nc.semaphore(f"a{L}_av"))
            S.o_sb = ctx.enter_context(nc.semaphore(f"a{L}_o_sb"))
            S.oN_ps = ctx.enter_context(nc.semaphore(f"a{L}_oN_ps"))
            S.rinv = ctx.enter_context(nc.semaphore(f"a{L}_rinv"))
            S.on_sb = ctx.enter_context(nc.semaphore(f"a{L}_on_sb"))
            S.oT_ps = ctx.enter_context(nc.semaphore(f"a{L}_oT_ps"))
            S.oT_hi = ctx.enter_context(nc.semaphore(f"a{L}_oT_hi"))
            S.oT_lo = ctx.enter_context(nc.semaphore(f"a{L}_oT_lo"))
            S.o_ps = ctx.enter_context(nc.semaphore(f"a{L}_o_ps"))
            S.xr = ctx.enter_context(nc.semaphore(f"a{L}_xr"))
            xn = R.xn[L]
            scrq, scrk = dram[0:2], dram[2:4]

            def split_mm(pe, out_, lhs, rhs, start, stop):
                pe.matmul(out_, lhs[0], rhs[0], start=start, stop=False)
                pe.matmul(out_, lhs[0], rhs[1], start=False, stop=False)
                return pe.matmul(out_, lhs[1], rhs[0], start=False, stop=stop)

            def pe_xT(pe, s, bank):
                pe.wait_ge(S.xn, s * 2 + 2)
                for c in range(NC):
                    for j in range(NT):
                        mm = pe.transpose(ps[bank][:, c * T + j * P:c * T + (j + 1) * P],
                                          xn[:, j, c * P:(c + 1) * P], ident[:, :])
                mm.then_inc(S.xT_ps, 1)

            def pe_proj(pe, s, p, bank, c0, n, signal):
                pe.wait_ge(S.xT_lo, s + 1)
                for j in range(NT):
                    o = ps[bank][:, j * T:j * T + n]
                    if L == 1:
                        pe.matmul(o, ones[:, :], bias[:, 0:n], start=True, stop=False)
                    for c in range(NC):
                        xs = [t[:, p, c * T + j * P:c * T + (j + 1) * P] for t in (R.xT_hi, R.xT_lo)]
                        ws = [wqkv_at(w, L, c, c0, n) for w in (wat_hi, wat_lo)]
                        mm = split_mm(pe, o, xs, ws, start=(c == 0 and L == 0), stop=(c == NC - 1))
                mm.then_inc(signal, 1)

            def pe_qkT(pe, s, b, bank):
                pe.wait_ge(S.r_ok, s * A.RB + b + 1)
                for c in range(A.NCH):
                    for j in range(NT):
                        mm = pe.transpose(ps[bank][:, c * T + j * P:c * T + (j + 1) * P],
                                          R.rot[:, b, j, c * P:(c + 1) * P], ident[:, :])
                mm.then_inc(S.qkT_ps, 1)

            def pe_rows(pe, s, p, u):
                g, kind, heads = A.unit(u)
                bank = (U * p + u) % 2
                if heads[0] < HB:
                    pe.wait_ge(S.half0, s * 96 + 96)
                if heads[-1] >= HB:
                    pe.wait_ge(S.half1, s * 96 + 96)
                if not (isinstance(s, int) and U * s + u < 2):
                    pe.wait_ge(S.mx, s * U + (u - 1))
                if kind == "A":
                    o = ps[bank][:, :].rearrange("p (h k) -> p h k", h=2)
                    pe.matmul(o[:, :, P:T], identb[:, :], maskb[:, 0:2, :], start=True, stop=False,
                              skip_group_check=True)
                    for i, h in enumerate(heads):
                        b, sl = A.stack(h)
                        mm = pe.matmul(o[:, i, :], R.Q[b:b + 48, p, sl, P:T], R.K[b:b + 48, p, sl, :],
                                       start=False, stop=True, skip_group_check=True)
                else:
                    o = ps[bank][:, :].rearrange("p (h k) -> p h k", h=4)
                    pe.matmul(o, identb[:, :], maskb[:, :, :], start=True, stop=False,
                              skip_group_check=True)
                    for i, h in enumerate(heads):
                        b, sl = A.stack(h)
                        mm = pe.matmul(o[:, i, :], R.Q[b:b + 48, p, sl, 0:P], R.K[b:b + 48, p, sl, 0:P],
                                       start=False, stop=True, skip_group_check=True)
                mm.then_inc(S.rows_ps, 1)

            def pe_mT(pe, s, p, bank):
                pe.wait_ge(S.mx, s * U + U)
                for j in range(NT):
                    mm = pe.transpose(ps[bank][0:H, j * P:(j + 1) * P], R.negm[:, p, j, 0:H], ident[:, :])
                mm.then_inc(S.m_ps, 1)

            def pe_main(pe, s, p, u):
                g, kind, heads = A.unit(u)
                bank = 2 + (U * p + u) % 2
                if u == 0 and L == 1:
                    pe.wait_ge(S.m_lo, s + 1)
                if u == 0 and L == 0:
                    pe.wait_ge(S.m_in, s * (16 * A.NH) + 16 * A.NH)
                if not (isinstance(s, int) and U * s + u < 2):
                    pe.wait_ge(S.ex, s * U + (u - 1))
                for i, h in enumerate(heads):
                    b, sl = A.stack(h)
                    if kind == "A":
                        o, keys, queries = ps[bank][:, i * T:(i + 1) * T], slice(0, P), slice(0, T)
                    else:
                        o, keys, queries = ps[bank][:, i * P:(i + 1) * P], slice(P, T), slice(P, T)
                    mm = pe.matmul(o, R.K[b:b + A.DEPTH, p, sl, keys], R.Q[b:b + A.DEPTH, p, sl, queries],
                                   start=True, stop=(L == 0))
                    if L == 1:
                        mm = pe.matmul(o, R.pick[:, h, :], R.mT[:, queries], start=False, stop=True)
                mm.then_inc(S.main_ps, 1)

            def pe_av(pe, s, p, g):
                pg = (NG * p + g) % 2
                pe.wait_ge(S.cz, s * NG + g + 1)
                if g == 0:
                    pe.wait_ge(S.v_sb, s + 1)
                if g % 2 == 0 and not (isinstance(s, int) and A.OE * s + g // 2 < 1):
                    pe.wait_ge(S.o_sb, s * A.OE + g // 2)
                c0 = (g % 2) * T if NG > 1 else 0
                for kt in range(2):
                    for i in range(4):
                        h = 4 * g + i
                        o = ps[4][32 * i:32 * i + 32, c0 + kt * P:c0 + T]
                        rhs = R.prob[:, pg, 0:3:2, i, :] if kt == 0 else R.prob[:, pg, 1, i, :]
                        mm = pe.matmul(o, R.v[:, p, kt, h, :], rhs, start=(kt == 0), stop=(kt == 1),
                                       skip_group_check=True)
                mm.then_inc(S.av, 1)

            def pe_oN(pe, s, bank, tiles):
                pe.wait_ge(S.o_sb, s * A.OE + A.OE)
                for n, j in enumerate(tiles):
                    for g in range(NG):
                        mm = pe.transpose(ps[bank][:, (n * NG + g) * P:(n * NG + g + 1) * P],
                                          R.o[:, g, j * P:(j + 1) * P], ident[:, :])
                mm.then_inc(S.oN_ps, 1)

            def pe_oT(pe, s, bank):
                pe.wait_ge(S.on_sb, s * 2 + 2)
                plain(pe)
                w = min(QC, P)
                for c in range(max(1, QC // P)):
                    for j in range(NT):
                        mm = pe.transpose(ps[bank][0:w, c * T + j * P:c * T + (j + 1) * P],
                                          R.on[:, j, c * w:(c + 1) * w], ident[:, :])
                mm.then_inc(S.oT_ps, 1)

            def pe_out(pe, s, bank):
                pe.wait_ge(S.oT_lo, s + 1)
                w, nch = min(QC, P), max(1, QC // P)
                for j in range(NT):
                    o = ps[bank][:, j * E:(j + 1) * E]
                    if L == 1:
                        pe.matmul(o, ones[:, :], bias[:, E:2 * E], start=True, stop=False)
                    for c in range(nch):
                        xs = [t[0:w, c * T + j * P:c * T + (j + 1) * P] for t in (R.oT_hi, R.oT_lo)]
                        mm = split_mm(pe, o, xs, [wo_at(t, L, c) for t in (wat_hi, wat_lo)],
                                      start=(c == 0 and L == 0), stop=(c == nch - 1))
                mm.then_inc(S.o_ps, 1)

            def pe_step0(pe, t, p):
                q = 1 - p

                def units(g, fillers):
                    for i in range(3):
                        if live(t + 1):
                            pe_rows(pe, t + 1, q, 3 * g + i)
                        if g == 0 and live(t - 1):
                            pe_main(pe, t - 1, q, 9 + i)
                        if g > 0 and live(t):
                            pe_main(pe, t, p, 3 * (g - 1) + i)
                        fillers[i]()

                def proj_q():
                    if live(t + 2):
                        pe_proj(pe, t + 2, p, 5, 0, E, S.qk_ps)

                def proj_k():
                    if live(t + 2):
                        if live(t):
                            pe.wait_ge(S.m_lo, t + 1)
                        pe_proj(pe, t + 2, p, 7, E, E, S.qk_ps)

                def out():
                    if live(t - 2):
                        pe_out(pe, t - 2, 6)

                def av_2():
                    if live(t - 1):
                        pe_av(pe, t - 1, q, 2)

                def av_3():
                    if live(t - 1):
                        pe_av(pe, t - 1, q, 3)

                def proj_v():
                    if live(t + 1):
                        if live(t - 2):
                            pe.wait_ge(S.xr, t - 1)
                        pe_proj(pe, t + 1, q, 6, 2 * E, E, S.v_ps)

                def qT():
                    if live(t + 2):
                        pe_qkT(pe, t + 2, 0, 5)

                def kT():
                    if live(t + 2):
                        pe_qkT(pe, t + 2, 1, 7)

                def av_0():
                    if live(t):
                        pe_av(pe, t, p, 0)

                def oN():
                    if live(t - 1):
                        if live(t + 1):
                            pe.wait_ge(S.v_sb, t + 2)
                        elif live(t - 2):
                            pe.wait_ge(S.xr, t - 1)
                        pe_oN(pe, t - 1, 6, [0])
                        if live(t + 2):
                            pe.wait_ge(S.qkT_lo, (t + 2) * 2 + 2)
                        pe_oN(pe, t - 1, 7, [1])

                def xT():
                    if live(t + 3):
                        if live(t + 2):
                            pe.wait_ge(S.qkT_lo, (t + 2) * 2 + 1)
                        pe_xT(pe, t + 3, 5)

                def oT():
                    if live(t - 1):
                        pe_oT(pe, t - 1, 6)

                def av_1_and_maxima():
                    if live(t):
                        pe_av(pe, t, p, 1)
                    if live(t + 1):
                        if live(t - 1):
                            pe.wait_ge(S.on_sb, (t - 1) * 2 + 2)
                        pe_mT(pe, t + 1, q, 7)

                proj_q()
                units(0, [proj_k, out, av_2])
                units(1, [av_3, proj_v, qT])
                units(2, [kT, oN, av_0])
                units(3, [xT, oT, av_1_and_maxima])

            def pe_step1(pe, t, p):
                q = 1 - p
                if live(t + 2):
                    if live(t):
                        pe.wait_ge(S.m_lo, t + 1)
                    pe_qkT(pe, t + 2, 0, 7)
                if live(t):
                    pe_main(pe, t, p, 0)
                    pe_main(pe, t, p, 1)
                if live(t + 3):
                    if live(t + 2):
                        pe.wait_ge(S.r_ok, t + 3)
                        pe.wait_ge(S.hold, t + 3)
                    pe_xT(pe, t + 3, 5)
                if live(t):
                    pe_main(pe, t, p, 2)
                if live(t - 1):
                    if live(t - 2):
                        pe.wait_ge(S.xr, t - 1)
                    pe_oN(pe, t - 1, 6, [0, 1])
                if live(t + 1):
                    pe_rows(pe, t + 1, q, 0)
                    pe_rows(pe, t + 1, q, 1)
                if live(t + 3):
                    pe_proj(pe, t + 3, q, 5, 0, E, S.qk_ps)
                if live(t + 1):
                    pe_rows(pe, t + 1, q, 2)
                if live(t - 1):
                    pe_oT(pe, t - 1, 6)
                if live(t):
                    pe_av(pe, t, p, 0)
                if live(t + 1):
                    if live(t + 2):
                        pe.wait_ge(S.qkT_lo, t + 3)
                    pe_mT(pe, t + 1, q, 7)
                if live(t - 1):
                    pe_out(pe, t - 1, 6)

            def m_rows(r):
                return R.msplit[0:H, r, :] if L == 0 else R.mT[32 * r:32 * r + H, :]

            def act_xn(act, s):
                act.wait_ge(S.ln_rs, s * 4 + 4)
                if live(s - 1) and L == 0:
                    act.wait_ge(S.r_ok, (s - 1) * A.RB + A.RB)
                if live(s - 1) and L == 1:
                    act.wait_ge(S.xT_ps, s)
                for j in range(NT):
                    nc.scalar.activation(xn[:, j:j + 1, :], x[:, cols(2 * s + j, 1), :], ACT.Identity,
                                         bias=nmr[:, j:j + 1], scale=rs[:, 1, j:j + 1]).then_inc(S.xn, 1)

            def act_xT(act, s, p, bank):
                act.wait_ge(S.xT_ps, s + 1)
                if live(s - 2):
                    act.wait_ge(S.v_ps if L == 0 else S.qk_ps, s - 1)
                nc.scalar.copy(R.xT_hi[:, p, :], ps[bank][:, :]).then_inc(S.xT_hi, 1)

            def act_v(act, s, p, bank):
                act.wait_ge(S.v_ps, s + 1)
                if live(s - 2):
                    act.wait_ge(S.av, (s - 2) * NG + NG)
                nc.scalar.copy(R.v[:, p, :, 0:H, 0:HD], ps[bank][:, :]
                               .rearrange("p (j h d) -> p j h d", j=NT, h=H)).then_inc(S.v_sb, 1)

            def act_hold(act, s, p, bank):
                act.wait_ge(S.qk_ps, s + 1)
                if live(s - 2):
                    act.wait_ge(S.v_sb, s - 1)
                src = ps[bank][:, :].rearrange("p (j n) -> p j n", j=NT)[:, :, 2 * QC:3 * QC]
                nc.scalar.copy(R.hold[:, p, :].rearrange("p (j n) -> p j n", j=NT), src).then_inc(S.hold, 1)

            def act_v_from_hold(act, s, p):
                act.wait_ge(S.hold, s + 1)
                if live(s - 2):
                    act.wait_ge(S.av, s - 1)
                nc.scalar.copy(R.v[:, p, :, 0:H, 0:HD], R.hold[:, p, :]
                               .rearrange("p (j h d) -> p j h d", j=NT, h=H)).then_inc(S.v_sb, 1)

            def act_qkT(act, s, b, bank):
                act.wait_ge(S.qkT_ps, s * A.RB + b + 1)
                if live(s - 1):
                    act.wait_ge(S.k_out if b else S.q_out, s * 32)
                n = A.NCH * T
                nc.scalar.copy(R.split[:, b, 0, 0:n], ps[bank][:, 0:n]).then_inc(S.qkT_hi, 1)

            def act_m(act, s, bank):
                act.wait_ge(S.m_ps, s + 1)
                if live(s - 1) and L == 0:
                    act.wait_ge(S.m_out, (s - 1) * 16 + 16)
                if live(s - 1) and L == 1:
                    act.wait_ge(S.main_ps, s * U)
                nc.scalar.copy(m_rows(0), ps[bank][0:H, 0:T]).then_inc(S.m_hi, 1)

            def act_exp(act, s, p, u):
                g, kind, heads = A.unit(u)
                bank, pg = 2 + (U * p + u) % 2, (NG * p + g) % 2
                act.wait_ge(S.main_ps, s * U + u + 1)
                if u % 3 == 0 and not (isinstance(s, int) and NG * s + g < 2):
                    act.wait_ge(S.av, s * NG + (g - 1))
                if kind == "A":
                    i = heads[0] % 4
                    o = R.prob[:, pg, 0:3:2, i:i + 2, :]
                    src = ps[bank][:, :].rearrange("p (h a q) -> p a h q", h=2, a=2)
                else:
                    o = R.prob[:, pg, 1, :, :]
                    src = ps[bank][:, :].rearrange("p (h k) -> p h k", h=4)
                nc.scalar.activation(o, src, ACT.Exp, scale=float(HD) ** -0.5).then_inc(S.ex, 1)

            def act_o(act, s, e):
                n = min(NG, 2)
                act.wait_ge(S.av, s * NG + n * (e + 1))
                if live(s - 1):
                    act.wait_ge(S.oN_ps, s * (2 if L == 0 else 1))
                nc.scalar.copy(R.o[:, n * e:n * (e + 1), :], ps[4][:, 0:n * T]
                               .rearrange("p (g q) -> p g q", g=n)).then_inc(S.o_sb, 1)

            def act_oT(act, s, bank):
                act.wait_ge(S.oT_ps, s + 1)
                if live(s - 1):
                    act.wait_ge(S.o_ps, s)
                w, n = min(QC, P), max(1, QC // P) * T
                nc.scalar.copy(R.oT_hi[0:w, 0:n], ps[bank][0:w, 0:n]).then_inc(S.oT_hi, 1)

            def act_step0(act, t, p):
                q = 1 - p

                def exp(g, i):
                    if g == 0 and live(t - 1):
                        act_exp(act, t - 1, q, 9 + i)
                    if g > 0 and live(t):
                        act_exp(act, t, p, 3 * (g - 1) + i)

                for i in range(3):
                    exp(0, i)
                exp(1, 0)
                if live(t - 1):
                    act_o(act, t - 1, 1)
                exp(1, 1)
                if live(t + 1):
                    act_v(act, t + 1, q, 6)
                exp(1, 2)
                if live(t + 2):
                    act_qkT(act, t + 2, 0, 5)
                exp(2, 0)
                if live(t + 2):
                    act_qkT(act, t + 2, 1, 7)
                exp(2, 1)
                exp(2, 2)
                if live(t + 3):
                    act_xn(act, t + 3)
                exp(3, 0)
                if live(t + 3):
                    act_xT(act, t + 3, q, 5)
                exp(3, 1)
                if live(t - 1):
                    act_oT(act, t - 1, 6)
                exp(3, 2)
                if live(t):
                    act_o(act, t, 0)
                if live(t + 1):
                    act_m(act, t + 1, 7)

            def act_step1(act, t, p):
                q = 1 - p
                if live(t + 2):
                    act_qkT(act, t + 2, 0, 7)
                if live(t):
                    act_exp(act, t, p, 0)
                    act_exp(act, t, p, 1)
                if live(t + 3):
                    act_xT(act, t + 3, q, 5)
                if live(t):
                    act_exp(act, t, p, 2)
                if live(t + 4):
                    act_xn(act, t + 4)
                if live(t + 3):
                    act_hold(act, t + 3, q, 5)
                if live(t - 1):
                    act_oT(act, t - 1, 6)
                if live(t):
                    act_o(act, t, 0)
                if live(t + 1):
                    act_m(act, t + 1, 7)
                if live(t + 2):
                    act_v_from_hold(act, t + 2, p)

            def v_ln(dve, s):
                if L == 0:
                    if isinstance(s, int) and s < 2:
                        dve.wait_ge(setup.x_first, 16)
                    else:
                        dve.wait_ge(setup.x_rest, 16)
                if live(s - 1):
                    dve.wait_ge(S.ln_mv, s * 2)
                for j in range(NT):
                    nc.vector.bn_stats(st[:, j, :], x[:, cols(2 * s + j, 1), :].rearrange("p a e -> p (a e)"))\
                        .then_inc(S.ln_st, 1)
                dve.wait_ge(S.ln_st, s * 2 + 2)
                if live(s - 1):
                    dve.wait_ge(S.ln_rs, (s - 1) * 4 + 4)
                plain(dve)
                for j in range(NT):
                    nc.vector.bn_aggr(mv[:, j, :], st[:, j, :]).then_inc(S.ln_mv, 1)

            def v_xT(dve, s, p, bank):
                dve.wait_ge(S.xT_hi, s + 1)
                nc.vector.tensor_tensor(R.xT_lo[:, p, :], ps[bank][:, :], R.xT_hi[:, p, :].bitcast(F32),
                                        ALU.subtract).then_inc(S.xT_lo, 1)

            def v_rope(dve, s, b, bank):
                dve.wait_ge(S.qk_ps, s * A.RB + b + 1)
                if L == 1:
                    dve.wait_ge(S.hold, s + 1)
                if live(s - 1):
                    dve.wait_ge(S.qkT_ps, (s - 1) * A.RB + b + 1)
                if live(s - 4) and L == 0:
                    dve.wait_ge(S.oT_ps, s - 3)
                n = A.RC
                src = ps[bank][:, :].rearrange("p (j n) -> p j n", j=NT)[:, :, 0:n]\
                    .rearrange("p j (h d) -> p j h d", h=A.RH)
                o1 = R.rot[:, b, :, 0:n].rearrange("p j (h d) -> p j h d", h=A.RH)
                o2 = R.rot2[:, b, :, 0:n].rearrange("p j (h d) -> p j h d", h=A.RH)
                hd = HD // 2
                c_b = cos[:, :, :].rearrange("p j (o d) -> p j o d", o=1).to_broadcast([P, NT, A.RH, HD])
                nc.vector.tensor_tensor(o1, src, c_b, ALU.mult).then_inc(S.rope_t, 1)
                for a, z in ((0, hd), (hd, 0)):
                    s_b = sin[:, :, a:a + hd].rearrange("p j (o d) -> p j o d", o=1)\
                        .to_broadcast([P, NT, A.RH, hd])
                    nc.vector.tensor_tensor(o2[:, :, :, a:a + hd], src[:, :, :, z:z + hd], s_b,
                                            ALU.mult).then_inc(S.rope_t, 1)

            def v_qkT(dve, s, b, bank):
                dve.wait_ge(S.qkT_hi, s * A.RB + b + 1)
                n = A.NCH * T
                nc.vector.tensor_tensor(R.split[:, b, 1, 0:n], ps[bank][:, 0:n],
                                        R.split[:, b, 0, 0:n].bitcast(F32),
                                        ALU.subtract).then_inc(S.qkT_lo, 1)

            def v_max(dve, s, p, u):
                g, kind, heads = A.unit(u)
                bank = (U * p + u) % 2
                dve.wait_ge(S.rows_ps, s * U + u + 1)
                if u == 0:
                    if live(s - 2):
                        dve.wait_ge(S.m_ps, s - 1)
                j, n = (1, 2) if kind == "A" else (0, 4)
                nc.vector.tensor_reduce(R.negm[:, p, j, heads[0]:heads[0] + n],
                                        ps[bank][:, :].rearrange("p (h k) -> p h k", h=n),
                                        axis=AX.X, op=ALU.max, negate=True).then_inc(S.mx, 1)

            def v_m(dve, s, bank):
                dve.wait_ge(S.m_hi, s + 1)
                nc.vector.tensor_tensor(m_rows(1), ps[bank][0:H, 0:T], m_rows(0).bitcast(F32),
                                        ALU.subtract).then_inc(S.m_lo, 1)

            def v_on(dve, s, bank, tiles):
                dve.wait_ge(S.oN_ps, s * (2 // len(tiles)) + tiles[0] + 1)
                if L == 0 and live(s + 3):
                    dve.wait_ge(S.r_ok, (s + 3) * A.RB + A.RB)
                if L == 1 and live(s - 1):
                    dve.wait_ge(S.oT_ps, s)
                for n, j in enumerate(tiles):
                    src = ps[bank][:, n * NG * P:(n + 1) * NG * P].rearrange("p (h d) -> p h d", h=H)
                    nc.vector.reciprocal(R.rinv[:, j, 0:H].rearrange("p (h o) -> p h o", o=1),
                                         src[:, :, HD:HD + 1]).then_inc(S.rinv, 1)
                for n, j in enumerate(tiles):
                    src = ps[bank][:, n * NG * P:(n + 1) * NG * P].rearrange("p (h d) -> p h d", h=H)
                    dve.wait_ge(S.rinv, s * 2 + j + 1)
                    r_b = R.rinv[:, j, 0:H].rearrange("p (h o) -> p h o", o=1).to_broadcast([P, H, HD])
                    nc.vector.tensor_tensor(R.on[:, j, 0:QC].rearrange("p (h d) -> p h d", h=H),
                                            src[:, :, 0:HD], r_b, ALU.mult).then_inc(S.on_sb, 1)

            def v_oT(dve, s, bank):
                dve.wait_ge(S.oT_hi, s + 1)
                w, n = min(QC, P), max(1, QC // P) * T
                nc.vector.tensor_tensor(R.oT_lo[0:w, 0:n], ps[bank][0:w, 0:n],
                                        R.oT_hi[0:w, 0:n].bitcast(F32), ALU.subtract).then_inc(S.oT_lo, 1)

            def v_res(dve, s, bank):
                dve.wait_ge(S.o_ps, s + 1)
                xs = x[:, cols(2 * s, 2), :]
                nc.vector.tensor_tensor(xs, ps[bank][:, :].rearrange("p (j e) -> p j e", j=NT), xs,
                                        ALU.add).then_inc(S.xr, 1)

            def v_step0(dve, t, p):
                q = 1 - p

                def maximum(g, i):
                    if live(t + 1):
                        v_max(dve, t + 1, q, 3 * g + i)

                if live(t + 2):
                    v_rope(dve, t + 2, 0, 5)
                maximum(0, 0)
                if live(t + 2):
                    v_rope(dve, t + 2, 1, 7)
                maximum(0, 1)
                if live(t - 2):
                    v_res(dve, t - 2, 6)
                maximum(0, 2)
                maximum(1, 0)
                maximum(1, 1)
                if live(t + 3):
                    v_ln(dve, t + 3)
                maximum(1, 2)
                if live(t + 2):
                    v_qkT(dve, t + 2, 0, 5)
                maximum(2, 0)
                if live(t + 2):
                    v_qkT(dve, t + 2, 1, 7)
                maximum(2, 1)
                if live(t - 1):
                    v_on(dve, t - 1, 6, [0])
                    v_on(dve, t - 1, 7, [1])
                maximum(2, 2)
                maximum(3, 0)
                if live(t + 3):
                    v_xT(dve, t + 3, q, 5)
                maximum(3, 1)
                if live(t - 1):
                    v_oT(dve, t - 1, 6)
                maximum(3, 2)
                if live(t + 1):
                    v_m(dve, t + 1, 7)

            def v_step1(dve, t, p):
                q = 1 - p
                if live(t + 2):
                    v_qkT(dve, t + 2, 0, 7)
                if live(t + 4):
                    v_ln(dve, t + 4)
                if live(t + 3):
                    v_xT(dve, t + 3, q, 5)
                if live(t - 1):
                    v_on(dve, t - 1, 6, [0, 1])
                if live(t + 1):
                    v_max(dve, t + 1, q, 0)
                    v_max(dve, t + 1, q, 1)
                if live(t + 3):
                    v_rope(dve, t + 3, 0, 5)
                if live(t + 1):
                    v_max(dve, t + 1, q, 2)
                if live(t - 1):
                    v_oT(dve, t - 1, 6)
                if live(t + 1):
                    v_m(dve, t + 1, 7)
                if live(t - 1):
                    v_res(dve, t - 1, 6)

            def p_ln(pool, s):
                pool.wait_ge(S.ln_mv, s * 2 + 2)
                if live(s - 1):
                    pool.wait_ge(S.xn, (s - 1) * 2 + 2)
                plain(pool)
                nc.gpsimd.tensor_scalar(rs[:, 0, 0:NT], mv[:, 0:NT, 1], EPS, None, ALU.add).then_inc(S.ln_rs, 1)
                pool.wait_ge(S.ln_rs, s * 4 + 1)
                nc.gpsimd.tensor_tensor(rs[:, 1, 0:NT], rs[:, 0, 0:NT], half[:, 0:NT], ALU.pow).then_inc(S.ln_rs, 1)
                pool.wait_ge(S.ln_rs, s * 4 + 2)
                plain(pool)
                for j in range(NT):
                    nc.gpsimd.tensor_scalar(nmr[:, j:j + 1], mv[:, j, 0:1], rs[:, 1, j:j + 1], -1.0,
                                            ALU.mult, ALU.mult).then_inc(S.ln_rs, 1)

            def p_rope(pool, s, b):
                pool.wait_ge(S.rope_t, s * (3 * A.RB) + 3 * (b + 1))
                nc.gpsimd.tensor_tensor(R.rot[:, b, :, 0:A.RC], R.rot[:, b, :, 0:A.RC],
                                        R.rot2[:, b, :, 0:A.RC], ALU.add).then_inc(S.r_ok, 1)

            def p_causal(pool, s, p, g):
                pg = (NG * p + g) % 2
                pool.wait_ge(S.ex, s * U + 3 * (g + 1))
                v = R.prob[:, pg, 0:2, :, :].rearrange("p a h q -> p (a h) q")
                plain(pool)
                nc.gpsimd.affine_select(out=v, in_=v, compare_op=ALU.is_ge, fill=0.0, base=0,
                                        pattern=[[0, 8], [1, P]], channel_multiplier=-1)\
                    .then_inc(S.cz, 1)

            def p_weights(pool, n):
                chunk = WB_CHUNK if L == 0 else WD_CHUNK
                w_in, w_hi, w_lo = (wf.in0, wf.hi0, wf.lo0) if L == 0 else (wf.in1, wf.hi1, wf.lo1)
                pool.wait_ge(w_in, n * 16 + 16)
                hi, lo = (w[:, cols(n * chunk, chunk)] for w in (wff_hi, wff_lo))
                nc.gpsimd.tensor_copy(hi, wstage[:, 0:chunk]).then_inc(w_hi, 1)
                pool.wait_ge(w_hi, n + 1)
                nc.gpsimd.tensor_tensor(lo, wstage[:, 0:chunk], hi.bitcast(F32), ALU.subtract).then_inc(w_lo, 1)

            def p_step0(pool, t, p):
                if live(t + 2):
                    p_rope(pool, t + 2, 0)
                if live(t - 1):
                    p_causal(pool, t - 1, 1 - p, 3)
                if live(t + 2):
                    p_rope(pool, t + 2, 1)
                if live(t):
                    p_causal(pool, t, p, 0)
                if live(t + 3):
                    p_ln(pool, t + 3)
                if live(t):
                    p_causal(pool, t, p, 1)
                if live(t + 2):
                    p_weights(pool, t + 2)
                if live(t):
                    p_causal(pool, t, p, 2)

            def p_step1(pool, t, p):
                if live(t + 4):
                    p_ln(pool, t + 4)
                if live(t):
                    p_causal(pool, t, p, 0)
                if live(t + 3):
                    p_rope(pool, t + 3, 0)
                if live(t + 2):
                    p_weights(pool, t + 2)

            def sp_weights(sp, n):
                chunk = WB_CHUNK if L == 0 else WD_CHUNK
                src, w_in, w_lo = (w_ff0, wf.in0, wf.lo0) if L == 0 else (w_moe, wf.in1, wf.lo1)
                if live(n - 1):
                    sp.wait_ge(w_lo, n)
                sp.dma_start(wstage[:, 0:chunk], src[:, cols(n * chunk, chunk)]).then_inc(w_in, 16)

            def sp_out(sp, s, b, p):
                sp.wait_ge(S.qkT_lo, s * A.RB + b + 1)
                n = A.NCH * T
                for r in range(2):
                    sp.dma_start((scrk if b else scrq)[p][r].rearrange("(c p) t -> p c t", p=P)[:, 0:A.NCH, :],
                                 R.split[:, b, r, 0:n].bitcast(F32).rearrange("p (c t) -> p c t", t=T))\
                        .then_inc((S.k_out if b else S.q_out), 16)

            def sp_half(sp, s, hf, p):
                done = S.half1 if hf else S.half0
                for stack, srcs, lay in ((R.Q, scrq, (0, 1, 0)), (R.K, scrk, (0, 0, 1))):
                    if L == 1:
                        srcs = scrq
                    row0 = hf * HB * HD + (QC if L == 1 and stack is R.K else 0)
                    for i, r in enumerate(lay):
                        src = srcs[p][r, row0:row0 + HB * HD, :].rearrange("(h d) t -> d h t", h=HB)
                        b0 = 64 * hf + HD * i
                        sp.dma_start(stack[b0:b0 + HD, p, 0:HB, :].bitcast(F32), src).then_inc(done, 16)

            def sp_maxima(sp, s, p):
                sp.wait_ge(S.m_lo, s + 1)
                sp.dma_start(dram_m[p][0:H], R.msplit[0:H, :, :].bitcast(F32)).then_inc(S.m_out, 16)
                sp.wait_ge(S.m_out, s * 16 + 16)
                for hf in range(A.NH):
                    src = dram_m[p][hf * HB:(hf + 1) * HB].rearrange("h r t -> r h t")
                    sp.dma_start(R.Q[64 * hf + 48:64 * hf + 50, p, 0:HB, :].bitcast(F32), src)\
                        .then_inc(S.m_in, 16)

            def sp_step0(sp, t, p):
                q = 1 - p
                if live(t):
                    sp_maxima(sp, t, p)
                if live(t + 1):
                    if live(t - 1):
                        sp.wait_ge(S.main_ps, (t - 1) * U + U)
                    sp_half(sp, t + 1, 1, q)
                if live(t + 2):
                    sp_weights(sp, t + 2)
                    sp_out(sp, t + 2, 0, p)
                    sp_out(sp, t + 2, 1, p)
                    sp.wait_ge(S.q_out, (t + 2) * 32 + 32)
                    sp.wait_ge(S.k_out, (t + 2) * 32 + 32)
                    if live(t):
                        sp.wait_ge(S.main_ps, t * U + U // 2)
                    sp_half(sp, t + 2, 0, p)

            def sp_step1(sp, t, p):
                if live(t + 2):
                    sp_out(sp, t + 2, 0, p)
                    sp_weights(sp, t + 2)
                    sp.wait_ge(S.q_out, (t + 2) * 32 + 32)
                    if live(t):
                        sp.wait_ge(S.main_ps, t * U + U)
                    sp_half(sp, t + 2, 0, p)

            return dict(pe=pe_step0 if L == 0 else pe_step1, act=act_step0 if L == 0 else act_step1,
                        dve=v_step0 if L == 0 else v_step1, pool=p_step0 if L == 0 else p_step1,
                        sp=sp_step0 if L == 0 else sp_step1, ahead=3 if L == 0 else 4, behind=2 if L == 0 else 1)

        def run_attention(eng, layer, engine):
            step, ahead, behind = layer[engine], layer["ahead"], layer["behind"]
            first = behind + behind % 2
            end = (NSEQ - ahead) // 2 * 2
            for t in range(-ahead, first):
                step(eng, t, t % 2)
            with eng.Fori(first // 2, end // 2) as i:
                step(eng, i * 2, 0)
                step(eng, i * 2 + 1, 1)
            for t in range(end, NSEQ + behind):
                step(eng, t, t % 2)

        def feed_forward(L, region):
            R = region
            NM = (INTER0 if L == 0 else INTER1) // P
            W1 = 2 * NM * P
            moe = L == 1
            S = Names()
            S.ln_st = ctx.enter_context(nc.semaphore(f"f{L}_ln_st"))
            S.ln_mv = ctx.enter_context(nc.semaphore(f"f{L}_ln_mv"))
            S.ln_rs = ctx.enter_context(nc.semaphore(f"f{L}_ln_rs"))
            S.xn = ctx.enter_context(nc.semaphore(f"f{L}_xn"))
            S.xT_ps = ctx.enter_context(nc.semaphore(f"f{L}_xT_ps"))
            S.xT_hi = ctx.enter_context(nc.semaphore(f"f{L}_xT_hi"))
            S.xT_lo = ctx.enter_context(nc.semaphore(f"f{L}_xT_lo"))
            S.g_ps = ctx.enter_context(nc.semaphore(f"f{L}_g_ps"))
            S.u_ps = ctx.enter_context(nc.semaphore(f"f{L}_u_ps"))
            S.silu = ctx.enter_context(nc.semaphore(f"f{L}_silu"))
            S.hh = ctx.enter_context(nc.semaphore(f"f{L}_hh"))
            S.h_hi = ctx.enter_context(nc.semaphore(f"f{L}_h_hi"))
            S.h_lo = ctx.enter_context(nc.semaphore(f"f{L}_h_lo"))
            S.dn = ctx.enter_context(nc.semaphore(f"f{L}_dn"))
            S.o_ps = ctx.enter_context(nc.semaphore(f"f{L}_o_ps"))
            S.xr = ctx.enter_context(nc.semaphore(f"f{L}_xr"))
            S.stored = ctx.enter_context(nc.semaphore(f"f{L}_stored"))
            S.sc_ps = ctx.enter_context(nc.semaphore(f"f{L}_sc_ps"))
            S.gate = ctx.enter_context(nc.semaphore(f"f{L}_gate"))
            S.tanh = ctx.enter_context(nc.semaphore(f"f{L}_tanh"))
            S.w_ok = ctx.enter_context(nc.semaphore(f"f{L}_w_ok"))
            S.wT_ps = ctx.enter_context(nc.semaphore(f"f{L}_wT_ps"))
            S.wT_hi = ctx.enter_context(nc.semaphore(f"f{L}_wT_hi"))
            S.wT_lo = ctx.enter_context(nc.semaphore(f"f{L}_wT_lo"))
            S.wb_ps = ctx.enter_context(nc.semaphore(f"f{L}_wb_ps"))
            HH = 2 if moe else 1

            def last_user(n, m, depth):
                if m >= depth:
                    return n * NM + m - depth + 1
                return n * NM + 1 - NM + max(k for k in range(NM) if k % depth == m % depth)

            def used_before(n, m, depth):
                return not isinstance(n, int) or last_user(n, m, depth) > 0

            def w_up(w, c, col):
                return w[:, c * W1 + col:c * W1 + col + P]

            def w_down(w, m):
                return w[:, NC * W1 + m * E:NC * W1 + (m + 1) * E]

            def blk_live(n):
                return not isinstance(n, int) or 0 <= n < NB

            def pe_xT(pe, n):
                for c in range(NC):
                    if c == 0:
                        pe.wait_ge(S.xn, n * BT + BT)
                        if moe:
                            if blk_live(n - 1):
                                pe.wait_ge(S.wT_lo, n)
                        else:
                            if blk_live(n - 1):
                                pe.wait_ge(S.xT_lo, (n - 1) * NC + NC)
                    else:
                        pe.wait_ge(S.xT_lo, n * NC + c)
                    for j in range(BT):
                        mm = pe.transpose(ps[6][:, j * P:(j + 1) * P], R.xnF[:, j, c * P:(c + 1) * P], ident[:, :])
                    mm.then_inc(S.xT_ps, 1)

            def pe_scores(pe, n, p):
                pe.wait_ge(S.xT_lo, n * NC + NC)
                for j in range(BT):
                    o = ps[6][:, j * NEXP:(j + 1) * NEXP]
                    for c in range(NC):
                        hi, lo = (t[:, p, c, j * P:(j + 1) * P] for t in (R.xF_hi, R.xF_lo))
                        gh, gl = (w[:, c * NEXP:(c + 1) * NEXP] for w in (wg_hi, wg_lo))
                        pe.matmul(o, hi, gh, start=(c == 0), stop=False)
                        pe.matmul(o, hi, gl, start=False, stop=False)
                        mm = pe.matmul(o, lo, gh, start=False, stop=(c == NC - 1))
                mm.then_inc(S.sc_ps, 1)

            def pe_wT(pe, n):
                pe.wait_ge(S.w_ok, n + 1)
                for j in range(BT):
                    mm = pe.transpose(ps[6][0:NEXP, j * P:(j + 1) * P], R.wexp[:, j, :], ident[:, :])
                mm.then_inc(S.wT_ps, 1)

            def act_xn(act, n):
                act.wait_ge(S.ln_rs, n * (BT + 2) + BT + 2)
                if blk_live(n - 1):
                    act.wait_ge(S.xT_ps, (n - 1) * NC + NC)
                for j in range(BT):
                    nc.scalar.activation(R.xnF[:, j:j + 1, :], x[:, cols(BT * n + j, 1), :], ACT.Identity,
                                         bias=nmr[:, j:j + 1], scale=rs[:, 1, j:j + 1]).then_inc(S.xn, 1)

            def act_xT(act, n, p):
                for c in range(NC):
                    act.wait_ge(S.xT_ps, n * NC + c + 1)
                    if c == 0:
                        if blk_live(n - 2):
                            act.wait_ge(S.u_ps, (n - 2) * NM + NM)
                    nc.scalar.copy(R.xF_hi[:, p, c, :], ps[6][:, :]).then_inc(S.xT_hi, 1)

            def act_wT(act, n, p):
                act.wait_ge(S.wT_ps, n + 1)
                if blk_live(n - 2):
                    act.wait_ge(S.wb_ps, (n - 2) * NM + NM)
                nc.scalar.copy(R.wT[0:NEXP, p, :], ps[6][0:NEXP, :]).then_inc(S.wT_hi, 1)

            def v_ln(dve, n):
                for j in range(BT):
                    nc.vector.bn_stats(st[:, j, :], x[:, cols(BT * n + j, 1), :].rearrange("p a e -> p (a e)"))\
                        .then_inc(S.ln_st, 1)
                dve.wait_ge(S.ln_st, n * BT + BT)
                if blk_live(n - 1):
                    dve.wait_ge(S.ln_rs, (n - 1) * (BT + 2) + BT + 2)
                plain(dve)
                for j in range(BT):
                    nc.vector.bn_aggr(mv[:, j, :], st[:, j, :]).then_inc(S.ln_mv, 1)

            def v_xT(dve, n, p):
                for c in range(NC):
                    dve.wait_ge(S.xT_hi, n * NC + c + 1)
                    nc.vector.tensor_tensor(R.xF_lo[:, p, c, :], ps[6][:, :], R.xF_hi[:, p, c, :].bitcast(F32),
                                            ALU.subtract).then_inc(S.xT_lo, 1)

            NGATE = 9

            def v_gate(dve, n):
                k = [0]

                def link(ins):
                    ins.then_inc(S.gate, 1)
                    k[0] += 1
                    dve.wait_ge(S.gate, n * NGATE + k[0])

                dve.wait_ge(S.sc_ps, n + 1)
                if blk_live(n - 1):
                    if blk_live(n - 1):
                        dve.wait_ge(S.tanh, n)
                sc = R.sc[:, :, :]
                link(nc.vector.tensor_copy(sc, ps[6][:, 0:BT * NEXP].rearrange("p (j e) -> p j e", j=BT)))
                for j in range(BT):
                    mine = R.sc[:, j, :].rearrange("p (e o) -> p e o", o=1).to_broadcast([P, NEXP, NEXP])
                    other = R.sc[:, j:j + 1, :].to_broadcast([P, NEXP, NEXP])
                    ins = nc.vector.tensor_tensor(R.gt[:, j], other, mine, ALU.is_gt)
                    ins2 = nc.vector.tensor_tensor(R.eq[:, j], other, mine, ALU.is_equal)
                link(ins2)
                tri_b = tri[:, :, :].rearrange("p e f -> p (e f)").rearrange("p (o n) -> p o n", o=1)\
                    .to_broadcast([P, BT, NEXP * NEXP])
                gt = R.gt[:, :, :, :].rearrange("p j e f -> p j (e f)")
                eq = R.eq[:, :, :, :].rearrange("p j e f -> p j (e f)")
                link(nc.vector.tensor_tensor(eq, eq, tri_b, ALU.mult))
                link(nc.vector.tensor_tensor(gt, gt, eq, ALU.add))
                link(nc.vector.tensor_reduce(R.rank[:, :, :], R.gt[:, :, :, :], axis=AX.X, op=ALU.add))
                link(nc.vector.tensor_scalar(R.halfsel[:, :, :], R.rank[:, :, :], 2.0, 0.5, ALU.is_lt, ALU.mult))
                link(nc.vector.tensor_tensor(R.tz[:, :, :], R.halfsel[:, :, :], sc, ALU.mult))
                link(nc.vector.tensor_reduce(R.mid[:, :], R.tz[:, :, :], axis=AX.X, op=ALU.add))
                mid_b = R.mid[:, :].rearrange("p (j o) -> p j o", o=1).to_broadcast([P, BT, NEXP])
                link(nc.vector.tensor_tensor(R.tz[:, :, :], sc, mid_b, ALU.subtract))
                dve.wait_ge(S.tanh, n + 1)
                if blk_live(n - 1):
                    dve.wait_ge(S.wT_ps, n)
                nc.vector.scalar_tensor_tensor(out=R.wexp[:, :, :], in0=R.th[:, :, :], scalar=1.0,
                                               in1=R.halfsel[:, :, :], op0=ALU.add, op1=ALU.mult)\
                    .then_inc(S.w_ok, 1)

            def act_tanh(act, n):
                act.wait_ge(S.gate, n * NGATE + NGATE)
                if blk_live(n - 1):
                    act.wait_ge(S.w_ok, n)
                nc.scalar.activation(R.th[:, :, :], R.tz[:, :, :], ACT.Tanh).then_inc(S.tanh, 1)

            def v_wT(dve, n, p):
                dve.wait_ge(S.wT_hi, n + 1)
                nc.vector.tensor_tensor(R.wT[32:32 + NEXP, p, :], ps[6][0:NEXP, :],
                                        R.wT[0:NEXP, p, :].bitcast(F32), ALU.subtract).then_inc(S.wT_lo, 1)

            def p_ln(pool, n):
                k = BT + 2
                pool.wait_ge(S.ln_mv, n * BT + BT)
                if blk_live(n - 1):
                    pool.wait_ge(S.xn, (n - 1) * BT + BT)
                plain(pool)
                nc.gpsimd.tensor_scalar(rs[:, 0, :], mv[:, :, 1], EPS, None, ALU.add).then_inc(S.ln_rs, 1)
                pool.wait_ge(S.ln_rs, n * k + 1)
                nc.gpsimd.tensor_tensor(rs[:, 1, :], rs[:, 0, :], half[:, :], ALU.pow).then_inc(S.ln_rs, 1)
                pool.wait_ge(S.ln_rs, n * k + 2)
                plain(pool)
                for j in range(BT):
                    nc.gpsimd.tensor_scalar(nmr[:, j:j + 1], mv[:, j, 0:1], rs[:, 1, j:j + 1], -1.0,
                                            ALU.mult, ALU.mult).then_inc(S.ln_rs, 1)

            def banks(n_par, m):
                b = 2 * (m % 2)
                return ps[b], ps[b + 1]

            def pe_up(pe, n, p, m):
                if m == 0:
                    pe.wait_ge(S.xT_lo, n * NC + NC)
                    if moe:
                        pe.wait_ge(S.wT_lo, n + 1)
                if used_before(n, m, 2):
                    pe.wait_ge(S.hh, last_user(n, m, 2) * HH)
                g_bank, u_bank = banks(p, m)
                for o, off, signal in ((g_bank, 0, S.g_ps), (u_bank, NM * P, S.u_ps)):
                    for c in range(NC):
                        wh, wl = (w_up(w, c, off + m * P) for w in (wff_hi, wff_lo))
                        xh, xl = R.xF_hi[:, p, c, :], R.xF_lo[:, p, c, :]
                        pe.matmul(o[:, :], wh, xh, start=(c == 0), stop=False)
                        pe.matmul(o[:, :], wh, xl, start=False, stop=False)
                        mm = pe.matmul(o[:, :], wl, xh, start=False, stop=(c == NC - 1))
                    mm.then_inc(signal, 1)
                if moe:
                    if used_before(n, m, 1):
                        pe.wait_ge(S.hh, last_user(n, m, 1) * HH)
                    pe.matmul(ps[7][:, :], R.sel[:, m, :], R.wT[:, p, :], start=True, stop=True)\
                        .then_inc(S.wb_ps, 1)

            def act_silu(act, n, p, m):
                act.wait_ge(S.g_ps, n * NM + m + 1)
                if used_before(n, m, 2):
                    act.wait_ge(S.hh, last_user(n, m, 2) * HH)
                nc.scalar.activation(R.sg[:, m % 2, :], banks(p, m)[0][:, :], ACT.Silu).then_inc(S.silu, 1)

            def act_hi(act, n, m):
                act.wait_ge(S.hh, n * (NM * HH) + HH * (m + 1))
                if used_before(n, m, 4):
                    act.wait_ge(S.dn, last_user(n, m, 4))
                nc.scalar.copy(R.h_hi[:, m % 4, :], R.hf[:, m % 2, :]).then_inc(S.h_hi, 1)

            def v_h(dve, n, p, m):
                dve.wait_ge(S.u_ps, n * NM + m + 1)
                dve.wait_ge(S.silu, n * NM + m + 1)
                if used_before(n, m, 2):
                    dve.wait_ge(S.h_lo, last_user(n, m, 2))
                h = R.hf[:, m % 2, :]
                nc.vector.tensor_tensor(h, banks(p, m)[1][:, :], R.sg[:, m % 2, :], ALU.mult).then_inc(S.hh, 1)
                if moe:
                    dve.wait_ge(S.wb_ps, n * NM + m + 1)
                    dve.wait_ge(S.hh, n * (NM * HH) + HH * m + 1)
                    nc.vector.tensor_tensor(h, ps[7][:, :], h, ALU.mult).then_inc(S.hh, 1)

            def v_lo(dve, n, m):
                dve.wait_ge(S.h_hi, n * NM + m + 1)
                nc.vector.tensor_tensor(R.h_lo[:, m % 4, :], R.hf[:, m % 2, :], R.h_hi[:, m % 4, :].bitcast(F32),
                                        ALU.subtract).then_inc(S.h_lo, 1)

            LAG = 2

            def pe_step(pe, n, p):
                for m in range(NM):
                    if blk_live(n):
                        pe_up(pe, n, p, m)
                    if m < LAG:
                        if blk_live(n - 1):
                            pe_down(pe, n - 1, NM - LAG + m)
                    elif blk_live(n):
                        pe_down(pe, n, m - LAG)
                    if blk_live(n + 1) and m == PREP:
                        pe_xT(pe, n + 1)
                    if moe and blk_live(n + 1):
                        if m == PREP + 1:
                            pe_scores(pe, n + 1, 1 - p)
                        if m == PREP + 3:
                            pe_wT(pe, n + 1)
                    if not blk_live(n) and m == LAG - 1:
                        break

            def pe_down(pe, n, m):
                pe.wait_ge(S.h_lo, n * NM + m + 1)
                if m == 0:
                    if blk_live(n - 1):
                        pe.wait_ge(S.xr, (n - 1) * 2 + 2)
                b = m % 4
                order = [0, 2, 1, 3]
                for j in order:
                    o = ps[4 + j // 2][:, (j % 2) * E:(j % 2 + 1) * E]
                    hi, lo = (t[:, b, j * P:(j + 1) * P] for t in (R.h_hi, R.h_lo))
                    pe.matmul(o, hi, w_down(wff_hi, m), start=(m == 0 and j % 2 == 0), stop=False,
                              skip_group_check=True)
                    pe.matmul(o, hi, w_down(wff_lo, m), start=False, stop=False, skip_group_check=True)
                    mm = pe.matmul(o, lo, w_down(wff_hi, m), start=False, stop=(m == NM - 1 and j % 2 == 1),
                                   skip_group_check=True)
                mm.then_inc(S.dn, 1)

            PREP = 3

            def act_step(act, n, p):
                if not blk_live(n):
                    return
                for m in range(NM):
                    act_silu(act, n, p, m)
                    act_hi(act, n, m)
                    if blk_live(n + 1):
                        if m == PREP - 2:
                            act_xn(act, n + 1)
                        if m == PREP:
                            act_xT(act, n + 1, 1 - p)
                        if moe and m == PREP + 2:
                            act_tanh(act, n + 1)
                        if moe and m == PREP + 3:
                            act_wT(act, n + 1, 1 - p)

            def v_step(dve, n, p):
                for m in range(NM):
                    if blk_live(n):
                        v_h(dve, n, p, m)
                        v_lo(dve, n, m)
                    if blk_live(n + 1) and blk_live(n):
                        if m == PREP - 3:
                            v_ln(dve, n + 1)
                        if m == PREP:
                            v_xT(dve, n + 1, 1 - p)
                        if moe and m == PREP + 2:
                            v_gate(dve, n + 1)
                        if moe and m == PREP + 3:
                            v_wT(dve, n + 1, 1 - p)
                    if m == LAG - 1 and blk_live(n - 1):
                        v_res(dve, n - 1)
                    if not blk_live(n) and m == LAG - 1:
                        break

            def v_res(dve, n):
                dve.wait_ge(S.dn, n * NM + NM)
                for r in range(2):
                    xs = x[:, cols(BT * n + 2 * r, 2), :]
                    nc.vector.tensor_tensor(xs, ps[4 + r][:, :].rearrange("p (j e) -> p j e", j=2), xs,
                                            ALU.add).then_inc(S.xr, 1)

            def p_step(pool, n, p):
                if blk_live(n + 1) and blk_live(n):
                    p_ln(pool, n + 1)

            def sp_step(sp, n, p):
                if moe and blk_live(n - 1):
                    if blk_live(n - 1):
                        sp.wait_ge(S.xr, (n - 1) * 2 + 2)
                    dst = out.rearrange("b (j p) e -> p (b j) e", p=P)
                    sp.dma_start(dst[:, cols(BT * (n - 1), BT), :], x[:, cols(BT * (n - 1), BT), :])\
                        .then_inc(S.stored, 16)

            def prep_first(engine, eng):
                if engine == "dve":
                    v_ln(eng, 0)
                    v_xT(eng, 0, 0)
                    if moe:
                        v_gate(eng, 0)
                        v_wT(eng, 0, 0)
                elif engine == "pool":
                    p_ln(eng, 0)
                elif engine == "act":
                    act_xn(eng, 0)
                    act_xT(eng, 0, 0)
                    if moe:
                        act_tanh(eng, 0)
                        act_wT(eng, 0, 0)
                elif engine == "pe":
                    pe_xT(eng, 0)
                    if moe:
                        pe_scores(eng, 0, 0)
                        pe_wT(eng, 0)

            return dict(pe=pe_step, act=act_step, dve=v_step, pool=p_step, sp=sp_step, first=prep_first,
                        stored=S.stored)

        def run_feed_forward(eng, F, engine):
            step = F[engine]
            F["first"](engine, eng)
            step(eng, 0, 0)
            step(eng, 1, 1)
            with eng.Fori(1, NB // 2 - 1) as i:
                step(eng, i * 2, 0)
                step(eng, i * 2 + 1, 1)
            step(eng, NB - 2, 0)
            step(eng, NB - 1, 1)
            step(eng, NB, 0)

        attn_buffers = ExitStack()

        def ra(name, shape, dt=F32):
            return attn_buffers.enter_context(nc.sbuf_tensor("a_" + name, shape, dt))

        RA = Names()
        RA.xT_hi = ra("xT_hi", [P, 2, NC * T], F32R)
        RA.xT_lo = ra("xT_lo", [P, 2, NC * T], F32R)
        RA.rot = ra("rot", [P, 2, NT, E])
        RA.rot2 = ra("rot2", [P, 2, NT, E])
        RA.split = ra("split", [P, 2, 2, NC * T], F32R)
        RA.Q = ra("Q", [P, 2, 8, T], F32R)
        RA.K = ra("K", [P, 2, 8, T], F32R)
        RA.prob = ra("prob", [P, 2, 3, 4, P])
        RA.v = ra("v", [P, 2, NT, 16, 2 * HD])
        RA.o = ra("o", [P, 4, T])
        RA.oT_hi = ra("oT_hi", [P, NC * T], F32R)
        RA.oT_lo = ra("oT_lo", [P, NC * T], F32R)
        RA.negm = ra("negm", [P, 2, NT, 16])
        RA.msplit = ra("msplit", [16, 2, T], F32R)
        RA.rinv = ra("rinv", [P, NT, 16])
        attn_buffers.close()
        RA.xn, RA.on = (RA.rot2[:, 0], RA.rot[:, 1]), RA.rot2[:, 1]
        RA.mT = RA.Q[0:64, 0, 4, :]
        RA.pick = RA.K[0:64, 0, 4:6, :].rearrange("p s (h k) -> p (s h) k", k=P)
        RA.hold = RA.o[:, 2:4, 0:NT * 4 * HD]

        def rf(name, shape, dt=F32):
            return ctx.enter_context(nc.sbuf_tensor("f_" + name, shape, dt))

        RF = Names()
        RF.xnF = rf("xnF", [P, BT, E])
        RF.xF_hi = rf("xF_hi", [P, 2, NC, BN], F32R)
        RF.xF_lo = rf("xF_lo", [P, 2, NC, BN], F32R)
        RF.sg = rf("sg", [P, 2, BN])
        RF.hf = rf("hf", [P, 2, BN])
        RF.h_hi = rf("h_hi", [P, 4, BN], F32R)
        RF.h_lo = rf("h_lo", [P, 4, BN], F32R)
        RF.sel = rf("sel", [64, INTER1 // P, P], F32R)
        RF.wT = rf("wT", [64, 2, BN], F32R)
        RF.selraw = rf("selraw", [64, INTER1 // P, P])
        RF.sc = rf("sc", [P, BT, NEXP])
        RF.gt = rf("gt", [P, BT, NEXP, NEXP])
        RF.eq = rf("eq", [P, BT, NEXP, NEXP])
        RF.rank = rf("rank", [P, BT, NEXP])
        RF.halfsel = rf("halfsel", [P, BT, NEXP])
        RF.tz = rf("tz", [P, BT, NEXP])
        RF.th = rf("th", [P, BT, NEXP])
        RF.mid = rf("mid", [P, BT])
        RF.wexp = rf("wexp", [P, BT, NEXP])

        A0 = attention(0, RA, 0)
        F0 = feed_forward(0, RF)
        A1 = attention(1, RA, 1)
        F1 = feed_forward(1, RF)

        raw0 = RA.v[:, :, :, :, :].rearrange("p a j h d -> p (a j h d)")
        NW0 = NC * (W0 + E)
        NQ1 = NC * E
        rawm = RA.rot[:, :, :, :].rearrange("p a j e -> p (a j e)")
        rawo = RA.rot2[:, :, :, :].rearrange("p a j e -> p (a j e)")
        sum1 = RA.o[:, 0:2, :].rearrange("p j e -> p (j e)")
        sumb = RA.o[:, 2:4, :].rearrange("p j e -> p (j e)")
        rawg = RA.prob[:, 0, 0, 0, :]
        pickraw = RA.prob[0:64, 1, 0, :, :]

        block = ctx.enter_context(nc.Block())

        @block.sync
        def _(sp):
            x_v = x_in.rearrange("b (j p) e -> p (b j) e", p=P)
            for dst, src in ((cos, c_cos), (sin, c_sin)):
                sp.dma_start(dst[:, :, :], src).then_inc(setup.const, 16)
            sp.dma_start(ident[:, :], c_ident).then_inc(setup.const, 16)
            sp.dma_start(tri[:, :, :], c_tri).then_inc(setup.const, 16)
            sp.dma_start(wstage[:, 0:P], c_mask).then_inc(setup.const, 16)
            sp.dma_start(x[:, 0:2 * NT, :], x_v[:, 0:2 * NT, :]).then_inc(setup.x_first, 16)
            sp.dma_start(raw0[:, 0:NC * W0].rearrange("p (c n) -> p c n", c=NC),
                         wqkv0.rearrange("(c p) n -> p c n", p=P)).then_inc(setup.w_raw, 16)
            sp.dma_start(raw0[:, NC * W0:NW0].rearrange("p (c n) -> p c n", c=NC),
                         wo0.rearrange("(c p) n -> p c n", p=P)).then_inc(setup.w_raw, 16)
            sp.dma_start(x[:, 2 * NT:, :], x_v[:, 2 * NT:, :]).then_inc(setup.x_rest, 16)
            sp.wait_ge(setup.const_cp, 3)
            sp.wait_ge(setup.w_lo, 1)
            run_attention(sp, A0, "sp")
            end_of_phase(sp, 1)
            run_feed_forward(sp, F0, "sp")
            end_of_phase(sp, 2)
            sp.dma_start(rawm[:, 0:2 * E].rearrange("p (c n) -> p c n", c=NC),
                         wq1.rearrange("(c p) n -> p c n", p=P)).then_inc(setup.raw1, 16)
            sp.dma_start(rawm[:, 2 * E:2 * E + 2 * P].rearrange("p (c n) -> p c n", c=NC),
                         wkv1.rearrange("(c p) n -> p c n", p=P)).then_inc(setup.raw1, 16)
            sp.dma_start(rawo[0:64, 0:E], wo1).then_inc(setup.raw1, 16)
            sp.dma_start(rawg[:, 0:NC * NEXP].rearrange("p (c n) -> p c n", c=NC),
                         w_gate.rearrange("(c p) n -> p c n", p=P)).then_inc(setup.raw1, 16)
            sp.dma_start(pickraw, c_pick).then_inc(setup.raw1, 16)
            sp.wait_ge(setup.sum1, 2)
            for row in (0, 32):
                sp.dma_start(rawo[row:row + 1, E:2 * E], bq1).then_inc(setup.raw1, 16)
                sp.dma_start(rawo[row:row + 1, 2 * E:2 * E + P], bkv1).then_inc(setup.raw1, 16)
                sp.dma_start(rawo[row:row + 1, 3 * E:4 * E], bo1).then_inc(setup.raw1, 16)
            sp.wait_ge(setup.lo1, 4)
            run_attention(sp, A1, "sp")
            end_of_phase(sp, 3)
            sp.dma_start(RF.selraw[:, :, :], c_sel).then_inc(setup.wg, 16)
            run_feed_forward(sp, F1, "sp")
            sp.wait_ge(F1["stored"], 16 * NB)
            end_of_phase(sp, 4)

        @block.gpsimd
        def _(pool):
            nc.gpsimd.memset(half[:, :], -0.5)
            pool.wait_ge(setup.w_lo, 1)
            nc.gpsimd.memset(RA.v[:, :, :, :, HD:2 * HD], 1.0)
            pool.drain().then_inc(setup.hi1, 1)
            pool.wait_ge(setup.const_cp, 3)
            run_attention(pool, A0, "pool")
            end_of_phase(pool, 1)
            run_feed_forward(pool, F0, "pool")
            end_of_phase(pool, 2)
            nc.gpsimd.memset(RA.v[:, :, :, :, HD:2 * HD], 1.0)
            pool.drain().then_inc(setup.hi1, 1)
            run_attention(pool, A1, "pool")
            end_of_phase(pool, 3)
            run_feed_forward(pool, F1, "pool")
            end_of_phase(pool, 4)

        @block.scalar
        def _(act):
            act.wait_ge(setup.w_raw, 32)
            nc.scalar.copy(wat_hi[:, 0:NW0], raw0[:, 0:NW0]).then_inc(setup.w_hi, 1)
            act.wait_ge(setup.hi1, 1)
            run_attention(act, A0, "act")
            end_of_phase(act, 1)
            run_feed_forward(act, F0, "act")
            end_of_phase(act, 2)
            act.wait_ge(setup.hi1, 2)
            run_attention(act, A1, "act")
            end_of_phase(act, 3)
            run_feed_forward(act, F1, "act")
            end_of_phase(act, 4)

        @block.vector
        def _(dve):
            dve.wait_ge(setup.const, 80)
            nc.vector.tensor_copy(identb[:, :], ident[:, :]).then_inc(setup.const_cp, 1)
            nc.vector.tensor_copy(maskb[:, :, :], wstage[:, 0:P].rearrange("p (o n) -> p o n", o=1)
                                  .to_broadcast([P, 4, P])).then_inc(setup.const_cp, 1)
            nc.vector.memset(ones[:, :].bitcast(F32), 1.0).then_inc(setup.const_cp, 1)
            dve.wait_ge(setup.w_hi, 1)
            nc.vector.tensor_tensor(wat_lo[:, 0:NW0], raw0[:, 0:NW0], wat_hi[:, 0:NW0].bitcast(F32),
                                    ALU.subtract)
            for b in (32, 96):
                nc.vector.memset(RA.K[b:b + 32, :, :, :].bitcast(F32), 1.0)
            dve.drain().then_inc(setup.w_lo, 1)
            run_attention(dve, A0, "dve")
            end_of_phase(dve, 1)
            run_feed_forward(dve, F0, "dve")
            end_of_phase(dve, 2)
            nc.vector.memset(rawo[0:64, E:4 * E], 0.0).then_inc(setup.sum1, 1)
            nc.vector.memset(RA.mT.bitcast(F32), 0.0)
            dve.drain().then_inc(setup.sum1, 1)
            dve.wait_ge(setup.raw1, 16 * 11)
            nc.vector.memset(sum1[:, :], 0.0)
            nc.vector.memset(sumb[0:64, :], 0.0)
            dve.drain().then_inc(setup.sum1, 1)
            dve.wait_ge(setup.sum1, 3)
            for c in range(NC):
                nc.vector.tensor_reduce(
                    sum1[:, c * E:c * E + 64].rearrange("p (k d) -> p k d", k=4),
                    rawm[:, c * E:(c + 1) * E].rearrange("p (k g d) -> p k d g", k=4, g=4), axis=AX.X, op=ALU.add)
                nc.vector.tensor_copy(sum1[:, c * E + 64:c * E + 192], rawm[:, 2 * E + c * P:2 * E + (c + 1) * P])
            nc.vector.tensor_reduce(sumb[0:64, 0:64].rearrange("p (k d) -> p k d", k=4),
                                    rawo[0:64, E:2 * E].rearrange("p (k g d) -> p k d g", k=4, g=4),
                                    axis=AX.X, op=ALU.add)
            nc.vector.tensor_copy(sumb[0:64, 64:192], rawo[0:64, 2 * E:2 * E + P])
            nc.vector.tensor_copy(sumb[0:64, E:2 * E], rawo[0:64, 3 * E:4 * E])
            dve.drain().then_inc(setup.sum1, 1)
            dve.wait_ge(setup.sum1, 4)
            nc.vector.tensor_copy(wat_hi[:, 0:NQ1], sum1[:, :])
            nc.vector.tensor_copy(wat_hi[0:64, NQ1:NQ1 + E], rawo[0:64, 0:E])
            nc.vector.tensor_copy(RA.pick, pickraw)
            nc.vector.tensor_copy(wg_hi[:, :], rawg[:, 0:NC * NEXP])
            nc.vector.tensor_copy(bias[:, :], sumb[0:64, :])
            dve.drain().then_inc(setup.lo1, 1)
            dve.wait_ge(setup.lo1, 1)
            nc.vector.tensor_tensor(wat_lo[:, 0:NQ1], sum1[:, :], wat_hi[:, 0:NQ1].bitcast(F32), ALU.subtract)
            nc.vector.tensor_tensor(wat_lo[0:64, NQ1:NQ1 + E], rawo[0:64, 0:E],
                                    wat_hi[0:64, NQ1:NQ1 + E].bitcast(F32), ALU.subtract)
            nc.vector.tensor_tensor(wg_lo[:, :], rawg[:, 0:NC * NEXP], wg_hi[:, :].bitcast(F32), ALU.subtract)
            nc.vector.tensor_tensor(bias[32:64, :], sumb[32:64, :], bias[32:64, :].bitcast(F32), ALU.subtract)
            dve.drain().then_inc(setup.lo1, 3)
            dve.wait_ge(setup.lo1, 4)
            run_attention(dve, A1, "dve")
            end_of_phase(dve, 3)
            dve.wait_ge(setup.wg, 16)
            nc.vector.tensor_copy(RF.sel[:, :, :], RF.selraw[:, :, :])
            nc.vector.memset(RF.wT[:, :, :].bitcast(F32), 0.0)
            dve.drain().then_inc(setup.wg, 1)
            dve.wait_ge(setup.wg, 17)
            run_feed_forward(dve, F1, "dve")
            end_of_phase(dve, 4)

        @block.tensor
        def _(pe):
            pe.wait_ge(setup.const_cp, 3)
            pe.wait_ge(setup.w_lo, 1)
            run_attention(pe, A0, "pe")
            end_of_phase(pe, 1)
            run_feed_forward(pe, F0, "pe")
            end_of_phase(pe, 2)
            pe.wait_ge(setup.lo1, 4)
            run_attention(pe, A1, "pe")
            end_of_phase(pe, 3)
            pe.wait_ge(setup.wg, 17)
            run_feed_forward(pe, F1, "pe")
            end_of_phase(pe, 4)


def constants():
    f = np.float32
    inv = (f(1.0) / np.power(f(10000.0), np.arange(0, HD, 2, dtype=f) / f(HD))).astype(f)
    ang = (np.arange(T, dtype=f)[:, None] * inv[None, :]).astype(f)
    c, s = np.cos(ang).astype(f), np.sin(ang).astype(f)
    cos = np.concatenate([c, c], 1).reshape(NT, P, HD).transpose(1, 0, 2)
    sin = np.concatenate([-s, s], 1).reshape(NT, P, HD).transpose(1, 0, 2)
    ident = np.eye(P, dtype=f)
    mask = np.where(np.arange(P)[None, :] > np.arange(P)[:, None], f(MASK), f(0.0)).astype(f)
    tri = np.broadcast_to(np.tril(np.ones((NEXP, NEXP), f), -1), (P, NEXP, NEXP))
    sel = np.zeros((64, INTER1), f)
    for e in range(NEXP):
        sel[e, e * HID:(e + 1) * HID] = 1.0
        sel[32 + e, e * HID:(e + 1) * HID] = 1.0
    sel = sel.reshape(64, INTER1 // P, P)
    pick = np.zeros((64, 4, P), f)
    for h in range(4):
        pick[h, h] = pick[32 + h, h] = 1.0
    return {k: np.ascontiguousarray(v) for k, v in
            dict(c_cos=cos, c_sin=sin, c_ident=ident, c_mask=mask, c_tri=tri, c_sel=sel, c_pick=pick).items()}


def kernel(**inputs):
    import concourse.bacc as bacc
    from concourse.bass_utils import run_bass_kernel_spmd as run

    i = {k: np.asarray(v) for k, v in inputs.items()}
    perm = np.concatenate([np.arange(0, HD, 2), np.arange(1, HD, 2)])

    def heads(w):
        return w.reshape(w.shape[0], -1, HD)[:, :, perm].reshape(w.shape[0], -1)

    def by_partition(w):
        k, n = w.shape
        return w.reshape(k // P, P, n).transpose(1, 0, 2).reshape(P, -1)

    w1 = i["L1_ffn_W1"].reshape(INTER1, E).T
    w2 = i["L1_ffn_W2"].reshape(INTER1, E).T
    w3 = i["L1_ffn_W3"].transpose(0, 2, 1).reshape(INTER1, E)
    arrays = dict(
        x_in=i["L0_attn_x"],
        wqkv0=np.concatenate([i["L0_attn_wq"], i["L0_attn_wk"], i["L0_attn_wv"]], 1),
        wo0=i["L0_attn_wo"],
        w_ff0=np.concatenate([by_partition(i["L0_ffn_w_gate_up"].T), by_partition(i["L0_ffn_w_down"].T)], 1),
        wq1=heads(i["L1_attn_Wq"]),
        wkv1=np.concatenate([heads(i["L1_attn_Wk"]), i["L1_attn_Wv"]], 1),
        bq1=heads(i["L1_attn_bq"][None, :]),
        bkv1=np.concatenate([heads(i["L1_attn_bk"][None, :]), i["L1_attn_bv"][None, :]], 1),
        wo1=i["L1_attn_Wo"],
        bo1=i["L1_attn_bo"][None, :],
        w_moe=np.concatenate([by_partition(np.concatenate([w1, w2], 1)), by_partition(w3)], 1),
        w_gate=i["L1_ffn_Wg"].T,
        **constants(),
    )
    arrays = {k: np.ascontiguousarray(v) for k, v in arrays.items()}
    nc = bacc.Bacc("TRN2", target_bir_lowering=False, num_devices=1)
    args = [nc.dram_tensor(k, v.shape, mybir.dt.from_np(v.dtype), kind="ExternalInput").ap()
            for k, v in arrays.items()]
    out = nc.dram_tensor("out", (NSEQ, T, E), F32, kind="ExternalOutput").ap()
    build(nc, *args, out)
    r = run(nc, [arrays], core_ids=[0])
    return r.results[0]["out"]
```

```python
from contextlib import ExitStack

import numpy as np

import concourse.bass as bass
from concourse import mybir

F32 = mybir.dt.float32
F32R = mybir.dt.float32r
BF16 = mybir.dt.bfloat16
ALU = mybir.AluOpType
ACT = mybir.ActivationFunctionType
AX = mybir.AxisListType

P = 128
NSEQ, T, E = 16, 256, 256
NT = T // P
NC = E // P
HD = 16
EPS = 1e-5
MASK = -1e30
INTER0 = 1024
NEXP, HID = 8, 176
INTER1 = NEXP * HID
NB = 8
BT = 4
BN = BT * P
W0 = 3 * E
WB_CHUNK = (2 * INTER0 * NC + INTER0 // P * E) // NSEQ
WD_CHUNK = (2 * INTER1 * NC + INTER1 // P * E) // NSEQ
WMAX = WD_CHUNK * NSEQ


def cols(start, size):
    return bass.ds(start, size)


class Names:
    pass


def live(seq):
    return not isinstance(seq, int) or 0 <= seq < NSEQ


class Attn:

    def __init__(self, layer):
        self.layer = layer
        self.H = 16 if layer == 0 else 4
        self.NG = self.H // 4
        self.HB = min(8, self.H)
        self.NH = self.H // self.HB
        self.U = 3 * self.NG
        self.QC = self.H * HD
        self.RB = 2 if layer == 0 else 1
        self.RH = 16 if layer == 0 else 8
        self.RC = self.RH * HD
        self.NCH = self.RC // P
        self.DEPTH = 50 if layer == 0 else 48
        self.OE = max(1, self.NG // 2)

    def stack(self, h):
        return 64 * (h // self.HB), h % self.HB

    def unit(self, u):
        g, r = divmod(u, 3)
        return (g, "A", [4 * g + 2 * r, 4 * g + 2 * r + 1]) if r < 2 else (g, "B", [4 * g + i for i in range(4)])


def build(nc, x_in, wqkv0, wo0, w_ff0, wq1, wkv1, bq1, bkv1, wo1, bo1, w_moe, w_gate,
          c_cos, c_sin, c_ident, c_mask, c_tri, c_sel, c_pick, out):
    ctx = ExitStack()
    with ctx:
        def sb(name, shape, dt=F32):
            return ctx.enter_context(nc.sbuf_tensor(name, shape, dt))

        x = sb("x_res", [P, NSEQ * NT, E])
        wff_hi = sb("wff_hi", [P, WMAX], F32R)
        wff_lo = sb("wff_lo", [P, WMAX], F32R)
        wat_hi = sb("wat_hi", [P, NC * (W0 + E)], F32R)
        wat_lo = sb("wat_lo", [P, NC * (W0 + E)], F32R)
        wstage = sb("wstage", [P, WD_CHUNK])
        cos = sb("cos", [P, NT, HD])
        sin = sb("sin", [P, NT, HD])
        ident = sb("ident", [P, P])
        identb = sb("identb", [P, P], BF16)
        maskb = sb("maskb", [P, 4, P], BF16)
        half = sb("minus_half", [P, BT])
        bias = sb("bias_rows", [64, 2 * E], F32R)
        ones = sb("ones_rows", [64, P], F32R)
        wg_hi = sb("wg_hi", [P, NC * NEXP], F32R)
        wg_lo = sb("wg_lo", [P, NC * NEXP], F32R)
        tri = sb("tri", [P, NEXP, NEXP])
        mv = sb("mv", [P, BT, 2])
        st = sb("st", [P, BT, 6])
        rs = sb("rs", [P, 2, BT])
        nmr = sb("nmr", [P, BT])

        ps = [ctx.enter_context(nc.psum_tensor(f"bank{i}", [P, 512], F32)) for i in range(8)]

        setup = Names()
        setup.tick = ctx.enter_context(nc.semaphore("su_tick"))
        setup.x_first = ctx.enter_context(nc.semaphore("su_x_first"))
        setup.x_rest = ctx.enter_context(nc.semaphore("su_x_rest"))
        setup.w_raw = ctx.enter_context(nc.semaphore("su_w_raw"))
        setup.w_hi = ctx.enter_context(nc.semaphore("su_w_hi"))
        setup.k_ones = ctx.enter_context(nc.semaphore("su_k_ones"))
        setup.wo_raw = ctx.enter_context(nc.semaphore("su_wo_raw"))
        setup.w_lo = ctx.enter_context(nc.semaphore("su_w_lo"))
        setup.const = ctx.enter_context(nc.semaphore("su_const"))
        setup.const_cp = ctx.enter_context(nc.semaphore("su_const_cp"))
        setup.raw1 = ctx.enter_context(nc.semaphore("su_raw1"))
        setup.sum1 = ctx.enter_context(nc.semaphore("su_sum1"))
        setup.hi1 = ctx.enter_context(nc.semaphore("su_hi1"))
        setup.lo1 = ctx.enter_context(nc.semaphore("su_lo1"))
        setup.wg = ctx.enter_context(nc.semaphore("su_wg"))
        phase = Names()
        phase.done = ctx.enter_context(nc.semaphore("ph_done"))
        wf = Names()
        wf.in0 = ctx.enter_context(nc.semaphore("wf_in0"))
        wf.hi0 = ctx.enter_context(nc.semaphore("wf_hi0"))
        wf.lo0 = ctx.enter_context(nc.semaphore("wf_lo0"))
        wf.in1 = ctx.enter_context(nc.semaphore("wf_in1"))
        wf.hi1 = ctx.enter_context(nc.semaphore("wf_hi1"))
        wf.lo1 = ctx.enter_context(nc.semaphore("wf_lo1"))
        dram = [nc.dram_tensor(f"scr{b}{p}", [2, 2 * P, T], F32, kind="Internal").ap()
                for b in range(2) for p in range(2)]
        dram_m = [nc.dram_tensor(f"scrm{p}", [16, 2, T], F32, kind="Internal").ap() for p in range(2)]

        def wqkv_at(w, layer, c, c0, n):
            base = c * W0 if layer == 0 else c * E
            return w[:, base + c0:base + c0 + n]

        def wo_at(w, layer, c):
            base = NC * W0 + c * E if layer == 0 else NC * E
            return w[0:P if layer == 0 else 64, base:base + E]

        def end_of_phase(eng, n):
            eng.drain().then_inc(phase.done, 1)
            eng.wait_ge(phase.done, 5 * n)

        def plain(eng):
            eng.sem_inc(setup.tick, 1)

        def attention(L, region):
            A = Attn(L)
            H, NG, HB, U, QC = A.H, A.NG, A.HB, A.U, A.QC
            R = region
            S = Names()
            S.ln_st = ctx.enter_context(nc.semaphore(f"a{L}_ln_st"))
            S.ln_mv = ctx.enter_context(nc.semaphore(f"a{L}_ln_mv"))
            S.ln_rs = ctx.enter_context(nc.semaphore(f"a{L}_ln_rs"))
            S.xn = ctx.enter_context(nc.semaphore(f"a{L}_xn"))
            S.xT_ps = ctx.enter_context(nc.semaphore(f"a{L}_xT_ps"))
            S.xT_hi = ctx.enter_context(nc.semaphore(f"a{L}_xT_hi"))
            S.xT_lo = ctx.enter_context(nc.semaphore(f"a{L}_xT_lo"))
            S.qk_ps = ctx.enter_context(nc.semaphore(f"a{L}_qk_ps"))
            S.v_ps = ctx.enter_context(nc.semaphore(f"a{L}_v_ps"))
            S.v_sb = ctx.enter_context(nc.semaphore(f"a{L}_v_sb"))
            S.rope_terms = ctx.enter_context(nc.semaphore(f"a{L}_rope_terms"))
            S.hold = ctx.enter_context(nc.semaphore(f"a{L}_hold"))
            S.rotated = ctx.enter_context(nc.semaphore(f"a{L}_rotated"))
            S.qkT_ps = ctx.enter_context(nc.semaphore(f"a{L}_qkT_ps"))
            S.qkT_hi = ctx.enter_context(nc.semaphore(f"a{L}_qkT_hi"))
            S.qkT_lo = ctx.enter_context(nc.semaphore(f"a{L}_qkT_lo"))
            S.q_out = ctx.enter_context(nc.semaphore(f"a{L}_q_out"))
            S.k_out = ctx.enter_context(nc.semaphore(f"a{L}_k_out"))
            S.half0 = ctx.enter_context(nc.semaphore(f"a{L}_half0"))
            S.half1 = ctx.enter_context(nc.semaphore(f"a{L}_half1"))
            S.rows_ps = ctx.enter_context(nc.semaphore(f"a{L}_rows_ps"))
            S.row_max = ctx.enter_context(nc.semaphore(f"a{L}_row_max"))
            S.maxT_ps = ctx.enter_context(nc.semaphore(f"a{L}_maxT_ps"))
            S.maxT_hi = ctx.enter_context(nc.semaphore(f"a{L}_maxT_hi"))
            S.maxT_lo = ctx.enter_context(nc.semaphore(f"a{L}_maxT_lo"))
            S.max_out = ctx.enter_context(nc.semaphore(f"a{L}_max_out"))
            S.max_in = ctx.enter_context(nc.semaphore(f"a{L}_max_in"))
            S.main_ps = ctx.enter_context(nc.semaphore(f"a{L}_main_ps"))
            S.exps = ctx.enter_context(nc.semaphore(f"a{L}_exps"))
            S.masked = ctx.enter_context(nc.semaphore(f"a{L}_masked"))
            S.av = ctx.enter_context(nc.semaphore(f"a{L}_av"))
            S.o_sb = ctx.enter_context(nc.semaphore(f"a{L}_o_sb"))
            S.oN_ps = ctx.enter_context(nc.semaphore(f"a{L}_oN_ps"))
            S.rinv = ctx.enter_context(nc.semaphore(f"a{L}_rinv"))
            S.divided = ctx.enter_context(nc.semaphore(f"a{L}_divided"))
            S.oT_ps = ctx.enter_context(nc.semaphore(f"a{L}_oT_ps"))
            S.oT_hi = ctx.enter_context(nc.semaphore(f"a{L}_oT_hi"))
            S.oT_lo = ctx.enter_context(nc.semaphore(f"a{L}_oT_lo"))
            S.o_ps = ctx.enter_context(nc.semaphore(f"a{L}_o_ps"))
            S.residual = ctx.enter_context(nc.semaphore(f"a{L}_residual"))
            xn = R.xn[L]
            scrq, scrk = dram[0:2], dram[2:4]

            def split_mm(pe, out_, lhs, rhs, start, stop):
                pe.matmul(out_, lhs[0], rhs[0], start=start, stop=False)
                pe.matmul(out_, lhs[0], rhs[1], start=False, stop=False)
                return pe.matmul(out_, lhs[1], rhs[0], start=False, stop=stop)

            def pe_xT(pe, s, bank):
                pe.wait_ge(S.xn, s * 2 + 2)
                for c in range(NC):
                    for j in range(NT):
                        mm = pe.transpose(ps[bank][:, c * T + j * P:c * T + (j + 1) * P],
                                          xn[:, j, c * P:(c + 1) * P], ident[:, :])
                mm.then_inc(S.xT_ps, 1)

            def pe_proj(pe, s, p, bank, c0, n, signal):
                pe.wait_ge(S.xT_lo, s + 1)
                for j in range(NT):
                    o = ps[bank][:, j * T:j * T + n]
                    if L == 1:
                        pe.matmul(o, ones[:, :], bias[:, 0:n], start=True, stop=False)
                    for c in range(NC):
                        xs = [t[:, p, c * T + j * P:c * T + (j + 1) * P] for t in (R.xT_hi, R.xT_lo)]
                        ws = [wqkv_at(w, L, c, c0, n) for w in (wat_hi, wat_lo)]
                        mm = split_mm(pe, o, xs, ws, start=(c == 0 and L == 0), stop=(c == NC - 1))
                mm.then_inc(signal, 1)

            def pe_qkT(pe, s, b, bank):
                pe.wait_ge(S.rotated, s * A.RB + b + 1)
                for c in range(A.NCH):
                    for j in range(NT):
                        mm = pe.transpose(ps[bank][:, c * T + j * P:c * T + (j + 1) * P],
                                          R.rot[:, b, j, c * P:(c + 1) * P], ident[:, :])
                mm.then_inc(S.qkT_ps, 1)

            def pe_rows(pe, s, p, u):
                g, kind, heads = A.unit(u)
                bank = (U * p + u) % 2
                if heads[0] < HB:
                    pe.wait_ge(S.half0, s * 96 + 96)
                if heads[-1] >= HB:
                    pe.wait_ge(S.half1, s * 96 + 96)
                if not (isinstance(s, int) and U * s + u < 2):
                    pe.wait_ge(S.row_max, s * U + (u - 1))
                if kind == "A":
                    o = ps[bank][:, :].rearrange("p (h k) -> p h k", h=2)
                    pe.matmul(o[:, :, P:T], identb[:, :], maskb[:, 0:2, :], start=True, stop=False,
                              skip_group_check=True)
                    for i, h in enumerate(heads):
                        b, sl = A.stack(h)
                        mm = pe.matmul(o[:, i, :], R.Q[b:b + 48, p, sl, P:T], R.K[b:b + 48, p, sl, :],
                                       start=False, stop=True, skip_group_check=True)
                else:
                    o = ps[bank][:, :].rearrange("p (h k) -> p h k", h=4)
                    pe.matmul(o, identb[:, :], maskb[:, :, :], start=True, stop=False,
                              skip_group_check=True)
                    for i, h in enumerate(heads):
                        b, sl = A.stack(h)
                        mm = pe.matmul(o[:, i, :], R.Q[b:b + 48, p, sl, 0:P], R.K[b:b + 48, p, sl, 0:P],
                                       start=False, stop=True, skip_group_check=True)
                mm.then_inc(S.rows_ps, 1)

            def pe_mT(pe, s, p, bank):
                pe.wait_ge(S.row_max, s * U + U)
                for j in range(NT):
                    mm = pe.transpose(ps[bank][0:H, j * P:(j + 1) * P], R.negm[:, p, j, 0:H], ident[:, :])
                mm.then_inc(S.maxT_ps, 1)

            def pe_main(pe, s, p, u):
                g, kind, heads = A.unit(u)
                bank = 2 + (U * p + u) % 2
                if u == 0 and L == 1:
                    pe.wait_ge(S.maxT_lo, s + 1)
                if u == 0 and L == 0:
                    pe.wait_ge(S.max_in, s * (16 * A.NH) + 16 * A.NH)
                if not (isinstance(s, int) and U * s + u < 2):
                    pe.wait_ge(S.exps, s * U + (u - 1))
                for i, h in enumerate(heads):
                    b, sl = A.stack(h)
                    if kind == "A":
                        o, keys, queries = ps[bank][:, i * T:(i + 1) * T], slice(0, P), slice(0, T)
                    else:
                        o, keys, queries = ps[bank][:, i * P:(i + 1) * P], slice(P, T), slice(P, T)
                    mm = pe.matmul(o, R.K[b:b + A.DEPTH, p, sl, keys], R.Q[b:b + A.DEPTH, p, sl, queries],
                                   start=True, stop=(L == 0))
                    if L == 1:
                        mm = pe.matmul(o, R.pick[h], R.mT[:, queries], start=False, stop=True)
                mm.then_inc(S.main_ps, 1)

            def pe_av(pe, s, p, g):
                pg = (NG * p + g) % 2
                pe.wait_ge(S.masked, s * NG + g + 1)
                if g == 0:
                    pe.wait_ge(S.v_sb, s + 1)
                if g % 2 == 0 and not (isinstance(s, int) and A.OE * s + g // 2 < 1):
                    pe.wait_ge(S.o_sb, s * A.OE + g // 2)
                c0 = (g % 2) * T if NG > 1 else 0
                for kt in range(2):
                    for i in range(4):
                        h = 4 * g + i
                        o = ps[4][32 * i:32 * i + 32, c0 + kt * P:c0 + T]
                        rhs = R.prob[:, pg, 0:3:2, i, :] if kt == 0 else R.prob[:, pg, 1, i, :]
                        mm = pe.matmul(o, R.v[:, p, kt, h, :], rhs, start=(kt == 0), stop=(kt == 1),
                                       skip_group_check=True)
                mm.then_inc(S.av, 1)

            def pe_oN(pe, s, bank, tiles):
                pe.wait_ge(S.o_sb, s * A.OE + A.OE)
                for n, j in enumerate(tiles):
                    for g in range(NG):
                        mm = pe.transpose(ps[bank][:, (n * NG + g) * P:(n * NG + g + 1) * P],
                                          R.o[:, g, j * P:(j + 1) * P], ident[:, :])
                mm.then_inc(S.oN_ps, 1)

            def pe_oT(pe, s, bank):
                pe.wait_ge(S.divided, s * 2 + 2)
                plain(pe)
                w = min(QC, P)
                for c in range(max(1, QC // P)):
                    for j in range(NT):
                        mm = pe.transpose(ps[bank][0:w, c * T + j * P:c * T + (j + 1) * P],
                                          R.on[:, j, c * w:(c + 1) * w], ident[:, :])
                mm.then_inc(S.oT_ps, 1)

            def pe_out(pe, s, bank):
                pe.wait_ge(S.oT_lo, s + 1)
                w, nch = min(QC, P), max(1, QC // P)
                for j in range(NT):
                    o = ps[bank][:, j * E:(j + 1) * E]
                    if L == 1:
                        pe.matmul(o, ones[:, :], bias[:, E:2 * E], start=True, stop=False)
                    for c in range(nch):
                        xs = [t[0:w, c * T + j * P:c * T + (j + 1) * P] for t in (R.oT_hi, R.oT_lo)]
                        mm = split_mm(pe, o, xs, [wo_at(t, L, c) for t in (wat_hi, wat_lo)],
                                      start=(c == 0 and L == 0), stop=(c == nch - 1))
                mm.then_inc(S.o_ps, 1)

            def pe_step0(pe, t, p):
                q = 1 - p

                def units(g, fillers):
                    for i in range(3):
                        if g == 0 and live(t - 1):
                            pe_main(pe, t - 1, q, 9 + i)
                        if g > 0 and live(t):
                            pe_main(pe, t, p, 3 * (g - 1) + i)
                        if live(t + 1):
                            pe_rows(pe, t + 1, q, 3 * g + i)
                        fillers[i]()

                def proj_q():
                    if live(t + 2):
                        pe_proj(pe, t + 2, p, 5, 0, E, S.qk_ps)

                def proj_k():
                    if live(t + 2):
                        if live(t):
                            pe.wait_ge(S.maxT_lo, t + 1)
                        pe_proj(pe, t + 2, p, 7, E, E, S.qk_ps)

                def out():
                    if live(t - 2):
                        pe_out(pe, t - 2, 6)

                def av_2():
                    if live(t - 1):
                        pe_av(pe, t - 1, q, 2)

                def av_3():
                    if live(t - 1):
                        pe_av(pe, t - 1, q, 3)

                def proj_v():
                    if live(t + 1):
                        if live(t - 2):
                            pe.wait_ge(S.residual, t - 1)
                        pe_proj(pe, t + 1, q, 6, 2 * E, E, S.v_ps)

                def qT():
                    if live(t + 2):
                        pe_qkT(pe, t + 2, 0, 5)

                def kT():
                    if live(t + 2):
                        pe_qkT(pe, t + 2, 1, 7)

                def av_0():
                    if live(t):
                        pe_av(pe, t, p, 0)

                def oN():
                    if live(t - 1):
                        if live(t + 1):
                            pe.wait_ge(S.v_sb, t + 2)
                        elif live(t - 2):
                            pe.wait_ge(S.residual, t - 1)
                        pe_oN(pe, t - 1, 6, [0])
                        if live(t + 2):
                            pe.wait_ge(S.qkT_lo, (t + 2) * 2 + 2)
                        pe_oN(pe, t - 1, 7, [1])

                def xT():
                    if live(t + 3):
                        if live(t + 2):
                            pe.wait_ge(S.qkT_lo, (t + 2) * 2 + 1)
                        pe_xT(pe, t + 3, 5)

                def oT():
                    if live(t - 1):
                        pe_oT(pe, t - 1, 6)

                def av_1_and_maxima():
                    if live(t):
                        pe_av(pe, t, p, 1)
                    if live(t + 1):
                        if live(t - 1):
                            pe.wait_ge(S.divided, (t - 1) * 2 + 2)
                        pe_mT(pe, t + 1, q, 7)

                proj_q()
                units(0, [proj_k, av_2, out])
                units(1, [av_3, proj_v, qT])
                units(2, [kT, oN, av_0])
                units(3, [xT, oT, av_1_and_maxima])

            def pe_step1(pe, t, p):
                q = 1 - p
                if live(t + 2):
                    if live(t):
                        pe.wait_ge(S.maxT_lo, t + 1)
                    pe_qkT(pe, t + 2, 0, 7)
                if live(t):
                    pe_main(pe, t, p, 0)
                    pe_main(pe, t, p, 1)
                if live(t + 3):
                    if live(t + 2):
                        pe.wait_ge(S.rotated, t + 3)
                        pe.wait_ge(S.hold, t + 3)
                    pe_xT(pe, t + 3, 5)
                if live(t):
                    pe_main(pe, t, p, 2)
                if live(t - 1):
                    if live(t - 2):
                        pe.wait_ge(S.residual, t - 1)
                    pe_oN(pe, t - 1, 6, [0, 1])
                if live(t + 1):
                    pe_rows(pe, t + 1, q, 0)
                    pe_rows(pe, t + 1, q, 1)
                if live(t + 3):
                    pe_proj(pe, t + 3, q, 5, 0, E, S.qk_ps)
                if live(t + 1):
                    pe_rows(pe, t + 1, q, 2)
                if live(t - 1):
                    pe_oT(pe, t - 1, 6)
                if live(t):
                    pe_av(pe, t, p, 0)
                if live(t + 1):
                    if live(t + 2):
                        pe.wait_ge(S.qkT_lo, t + 3)
                    pe_mT(pe, t + 1, q, 7)
                if live(t - 1):
                    pe_out(pe, t - 1, 6)

            def m_rows(r):
                return R.msplit[0:H, r, :] if L == 0 else R.mT[32 * r:32 * r + H, :]

            def act_xn(act, s):
                act.wait_ge(S.ln_rs, s * 4 + 4)
                if live(s - 1) and L == 0:
                    act.wait_ge(S.rotated, (s - 1) * A.RB + A.RB)
                if live(s - 1) and L == 1:
                    act.wait_ge(S.xT_ps, s)
                for j in range(NT):
                    nc.scalar.activation(xn[:, j:j + 1, :], x[:, cols(2 * s + j, 1), :], ACT.Identity,
                                         bias=nmr[:, j:j + 1], scale=rs[:, 1, j:j + 1]).then_inc(S.xn, 1)

            def act_xT(act, s, p, bank):
                act.wait_ge(S.xT_ps, s + 1)
                if live(s - 2):
                    act.wait_ge(S.v_ps if L == 0 else S.qk_ps, s - 1)
                nc.scalar.copy(R.xT_hi[:, p, :], ps[bank][:, :]).then_inc(S.xT_hi, 1)

            def act_v(act, s, p, bank):
                act.wait_ge(S.v_ps, s + 1)
                if live(s - 2):
                    act.wait_ge(S.av, (s - 2) * NG + NG)
                nc.scalar.copy(R.v[:, p, :, 0:H, 0:HD], ps[bank][:, :]
                               .rearrange("p (j h d) -> p j h d", j=NT, h=H)).then_inc(S.v_sb, 1)

            def act_hold(act, s, p, bank):
                act.wait_ge(S.qk_ps, s + 1)
                if live(s - 2):
                    act.wait_ge(S.v_sb, s - 1)
                src = ps[bank][:, :].rearrange("p (j n) -> p j n", j=NT)[:, :, 2 * QC:3 * QC]
                nc.scalar.copy(R.hold[:, p, :].rearrange("p (j n) -> p j n", j=NT), src).then_inc(S.hold, 1)

            def act_v_from_hold(act, s, p):
                act.wait_ge(S.hold, s + 1)
                if live(s - 2):
                    act.wait_ge(S.av, s - 1)
                nc.scalar.copy(R.v[:, p, :, 0:H, 0:HD], R.hold[:, p, :]
                               .rearrange("p (j h d) -> p j h d", j=NT, h=H)).then_inc(S.v_sb, 1)

            def act_qkT(act, s, b, bank):
                act.wait_ge(S.qkT_ps, s * A.RB + b + 1)
                if live(s - 1):
                    act.wait_ge(S.k_out if b else S.q_out, s * 32)
                n = A.NCH * T
                nc.scalar.copy(R.split[:, b, 0, 0:n], ps[bank][:, 0:n]).then_inc(S.qkT_hi, 1)

            def act_m(act, s, bank):
                act.wait_ge(S.maxT_ps, s + 1)
                if live(s - 1) and L == 0:
                    act.wait_ge(S.max_out, (s - 1) * 16 + 16)
                if live(s - 1) and L == 1:
                    act.wait_ge(S.main_ps, s * U)
                nc.scalar.copy(m_rows(0), ps[bank][0:H, 0:T]).then_inc(S.maxT_hi, 1)

            def act_exp(act, s, p, u):
                g, kind, heads = A.unit(u)
                bank, pg = 2 + (U * p + u) % 2, (NG * p + g) % 2
                act.wait_ge(S.main_ps, s * U + u + 1)
                if u % 3 == 0 and not (isinstance(s, int) and NG * s + g < 2):
                    act.wait_ge(S.av, s * NG + (g - 1))
                if kind == "A":
                    i = heads[0] % 4
                    o = R.prob[:, pg, 0:3:2, i:i + 2, :]
                    src = ps[bank][:, :].rearrange("p (h a q) -> p a h q", h=2, a=2)
                else:
                    o = R.prob[:, pg, 1, :, :]
                    src = ps[bank][:, :].rearrange("p (h k) -> p h k", h=4)
                nc.scalar.activation(o, src, ACT.Exp, scale=float(HD) ** -0.5).then_inc(S.exps, 1)

            def act_o(act, s, e):
                n = min(NG, 2)
                act.wait_ge(S.av, s * NG + n * (e + 1))
                if live(s - 1):
                    act.wait_ge(S.oN_ps, s * (2 if L == 0 else 1))
                nc.scalar.copy(R.o[:, n * e:n * (e + 1), :], ps[4][:, 0:n * T]
                               .rearrange("p (g q) -> p g q", g=n)).then_inc(S.o_sb, 1)

            def act_oT(act, s, bank):
                act.wait_ge(S.oT_ps, s + 1)
                if live(s - 1):
                    act.wait_ge(S.o_ps, s)
                w, n = min(QC, P), max(1, QC // P) * T
                nc.scalar.copy(R.oT_hi[0:w, 0:n], ps[bank][0:w, 0:n]).then_inc(S.oT_hi, 1)

            def act_step0(act, t, p):
                q = 1 - p

                def exp(g, i):
                    if g == 0 and live(t - 1):
                        act_exp(act, t - 1, q, 9 + i)
                    if g > 0 and live(t):
                        act_exp(act, t, p, 3 * (g - 1) + i)

                for i in range(3):
                    exp(0, i)
                exp(1, 0)
                if live(t - 1):
                    act_o(act, t - 1, 1)
                exp(1, 1)
                if live(t + 1):
                    act_v(act, t + 1, q, 6)
                exp(1, 2)
                if live(t + 2):
                    act_qkT(act, t + 2, 0, 5)
                exp(2, 0)
                if live(t + 2):
                    act_qkT(act, t + 2, 1, 7)
                exp(2, 1)
                exp(2, 2)
                if live(t + 3):
                    act_xn(act, t + 3)
                exp(3, 0)
                if live(t + 3):
                    act_xT(act, t + 3, q, 5)
                exp(3, 1)
                if live(t - 1):
                    act_oT(act, t - 1, 6)
                exp(3, 2)
                if live(t + 1):
                    act_m(act, t + 1, 7)
                if live(t):
                    act_o(act, t, 0)

            def act_step1(act, t, p):
                q = 1 - p
                if live(t + 2):
                    act_qkT(act, t + 2, 0, 7)
                if live(t):
                    act_exp(act, t, p, 0)
                    act_exp(act, t, p, 1)
                if live(t + 3):
                    act_xT(act, t + 3, q, 5)
                if live(t):
                    act_exp(act, t, p, 2)
                if live(t + 4):
                    act_xn(act, t + 4)
                if live(t + 3):
                    act_hold(act, t + 3, q, 5)
                if live(t - 1):
                    act_oT(act, t - 1, 6)
                if live(t + 1):
                    act_m(act, t + 1, 7)
                if live(t):
                    act_o(act, t, 0)
                if live(t + 2):
                    act_v_from_hold(act, t + 2, p)

            def v_ln(dve, s):
                if L == 0:
                    if isinstance(s, int) and s < 2:
                        dve.wait_ge(setup.x_first, 16)
                    else:
                        dve.wait_ge(setup.x_rest, 16)
                if live(s - 1):
                    dve.wait_ge(S.ln_mv, s * 2)
                for j in range(NT):
                    nc.vector.bn_stats(st[:, j, :], x[:, cols(2 * s + j, 1), :].rearrange("p a e -> p (a e)"))\
                        .then_inc(S.ln_st, 1)
                dve.wait_ge(S.ln_st, s * 2 + 2)
                if live(s - 1):
                    dve.wait_ge(S.ln_rs, (s - 1) * 4 + 4)
                plain(dve)
                for j in range(NT):
                    nc.vector.bn_aggr(mv[:, j, :], st[:, j, :]).then_inc(S.ln_mv, 1)

            def v_xT(dve, s, p, bank):
                dve.wait_ge(S.xT_hi, s + 1)
                nc.vector.tensor_tensor(R.xT_lo[:, p, :], ps[bank][:, :], R.xT_hi[:, p, :].bitcast(F32),
                                        ALU.subtract).then_inc(S.xT_lo, 1)

            def v_rope(dve, s, b, bank):
                dve.wait_ge(S.qk_ps, s * A.RB + b + 1)
                if L == 1:
                    dve.wait_ge(S.hold, s + 1)
                if live(s - 1):
                    dve.wait_ge(S.qkT_ps, (s - 1) * A.RB + b + 1)
                if live(s - 4) and L == 0:
                    dve.wait_ge(S.oT_ps, s - 3)
                n = A.RC
                src = ps[bank][:, :].rearrange("p (j n) -> p j n", j=NT)[:, :, 0:n]\
                    .rearrange("p j (h d) -> p j h d", h=A.RH)
                o1 = R.rot[:, b, :, 0:n].rearrange("p j (h d) -> p j h d", h=A.RH)
                o2 = R.rot2[:, b, :, 0:n].rearrange("p j (h d) -> p j h d", h=A.RH)
                hd = HD // 2
                c_b = cos[:, :, :].rearrange("p j (o d) -> p j o d", o=1).to_broadcast([P, NT, A.RH, HD])
                nc.vector.tensor_tensor(o1, src, c_b, ALU.mult).then_inc(S.rope_terms, 1)
                for a, z in ((0, hd), (hd, 0)):
                    s_b = sin[:, :, a:a + hd].rearrange("p j (o d) -> p j o d", o=1)\
                        .to_broadcast([P, NT, A.RH, hd])
                    nc.vector.tensor_tensor(o2[:, :, :, a:a + hd], src[:, :, :, z:z + hd], s_b,
                                            ALU.mult).then_inc(S.rope_terms, 1)

            def v_qkT(dve, s, b, bank):
                dve.wait_ge(S.qkT_hi, s * A.RB + b + 1)
                n = A.NCH * T
                nc.vector.tensor_tensor(R.split[:, b, 1, 0:n], ps[bank][:, 0:n],
                                        R.split[:, b, 0, 0:n].bitcast(F32),
                                        ALU.subtract).then_inc(S.qkT_lo, 1)

            def v_max(dve, s, p, u):
                g, kind, heads = A.unit(u)
                bank = (U * p + u) % 2
                dve.wait_ge(S.rows_ps, s * U + u + 1)
                if u == 0:
                    if live(s - 2):
                        dve.wait_ge(S.maxT_ps, s - 1)
                j, n = (1, 2) if kind == "A" else (0, 4)
                nc.vector.tensor_reduce(R.negm[:, p, j, heads[0]:heads[0] + n],
                                        ps[bank][:, :].rearrange("p (h k) -> p h k", h=n),
                                        axis=AX.X, op=ALU.max, negate=True).then_inc(S.row_max, 1)

            def v_m(dve, s, bank):
                dve.wait_ge(S.maxT_hi, s + 1)
                nc.vector.tensor_tensor(m_rows(1), ps[bank][0:H, 0:T], m_rows(0).bitcast(F32),
                                        ALU.subtract).then_inc(S.maxT_lo, 1)

            def v_on(dve, s, bank, tiles):
                dve.wait_ge(S.oN_ps, s * (2 // len(tiles)) + tiles[0] + 1)
                if L == 0 and live(s + 3):
                    dve.wait_ge(S.rotated, (s + 3) * A.RB + A.RB)
                if L == 1 and live(s - 1):
                    dve.wait_ge(S.oT_ps, s)
                for n, j in enumerate(tiles):
                    src = ps[bank][:, n * NG * P:(n + 1) * NG * P].rearrange("p (h d) -> p h d", h=H)
                    nc.vector.reciprocal(R.rinv[:, j, 0:H].rearrange("p (h o) -> p h o", o=1),
                                         src[:, :, HD:HD + 1]).then_inc(S.rinv, 1)
                for n, j in enumerate(tiles):
                    src = ps[bank][:, n * NG * P:(n + 1) * NG * P].rearrange("p (h d) -> p h d", h=H)
                    dve.wait_ge(S.rinv, s * 2 + j + 1)
                    r_b = R.rinv[:, j, 0:H].rearrange("p (h o) -> p h o", o=1).to_broadcast([P, H, HD])
                    nc.vector.tensor_tensor(R.on[:, j, 0:QC].rearrange("p (h d) -> p h d", h=H),
                                            src[:, :, 0:HD], r_b, ALU.mult).then_inc(S.divided, 1)

            def v_oT(dve, s, bank):
                dve.wait_ge(S.oT_hi, s + 1)
                w, n = min(QC, P), max(1, QC // P) * T
                nc.vector.tensor_tensor(R.oT_lo[0:w, 0:n], ps[bank][0:w, 0:n],
                                        R.oT_hi[0:w, 0:n].bitcast(F32), ALU.subtract).then_inc(S.oT_lo, 1)

            def v_res(dve, s, bank):
                dve.wait_ge(S.o_ps, s + 1)
                xs = x[:, cols(2 * s, 2), :]
                nc.vector.tensor_tensor(xs, ps[bank][:, :].rearrange("p (j e) -> p j e", j=NT), xs,
                                        ALU.add).then_inc(S.residual, 1)

            def v_step0(dve, t, p):
                q = 1 - p

                def maximum(g, i):
                    if live(t + 1):
                        v_max(dve, t + 1, q, 3 * g + i)

                if live(t + 2):
                    v_rope(dve, t + 2, 0, 5)
                maximum(0, 0)
                if live(t + 2):
                    v_rope(dve, t + 2, 1, 7)
                maximum(0, 1)
                if live(t - 2):
                    v_res(dve, t - 2, 6)
                maximum(0, 2)
                maximum(1, 0)
                maximum(1, 1)
                if live(t + 3):
                    v_ln(dve, t + 3)
                maximum(1, 2)
                if live(t + 2):
                    v_qkT(dve, t + 2, 0, 5)
                maximum(2, 0)
                if live(t + 2):
                    v_qkT(dve, t + 2, 1, 7)
                maximum(2, 1)
                if live(t - 1):
                    v_on(dve, t - 1, 6, [0])
                    v_on(dve, t - 1, 7, [1])
                maximum(2, 2)
                maximum(3, 0)
                if live(t + 3):
                    v_xT(dve, t + 3, q, 5)
                maximum(3, 1)
                if live(t - 1):
                    v_oT(dve, t - 1, 6)
                maximum(3, 2)
                if live(t + 1):
                    v_m(dve, t + 1, 7)

            def v_step1(dve, t, p):
                q = 1 - p
                if live(t + 2):
                    v_qkT(dve, t + 2, 0, 7)
                if live(t + 4):
                    v_ln(dve, t + 4)
                if live(t + 3):
                    v_xT(dve, t + 3, q, 5)
                if live(t - 1):
                    v_on(dve, t - 1, 6, [0, 1])
                if live(t + 1):
                    v_max(dve, t + 1, q, 0)
                    v_max(dve, t + 1, q, 1)
                    v_max(dve, t + 1, q, 2)
                if live(t + 3):
                    v_rope(dve, t + 3, 0, 5)
                if live(t - 1):
                    v_oT(dve, t - 1, 6)
                if live(t + 1):
                    v_m(dve, t + 1, 7)
                if live(t - 1):
                    v_res(dve, t - 1, 6)

            def p_ln(pool, s):
                pool.wait_ge(S.ln_mv, s * 2 + 2)
                if live(s - 1):
                    pool.wait_ge(S.xn, (s - 1) * 2 + 2)
                plain(pool)
                nc.gpsimd.tensor_scalar(rs[:, 0, 0:NT], mv[:, 0:NT, 1], EPS, None, ALU.add).then_inc(S.ln_rs, 1)
                pool.wait_ge(S.ln_rs, s * 4 + 1)
                nc.gpsimd.tensor_tensor(rs[:, 1, 0:NT], rs[:, 0, 0:NT], half[:, 0:NT], ALU.pow).then_inc(S.ln_rs, 1)
                pool.wait_ge(S.ln_rs, s * 4 + 2)
                plain(pool)
                for j in range(NT):
                    nc.gpsimd.tensor_scalar(nmr[:, j:j + 1], mv[:, j, 0:1], rs[:, 1, j:j + 1], -1.0,
                                            ALU.mult, ALU.mult).then_inc(S.ln_rs, 1)

            def p_rope(pool, s, b):
                pool.wait_ge(S.rope_terms, s * (3 * A.RB) + 3 * (b + 1))
                nc.gpsimd.tensor_tensor(R.rot[:, b, :, 0:A.RC], R.rot[:, b, :, 0:A.RC],
                                        R.rot2[:, b, :, 0:A.RC], ALU.add).then_inc(S.rotated, 1)

            def p_causal(pool, s, p, g):
                pg = (NG * p + g) % 2
                pool.wait_ge(S.exps, s * U + 3 * (g + 1))
                v = R.prob[:, pg, 0:2, :, :].rearrange("p a h q -> p (a h) q")
                plain(pool)
                nc.gpsimd.affine_select(out=v, in_=v, compare_op=ALU.is_ge, fill=0.0, base=0,
                                        pattern=[[0, 8], [1, P]], channel_multiplier=-1)\
                    .then_inc(S.masked, 1)

            def p_weights(pool, n):
                chunk = WB_CHUNK if L == 0 else WD_CHUNK
                w_in, w_hi, w_lo = (wf.in0, wf.hi0, wf.lo0) if L == 0 else (wf.in1, wf.hi1, wf.lo1)
                pool.wait_ge(w_in, n * 16 + 16)
                hi, lo = (w[:, cols(n * chunk, chunk)] for w in (wff_hi, wff_lo))
                nc.gpsimd.tensor_copy(hi, wstage[:, 0:chunk]).then_inc(w_hi, 1)
                pool.wait_ge(w_hi, n + 1)
                nc.gpsimd.tensor_tensor(lo, wstage[:, 0:chunk], hi.bitcast(F32), ALU.subtract).then_inc(w_lo, 1)

            def p_step0(pool, t, p):
                if live(t + 2):
                    p_rope(pool, t + 2, 0)
                if live(t - 1):
                    p_causal(pool, t - 1, 1 - p, 3)
                if live(t + 2):
                    p_rope(pool, t + 2, 1)
                if live(t):
                    p_causal(pool, t, p, 0)
                if live(t + 3):
                    p_ln(pool, t + 3)
                if live(t):
                    p_causal(pool, t, p, 1)
                if live(t + 2):
                    p_weights(pool, t + 2)
                if live(t):
                    p_causal(pool, t, p, 2)

            def p_step1(pool, t, p):
                if live(t + 4):
                    p_ln(pool, t + 4)
                if live(t):
                    p_causal(pool, t, p, 0)
                if live(t + 3):
                    p_rope(pool, t + 3, 0)
                if live(t + 2):
                    p_weights(pool, t + 2)

            def sp_weights(sp, n):
                chunk = WB_CHUNK if L == 0 else WD_CHUNK
                src, w_in, w_lo = (w_ff0, wf.in0, wf.lo0) if L == 0 else (w_moe, wf.in1, wf.lo1)
                if live(n - 1):
                    sp.wait_ge(w_lo, n)
                sp.dma_start(wstage[:, 0:chunk], src[:, cols(n * chunk, chunk)]).then_inc(w_in, 16)

            def sp_out(sp, s, b, p):
                sp.wait_ge(S.qkT_lo, s * A.RB + b + 1)
                n = A.NCH * T
                for r in range(2):
                    sp.dma_start((scrk if b else scrq)[p][r].rearrange("(c p) t -> p c t", p=P)[:, 0:A.NCH, :],
                                 R.split[:, b, r, 0:n].bitcast(F32).rearrange("p (c t) -> p c t", t=T))\
                        .then_inc((S.k_out if b else S.q_out), 16)

            def sp_half(sp, s, hf, p):
                done = S.half1 if hf else S.half0
                for stack, srcs, lay in ((R.Q, scrq, (0, 1, 0)), (R.K, scrk, (0, 0, 1))):
                    if L == 1:
                        srcs = scrq
                    row0 = hf * HB * HD + (QC if L == 1 and stack is R.K else 0)
                    for i, r in enumerate(lay):
                        src = srcs[p][r, row0:row0 + HB * HD, :].rearrange("(h d) t -> d h t", h=HB)
                        b0 = 64 * hf + HD * i
                        sp.dma_start(stack[b0:b0 + HD, p, 0:HB, :].bitcast(F32), src).then_inc(done, 16)

            def sp_maxima(sp, s, p):
                sp.wait_ge(S.maxT_lo, s + 1)
                sp.dma_start(dram_m[p][0:H], R.msplit[0:H, :, :].bitcast(F32)).then_inc(S.max_out, 16)
                sp.wait_ge(S.max_out, s * 16 + 16)
                for hf in range(A.NH):
                    src = dram_m[p][hf * HB:(hf + 1) * HB].rearrange("h r t -> r h t")
                    sp.dma_start(R.Q[64 * hf + 48:64 * hf + 50, p, 0:HB, :].bitcast(F32), src)\
                        .then_inc(S.max_in, 16)

            def sp_step0(sp, t, p):
                q = 1 - p
                if live(t):
                    sp_maxima(sp, t, p)
                if live(t + 1):
                    if live(t - 1):
                        sp.wait_ge(S.main_ps, (t - 1) * U + U)
                    sp_half(sp, t + 1, 1, q)
                if live(t + 2):
                    sp_weights(sp, t + 2)
                    sp_out(sp, t + 2, 0, p)
                    sp_out(sp, t + 2, 1, p)
                    sp.wait_ge(S.q_out, (t + 2) * 32 + 32)
                    sp.wait_ge(S.k_out, (t + 2) * 32 + 32)
                    if live(t):
                        sp.wait_ge(S.main_ps, t * U + U // 2)
                    sp_half(sp, t + 2, 0, p)

            def sp_step1(sp, t, p):
                if live(t + 2):
                    sp_out(sp, t + 2, 0, p)
                    sp_weights(sp, t + 2)
                    sp.wait_ge(S.q_out, (t + 2) * 32 + 32)
                    if live(t):
                        sp.wait_ge(S.main_ps, t * U + U)
                    sp_half(sp, t + 2, 0, p)

            return dict(pe=pe_step0 if L == 0 else pe_step1, act=act_step0 if L == 0 else act_step1,
                        dve=v_step0 if L == 0 else v_step1, pool=p_step0 if L == 0 else p_step1,
                        sp=sp_step0 if L == 0 else sp_step1, ln=S, ln_tiles=NSEQ * NT, ln_smalls=NSEQ * 4,
                        v_ln=v_ln, p_ln=p_ln, ahead=3 if L == 0 else 4, behind=2 if L == 0 else 1)

        def first_ln(eng, engine, old, new):
            if engine == "dve":
                eng.wait_ge(old["ln"].ln_mv, old["ln_tiles"])
                eng.wait_ge(old["ln"].ln_rs, old["ln_smalls"])
                new["v_ln"](eng, 0)
            if engine == "pool":
                eng.wait_ge(old["ln"].xn, old["ln_tiles"])
                new["p_ln"](eng, 0)

        def run_attention(eng, layer, engine, following, t0=None):
            step, ahead, behind = layer[engine], layer["ahead"], layer["behind"]
            first = behind + behind % 2
            end = (NSEQ - ahead) // 2 * 2
            for t in range(-ahead if t0 is None else t0, first):
                step(eng, t, t % 2)
            with eng.Fori(first // 2, end // 2) as i:
                step(eng, i * 2, 0)
                step(eng, i * 2 + 1, 1)
            for t in range(end, NSEQ + behind - 1):
                step(eng, t, t % 2)
            first_ln(eng, engine, layer, following)
            step(eng, NSEQ + behind - 1, (behind - 1) % 2)

        def feed_forward(L, region):
            R = region
            NM = (INTER0 if L == 0 else INTER1) // P
            W1 = 2 * NM * P
            moe = L == 1
            S = Names()
            S.ln_st = ctx.enter_context(nc.semaphore(f"f{L}_ln_st"))
            S.ln_mv = ctx.enter_context(nc.semaphore(f"f{L}_ln_mv"))
            S.ln_rs = ctx.enter_context(nc.semaphore(f"f{L}_ln_rs"))
            S.xn = ctx.enter_context(nc.semaphore(f"f{L}_xn"))
            S.xT_ps = ctx.enter_context(nc.semaphore(f"f{L}_xT_ps"))
            S.xT_hi = ctx.enter_context(nc.semaphore(f"f{L}_xT_hi"))
            S.xT_lo = ctx.enter_context(nc.semaphore(f"f{L}_xT_lo"))
            S.g_ps = ctx.enter_context(nc.semaphore(f"f{L}_g_ps"))
            S.u_ps = ctx.enter_context(nc.semaphore(f"f{L}_u_ps"))
            S.silu = ctx.enter_context(nc.semaphore(f"f{L}_silu"))
            S.h_f32 = ctx.enter_context(nc.semaphore(f"f{L}_h_f32"))
            S.h_hi = ctx.enter_context(nc.semaphore(f"f{L}_h_hi"))
            S.h_lo = ctx.enter_context(nc.semaphore(f"f{L}_h_lo"))
            S.down = ctx.enter_context(nc.semaphore(f"f{L}_down"))
            S.o_ps = ctx.enter_context(nc.semaphore(f"f{L}_o_ps"))
            S.residual = ctx.enter_context(nc.semaphore(f"f{L}_residual"))
            S.stored = ctx.enter_context(nc.semaphore(f"f{L}_stored"))
            S.scores_ps = ctx.enter_context(nc.semaphore(f"f{L}_scores_ps"))
            S.gate = ctx.enter_context(nc.semaphore(f"f{L}_gate"))
            S.tanh = ctx.enter_context(nc.semaphore(f"f{L}_tanh"))
            S.w_sb = ctx.enter_context(nc.semaphore(f"f{L}_w_sb"))
            S.wT_ps = ctx.enter_context(nc.semaphore(f"f{L}_wT_ps"))
            S.wT_hi = ctx.enter_context(nc.semaphore(f"f{L}_wT_hi"))
            S.wT_lo = ctx.enter_context(nc.semaphore(f"f{L}_wT_lo"))
            S.w_bcast = ctx.enter_context(nc.semaphore(f"f{L}_w_bcast"))
            HH = 2 if moe else 1

            def last_user(n, m, depth):
                if m >= depth:
                    return n * NM + m - depth + 1
                return n * NM + 1 - NM + max(k for k in range(NM) if k % depth == m % depth)

            def used_before(n, m, depth):
                return not isinstance(n, int) or last_user(n, m, depth) > 0

            def w_up(w, c, col):
                return w[:, c * W1 + col:c * W1 + col + P]

            def w_down(w, m):
                return w[:, NC * W1 + m * E:NC * W1 + (m + 1) * E]

            def blk_live(n):
                return not isinstance(n, int) or 0 <= n < NB

            def pe_xT(pe, n, c):
                if c == 0:
                    if blk_live(n - 1) and moe:
                        pe.wait_ge(S.wT_lo, n)
                    if blk_live(n - 1) and not moe:
                        pe.wait_ge(S.xT_lo, n * NC)
                else:
                    pe.wait_ge(S.xT_lo, n * NC + c)
                for j in range(BT):
                    if c == 0:
                        pe.wait_ge(S.xn, n * BT + j + 1)
                        plain(pe)
                    mm = pe.transpose(ps[6][:, j * P:(j + 1) * P], R.xnF[:, j, c * P:(c + 1) * P], ident[:, :])
                mm.then_inc(S.xT_ps, 1)

            def pe_scores(pe, n, p):
                pe.wait_ge(S.xT_lo, n * NC + NC)
                for j in range(BT):
                    o = ps[6][:, j * NEXP:(j + 1) * NEXP]
                    for c in range(NC):
                        hi, lo = (t[:, p, c, j * P:(j + 1) * P] for t in (R.xF_hi, R.xF_lo))
                        gh, gl = (w[:, c * NEXP:(c + 1) * NEXP] for w in (wg_hi, wg_lo))
                        pe.matmul(o, hi, gh, start=(c == 0), stop=False)
                        pe.matmul(o, hi, gl, start=False, stop=False)
                        mm = pe.matmul(o, lo, gh, start=False, stop=(c == NC - 1))
                mm.then_inc(S.scores_ps, 1)

            def pe_wT(pe, n):
                pe.wait_ge(S.w_sb, n + 1)
                for j in range(BT):
                    mm = pe.transpose(ps[6][0:NEXP, j * P:(j + 1) * P], R.wexp[:, j, :], ident[:, :])
                mm.then_inc(S.wT_ps, 1)

            def act_xn(act, n):
                act.wait_ge(S.ln_rs, n * (BT + 2) + BT + 2)
                if blk_live(n - 1):
                    act.wait_ge(S.xT_ps, (n - 1) * NC + NC)
                for j in range(BT):
                    nc.scalar.activation(R.xnF[:, j:j + 1, :], x[:, cols(BT * n + j, 1), :], ACT.Identity,
                                         bias=nmr[:, j:j + 1], scale=rs[:, 1, j:j + 1]).then_inc(S.xn, 1)

            def act_xT(act, n, p, c):
                act.wait_ge(S.xT_ps, n * NC + c + 1)
                if c == 0 and blk_live(n - 2):
                    act.wait_ge(S.u_ps, (n - 2) * NM + NM)
                nc.scalar.copy(R.xF_hi[:, p, c, :], ps[6][:, :]).then_inc(S.xT_hi, 1)

            def act_wT(act, n, p):
                act.wait_ge(S.wT_ps, n + 1)
                if blk_live(n - 2):
                    act.wait_ge(S.w_bcast, (n - 2) * NM + NM)
                nc.scalar.copy(R.wT[0:NEXP, p, :], ps[6][0:NEXP, :]).then_inc(S.wT_hi, 1)

            def v_ln(dve, n):
                for j in range(BT):
                    nc.vector.bn_stats(st[:, j, :], x[:, cols(BT * n + j, 1), :].rearrange("p a e -> p (a e)"))\
                        .then_inc(S.ln_st, 1)
                dve.wait_ge(S.ln_st, n * BT + BT)
                if blk_live(n - 1):
                    dve.wait_ge(S.ln_rs, (n - 1) * (BT + 2) + BT + 2)
                plain(dve)
                for j in range(BT):
                    nc.vector.bn_aggr(mv[:, j, :], st[:, j, :]).then_inc(S.ln_mv, 1)

            def v_xT(dve, n, p, c):
                dve.wait_ge(S.xT_hi, n * NC + c + 1)
                nc.vector.tensor_tensor(R.xF_lo[:, p, c, :], ps[6][:, :], R.xF_hi[:, p, c, :].bitcast(F32),
                                        ALU.subtract).then_inc(S.xT_lo, 1)

            NGATE = 9

            def v_rank(dve, n):
                dve.wait_ge(S.scores_ps, n + 1)
                sc = R.sc[:, :, :]
                nc.vector.tensor_copy(sc, ps[6][:, 0:BT * NEXP].rearrange("p (j e) -> p j e", j=BT))\
                    .then_inc(S.gate, 1)
                dve.wait_ge(S.gate, n * NGATE + 1)
                for j in range(BT):
                    mine = R.sc[:, j, :].rearrange("p (e o) -> p e o", o=1).to_broadcast([P, NEXP, NEXP])
                    other = R.sc[:, j:j + 1, :].to_broadcast([P, NEXP, NEXP])
                    nc.vector.tensor_tensor(R.gt[:, j], other, mine, ALU.is_gt)
                    last = nc.vector.tensor_tensor(R.eq[:, j], other, mine, ALU.is_equal)
                last.then_inc(S.gate, 1)
                dve.wait_ge(S.gate, n * NGATE + 2)
                tri_b = tri[:, :, :].rearrange("p e f -> p (e f)").rearrange("p (o n) -> p o n", o=1)\
                    .to_broadcast([P, BT, NEXP * NEXP])
                gt = R.gt[:, :, :, :].rearrange("p j e f -> p j (e f)")
                eq = R.eq[:, :, :, :].rearrange("p j e f -> p j (e f)")
                nc.vector.tensor_tensor(eq, eq, tri_b, ALU.mult).then_inc(S.gate, 1)
                dve.wait_ge(S.gate, n * NGATE + 3)
                nc.vector.tensor_tensor(gt, gt, eq, ALU.add).then_inc(S.gate, 1)

            def v_select(dve, n):
                dve.wait_ge(S.gate, n * NGATE + 4)
                nc.vector.tensor_reduce(R.rank[:, :, :], R.gt[:, :, :, :], axis=AX.X, op=ALU.add)\
                    .then_inc(S.gate, 1)
                dve.wait_ge(S.gate, n * NGATE + 5)
                nc.vector.tensor_scalar(R.halfsel[:, :, :], R.rank[:, :, :], 2.0, 0.5, ALU.is_lt, ALU.mult)\
                    .then_inc(S.gate, 1)
                dve.wait_ge(S.gate, n * NGATE + 6)
                if blk_live(n - 1):
                    dve.wait_ge(S.tanh, n)
                nc.vector.tensor_tensor(R.tz[:, :, :], R.halfsel[:, :, :], R.sc[:, :, :], ALU.mult)\
                    .then_inc(S.gate, 1)
                dve.wait_ge(S.gate, n * NGATE + 7)
                nc.vector.tensor_reduce(R.mid[:, :], R.tz[:, :, :], axis=AX.X, op=ALU.add).then_inc(S.gate, 1)
                dve.wait_ge(S.gate, n * NGATE + 8)
                mid_b = R.mid[:, :].rearrange("p (j o) -> p j o", o=1).to_broadcast([P, BT, NEXP])
                nc.vector.tensor_tensor(R.tz[:, :, :], R.sc[:, :, :], mid_b, ALU.subtract).then_inc(S.gate, 1)

            def v_weights(dve, n):
                dve.wait_ge(S.tanh, n + 1)
                if blk_live(n - 1):
                    dve.wait_ge(S.wT_ps, n)
                nc.vector.scalar_tensor_tensor(out=R.wexp[:, :, :], in0=R.th[:, :, :], scalar=1.0,
                                               in1=R.halfsel[:, :, :], op0=ALU.add, op1=ALU.mult)\
                    .then_inc(S.w_sb, 1)

            def act_tanh(act, n):
                act.wait_ge(S.gate, n * NGATE + NGATE)
                if blk_live(n - 1):
                    act.wait_ge(S.w_sb, n)
                nc.scalar.activation(R.th[:, :, :], R.tz[:, :, :], ACT.Tanh).then_inc(S.tanh, 1)

            def v_wT(dve, n, p):
                dve.wait_ge(S.wT_hi, n + 1)
                nc.vector.tensor_tensor(R.wT[32:32 + NEXP, p, :], ps[6][0:NEXP, :],
                                        R.wT[0:NEXP, p, :].bitcast(F32), ALU.subtract).then_inc(S.wT_lo, 1)

            def p_ln(pool, n):
                k = BT + 2
                pool.wait_ge(S.ln_mv, n * BT + BT)
                if blk_live(n - 1):
                    pool.wait_ge(S.xn, (n - 1) * BT + BT)
                plain(pool)
                nc.gpsimd.tensor_scalar(rs[:, 0, :], mv[:, :, 1], EPS, None, ALU.add).then_inc(S.ln_rs, 1)
                pool.wait_ge(S.ln_rs, n * k + 1)
                nc.gpsimd.tensor_tensor(rs[:, 1, :], rs[:, 0, :], half[:, :], ALU.pow).then_inc(S.ln_rs, 1)
                pool.wait_ge(S.ln_rs, n * k + 2)
                plain(pool)
                for j in range(BT):
                    nc.gpsimd.tensor_scalar(nmr[:, j:j + 1], mv[:, j, 0:1], rs[:, 1, j:j + 1], -1.0,
                                            ALU.mult, ALU.mult).then_inc(S.ln_rs, 1)

            def turn(p, m):
                return (p * NM + m) % 2

            def banks(p, m):
                b = 2 * turn(p, m)
                return ps[b], ps[b + 1]

            def pe_up(pe, n, p, m):
                if m == 0:
                    pe.wait_ge(S.xT_lo, n * NC + NC)
                if not (isinstance(n, int) and n * NM + m < 2):
                    pe.wait_ge(S.h_f32, (n * NM + m - 1) * HH)
                g_bank, u_bank = banks(p, m)
                for o, off, signal in ((g_bank, 0, S.g_ps), (u_bank, NM * P, S.u_ps)):
                    for c in range(NC):
                        wh, wl = (w_up(w, c, off + m * P) for w in (wff_hi, wff_lo))
                        xh, xl = R.xF_hi[:, p, c, :], R.xF_lo[:, p, c, :]
                        pe.matmul(o[:, :], wh, xh, start=(c == 0), stop=False)
                        pe.matmul(o[:, :], wh, xl, start=False, stop=False)
                        mm = pe.matmul(o[:, :], wl, xh, start=False, stop=(c == NC - 1))
                    mm.then_inc(signal, 1)

            def pe_w(pe, n, p, m):
                if m == 0:
                    pe.wait_ge(S.wT_lo, n + 1)
                if not (isinstance(n, int) and n * NM + m < 1):
                    pe.wait_ge(S.h_f32, (n * NM + m) * HH)
                pe.matmul(ps[7][:, :], R.sel[:, m, :], R.wT[:, p, :], start=True, stop=True)\
                    .then_inc(S.w_bcast, 1)

            def act_silu(act, n, p, m):
                act.wait_ge(S.g_ps, n * NM + m + 1)
                if not (isinstance(n, int) and n * NM + m < 2):
                    act.wait_ge(S.h_f32, (n * NM + m - 1) * HH)
                nc.scalar.activation(R.sg[:, turn(p, m), :], banks(p, m)[0][:, :], ACT.Silu).then_inc(S.silu, 1)

            def act_hi(act, n, p, m):
                act.wait_ge(S.h_f32, n * (NM * HH) + HH * (m + 1))
                if used_before(n, m, 4):
                    act.wait_ge(S.down, last_user(n, m, 4))
                nc.scalar.copy(R.h_hi[:, m % 4, :], R.hf[:, turn(p, m), :]).then_inc(S.h_hi, 1)

            def v_h(dve, n, p, m):
                dve.wait_ge(S.u_ps, n * NM + m + 1)
                dve.wait_ge(S.silu, n * NM + m + 1)
                if not (isinstance(n, int) and n * NM + m < 2):
                    dve.wait_ge(S.h_lo, (n * NM + m - 1))
                h = R.hf[:, turn(p, m), :]
                nc.vector.tensor_tensor(h, banks(p, m)[1][:, :], R.sg[:, turn(p, m), :], ALU.mult).then_inc(S.h_f32, 1)
                if moe:
                    dve.wait_ge(S.w_bcast, n * NM + m + 1)
                    dve.wait_ge(S.h_f32, n * (NM * HH) + HH * m + 1)
                    nc.vector.tensor_tensor(h, ps[7][:, :], h, ALU.mult).then_inc(S.h_f32, 1)

            def v_lo(dve, n, p, m):
                dve.wait_ge(S.h_hi, n * NM + m + 1)
                nc.vector.tensor_tensor(R.h_lo[:, m % 4, :], R.hf[:, turn(p, m), :], R.h_hi[:, m % 4, :].bitcast(F32),
                                        ALU.subtract).then_inc(S.h_lo, 1)

            LAG = 2

            def pe_step(pe, n, p):
                for m in range(NM):
                    if blk_live(n):
                        pe_up(pe, n, p, m)
                        if moe and m == 0 and isinstance(n, int) and n == 0:
                            pe_wT(pe, 0)
                            pe.wait_ge(setup.wg, 17)
                        if moe:
                            pe_w(pe, n, p, m)
                    if m < LAG:
                        if blk_live(n - 1):
                            pe_down(pe, n - 1, NM - LAG + m)
                    elif blk_live(n):
                        pe_down(pe, n, m - LAG)
                    if blk_live(n + 1) and m in (PREP, PREP + 1):
                        pe_xT(pe, n + 1, m - PREP)
                    if moe and blk_live(n + 1):
                        if m == PREP + 2:
                            pe_scores(pe, n + 1, 1 - p)
                        if m == PREP + 5:
                            pe_wT(pe, n + 1)
                    if not blk_live(n) and m == LAG - 1:
                        break

            def pe_down(pe, n, m):
                pe.wait_ge(S.h_lo, n * NM + m + 1)
                if m == 0:
                    if blk_live(n - 1):
                        pe.wait_ge(S.residual, (n - 1) * 2 + 2)
                b = m % 4
                order = [0, 2, 1, 3]
                for j in order:
                    o = ps[4 + j // 2][:, (j % 2) * E:(j % 2 + 1) * E]
                    hi, lo = (t[:, b, j * P:(j + 1) * P] for t in (R.h_hi, R.h_lo))
                    pe.matmul(o, hi, w_down(wff_hi, m), start=(m == 0 and j % 2 == 0), stop=False,
                              skip_group_check=True)
                    pe.matmul(o, hi, w_down(wff_lo, m), start=False, stop=False, skip_group_check=True)
                    mm = pe.matmul(o, lo, w_down(wff_hi, m), start=False, stop=(m == NM - 1 and j % 2 == 1),
                                   skip_group_check=True)
                mm.then_inc(S.down, 1)

            PREP = 3

            def act_step(act, n, p):
                if not blk_live(n):
                    return
                for m in range(NM):
                    act_silu(act, n, p, m)
                    act_hi(act, n, p, m)
                    if blk_live(n + 1):
                        if m == PREP - 2:
                            act_xn(act, n + 1)
                        if m in (PREP, PREP + 1):
                            act_xT(act, n + 1, 1 - p, m - PREP)
                        if moe and m == PREP + 4:
                            act_tanh(act, n + 1)
                        if moe and m == PREP + 5:
                            act_wT(act, n + 1, 1 - p)

            def v_step(dve, n, p):
                for m in range(NM):
                    if blk_live(n):
                        v_h(dve, n, p, m)
                        v_lo(dve, n, p, m)
                    if blk_live(n + 1) and blk_live(n):
                        if m == PREP - 3:
                            v_ln(dve, n + 1)
                        if m in (PREP, PREP + 1):
                            v_xT(dve, n + 1, 1 - p, m - PREP)
                        if moe and m == PREP + 2:
                            v_rank(dve, n + 1)
                        if moe and m == PREP + 3:
                            v_select(dve, n + 1)
                        if moe and m == PREP + 4:
                            v_weights(dve, n + 1)
                        if moe and m == PREP + 5:
                            v_wT(dve, n + 1, 1 - p)
                    if m == LAG - 1 and blk_live(n - 1):
                        v_res(dve, n - 1)
                    if not blk_live(n) and m == LAG - 1:
                        break

            def v_res(dve, n):
                dve.wait_ge(S.down, n * NM + NM)
                for r in range(2):
                    xs = x[:, cols(BT * n + 2 * r, 2), :]
                    nc.vector.tensor_tensor(xs, ps[4 + r][:, :].rearrange("p (j e) -> p j e", j=2), xs,
                                            ALU.add).then_inc(S.residual, 1)

            def p_step(pool, n, p):
                if blk_live(n + 1) and blk_live(n):
                    p_ln(pool, n + 1)

            def sp_step(sp, n, p):
                if moe and blk_live(n - 1):
                    dst = out.rearrange("b (j p) e -> p (b j) e", p=P)
                    for r in range(2):
                        sp.wait_ge(S.residual, (n - 1) * 2 + r + 1)
                        tiles = cols(BT * (n - 1) + 2 * r, 2)
                        sp.dma_start(dst[:, tiles, :], x[:, tiles, :]).then_inc(S.stored, 16)

            def prep_first(engine, eng):
                if engine == "dve":
                    v_xT(eng, 0, 0, 0)
                    v_xT(eng, 0, 0, 1)
                    if moe:
                        eng.wait_ge(setup.wg, 16)
                        nc.vector.tensor_copy(R.sel[:, :, :], R.selraw[:, :, :])
                        nc.vector.memset(R.wT[:, :, :].bitcast(F32), 0.0)
                        eng.drain().then_inc(setup.wg, 1)
                        v_rank(eng, 0)
                        v_select(eng, 0)
                        v_weights(eng, 0)
                        v_wT(eng, 0, 0)
                elif engine == "act":
                    act_xn(eng, 0)
                    act_xT(eng, 0, 0, 0)
                    act_xT(eng, 0, 0, 1)
                    if moe:
                        eng.wait_ge(setup.wg, 17)
                        act_tanh(eng, 0)
                        act_wT(eng, 0, 0)
                elif engine == "pe":
                    pe_xT(eng, 0, 0)
                    pe_xT(eng, 0, 1)
                    if moe:
                        pe_scores(eng, 0, 0)

            return dict(pe=pe_step, act=act_step, dve=v_step, pool=p_step, sp=sp_step, first=prep_first,
                        ln=S, ln_tiles=NB * BT, ln_smalls=NB * (BT + 2), v_ln=v_ln, p_ln=p_ln,
                        stored=S.stored)

        def run_feed_forward(eng, F, engine, following=None, between=None):
            step = F[engine]
            F["first"](engine, eng)
            step(eng, 0, 0)
            if between:
                between(eng, 0)
            step(eng, 1, 1)
            if between:
                between(eng, 1)
            with eng.Fori(1, NB // 2 - 1) as i:
                step(eng, i * 2, 0)
                step(eng, i * 2 + 1, 1)
            if between:
                between(eng, 2)
            step(eng, NB - 2, 0)
            step(eng, NB - 1, 1)
            if following:
                first_ln(eng, engine, F, following)
            step(eng, NB, 0)

        attn_buffers = ExitStack()

        def ra(name, shape, dt=F32):
            return attn_buffers.enter_context(nc.sbuf_tensor("a_" + name, shape, dt))

        RA = Names()
        RA.xT_hi = ra("xT_hi", [P, 2, NC * T], F32R)
        RA.xT_lo = ra("xT_lo", [P, 2, NC * T], F32R)
        RA.rot = ra("rot", [P, 2, NT, E])
        RA.rot2 = ra("rot2", [P, 2, NT, E])
        RA.split = ra("split", [P, 2, 2, NC * T], F32R)
        RA.Q = ra("Q", [P, 2, 8, T], F32R)
        RA.K = ra("K", [P, 2, 8, T], F32R)
        RA.prob = ra("prob", [P, 2, 3, 4, P])
        RA.v = ra("v", [P, 2, NT, 16, 2 * HD])
        RA.o = ra("o", [P, 4, T])
        RA.oT_hi = ra("oT_hi", [P, NC * T], F32R)
        RA.oT_lo = ra("oT_lo", [P, NC * T], F32R)
        RA.negm = ra("negm", [P, 2, NT, 16])
        RA.msplit = ra("msplit", [64, 2, T], F32R)
        RA.rinv = ra("rinv", [P, NT, 16])
        attn_buffers.close()
        RA.xn, RA.on = (RA.rot2[:, 0], RA.rot[:, 1]), RA.rot2[:, 1]
        RA.mT = RA.msplit[:, 0, :]
        RA.pick = [(RA.oT_hi, RA.oT_lo)[h // 2][0:64, T + h % 2 * P:T + (h % 2 + 1) * P] for h in range(4)]
        RA.hold = RA.o[:, 2:4, 0:NT * 4 * HD]

        def rf(name, shape, dt=F32):
            return ctx.enter_context(nc.sbuf_tensor("f_" + name, shape, dt))

        RF = Names()
        RF.xnF = rf("xnF", [P, BT, E])
        RF.xF_hi = rf("xF_hi", [P, 2, NC, BN], F32R)
        RF.xF_lo = rf("xF_lo", [P, 2, NC, BN], F32R)
        RF.sg = rf("sg", [P, 2, BN])
        RF.hf = rf("hf", [P, 2, BN])
        RF.h_hi = rf("h_hi", [P, 4, BN], F32R)
        RF.h_lo = rf("h_lo", [P, 4, BN], F32R)
        RF.sel = rf("sel", [64, INTER1 // P, P], F32R)
        RF.wT = rf("wT", [64, 2, BN], F32R)
        RF.selraw = rf("selraw", [64, INTER1 // P, P])
        RF.sc = rf("sc", [P, BT, NEXP])
        RF.gt = rf("gt", [P, BT, NEXP, NEXP])
        RF.eq = rf("eq", [P, BT, NEXP, NEXP])
        RF.rank = rf("rank", [P, BT, NEXP])
        RF.halfsel = rf("halfsel", [P, BT, NEXP])
        RF.tz = rf("tz", [P, BT, NEXP])
        RF.th = rf("th", [P, BT, NEXP])
        RF.mid = rf("mid", [P, BT])
        RF.wexp = rf("wexp", [P, BT, NEXP])

        A0 = attention(0, RA)
        F0 = feed_forward(0, RF)
        A1 = attention(1, RA)
        F1 = feed_forward(1, RF)

        raw0 = RA.v[:, :, :, :, :].rearrange("p a j h d -> p (a j h d)")
        NW0 = NC * (W0 + E)
        NQ1 = NC * E
        rawm = RA.prob[:, 1, 1:3, :, :].rearrange("p a h q -> p (a h q)")
        rawo = RA.v[:, 0, :, :, :].rearrange("p j h d -> p (j h d)")
        sum1 = RA.o[:, 0:2, :].rearrange("p j e -> p (j e)")
        sumb = RA.o[:, 2:4, :].rearrange("p j e -> p (j e)")
        rawg = rawm[:, 2 * E + 2 * P:2 * E + 2 * P + NC * NEXP]
        pickraw = RA.prob[0:64, 1, 0, :, :]

        def prepare_layer1(dve, part):
            if part == 0:
                dve.wait_ge(setup.raw1, 16 * 11)
                nc.vector.memset(sum1[:, :], 0.0)
                nc.vector.memset(sumb[0:64, :], 0.0)
                dve.drain().then_inc(setup.sum1, 1)
                dve.wait_ge(setup.sum1, 3)
                for c in range(NC):
                    nc.vector.tensor_reduce(
                        sum1[:, c * E:c * E + 64].rearrange("p (k d) -> p k d", k=4),
                        rawm[:, c * E:(c + 1) * E].rearrange("p (k g d) -> p k d g", k=4, g=4), axis=AX.X, op=ALU.add)
                    nc.vector.tensor_copy(sum1[:, c * E + 64:c * E + 192], rawm[:, 2 * E + c * P:2 * E + (c + 1) * P])
                nc.vector.tensor_reduce(sumb[0:64, 0:64].rearrange("p (k d) -> p k d", k=4),
                                        rawo[0:64, E:2 * E].rearrange("p (k g d) -> p k d g", k=4, g=4),
                                        axis=AX.X, op=ALU.add)
                nc.vector.tensor_copy(sumb[0:64, 64:192], rawo[0:64, 2 * E:2 * E + P])
                nc.vector.tensor_copy(sumb[0:64, E:2 * E], rawo[0:64, 3 * E:4 * E])
                dve.drain().then_inc(setup.sum1, 1)
            elif part == 1:
                dve.wait_ge(setup.sum1, 4)
                nc.vector.tensor_copy(wat_hi[:, 0:NQ1], sum1[:, :])
                nc.vector.tensor_copy(wat_hi[0:64, NQ1:NQ1 + E], rawo[0:64, 0:E])
                for h in range(4):
                    nc.vector.tensor_copy(RA.pick[h], pickraw[:, h, :])
                nc.vector.tensor_copy(wg_hi[:, :], rawg[:, 0:NC * NEXP])
                nc.vector.tensor_copy(bias[:, :], sumb[0:64, :])
                dve.drain().then_inc(setup.lo1, 1)
            elif part == 2:
                dve.wait_ge(setup.lo1, 1)
                nc.vector.tensor_tensor(wat_lo[:, 0:NQ1], sum1[:, :], wat_hi[:, 0:NQ1].bitcast(F32), ALU.subtract)
                nc.vector.tensor_tensor(wat_lo[0:64, NQ1:NQ1 + E], rawo[0:64, 0:E],
                                        wat_hi[0:64, NQ1:NQ1 + E].bitcast(F32), ALU.subtract)
                nc.vector.tensor_tensor(wg_lo[:, :], rawg[:, 0:NC * NEXP], wg_hi[:, :].bitcast(F32), ALU.subtract)
                nc.vector.tensor_tensor(bias[32:64, :], sumb[32:64, :], bias[32:64, :].bitcast(F32), ALU.subtract)
                dve.drain().then_inc(setup.lo1, 3)

        def ones_beside_v(pool, part):
            if part < 2:
                return
            pool.wait_ge(setup.lo1, 4)
            nc.gpsimd.memset(RA.v[:, :, :, :, HD:2 * HD], 1.0)
            pool.drain().then_inc(setup.hi1, 1)

        block = ctx.enter_context(nc.Block())

        @block.sync
        def _(sp):
            x_v = x_in.rearrange("b (j p) e -> p (b j) e", p=P)
            sp.dma_start(x[:, 0:2 * NT, :], x_v[:, 0:2 * NT, :]).then_inc(setup.x_first, 16)
            for dst, src in ((cos, c_cos), (sin, c_sin)):
                sp.dma_start(dst[:, :, :], src).then_inc(setup.const, 16)
            sp.dma_start(ident[:, :], c_ident).then_inc(setup.const, 16)
            sp.dma_start(tri[:, :, :], c_tri).then_inc(setup.const, 16)
            sp.dma_start(wstage[:, 0:P], c_mask).then_inc(setup.const, 16)
            sp.dma_start(raw0[:, 0:NC * W0].rearrange("p (c n) -> p c n", c=NC),
                         wqkv0.rearrange("(c p) n -> p c n", p=P)).then_inc(setup.w_raw, 16)
            sp.dma_start(raw0[:, NC * W0:NW0].rearrange("p (c n) -> p c n", c=NC),
                         wo0.rearrange("(c p) n -> p c n", p=P)).then_inc(setup.wo_raw, 16)
            sp.dma_start(x[:, 2 * NT:, :], x_v[:, 2 * NT:, :]).then_inc(setup.x_rest, 16)
            sp.wait_ge(setup.const_cp, 3)
            sp.wait_ge(setup.k_ones, 3)
            run_attention(sp, A0, "sp", F0)
            end_of_phase(sp, 1)
            sp.dma_start(rawm[:, 0:2 * E].rearrange("p (c n) -> p c n", c=NC),
                         wq1.rearrange("(c p) n -> p c n", p=P)).then_inc(setup.raw1, 16)
            sp.dma_start(rawm[:, 2 * E:2 * E + 2 * P].rearrange("p (c n) -> p c n", c=NC),
                         wkv1.rearrange("(c p) n -> p c n", p=P)).then_inc(setup.raw1, 16)
            sp.dma_start(rawo[0:64, 0:E], wo1).then_inc(setup.raw1, 16)
            sp.dma_start(rawg[:, 0:NC * NEXP].rearrange("p (c n) -> p c n", c=NC),
                         w_gate.rearrange("(c p) n -> p c n", p=P)).then_inc(setup.raw1, 16)
            sp.dma_start(pickraw, c_pick).then_inc(setup.raw1, 16)
            sp.wait_ge(setup.sum1, 2)
            for row in (0, 32):
                sp.dma_start(rawo[row:row + 1, E:2 * E], bq1).then_inc(setup.raw1, 16)
                sp.dma_start(rawo[row:row + 1, 2 * E:2 * E + P], bkv1).then_inc(setup.raw1, 16)
                sp.dma_start(rawo[row:row + 1, 3 * E:4 * E], bo1).then_inc(setup.raw1, 16)
            run_feed_forward(sp, F0, "sp", A1)
            end_of_phase(sp, 2)
            run_attention(sp, A1, "sp", F1)
            end_of_phase(sp, 3)
            sp.dma_start(RF.selraw[:, :, :], c_sel).then_inc(setup.wg, 16)
            run_feed_forward(sp, F1, "sp")
            sp.wait_ge(F1["stored"], 16 * NB * 2)
            end_of_phase(sp, 4)

        @block.gpsimd
        def _(pool):
            nc.gpsimd.memset(half[:, :], -0.5).then_inc(setup.k_ones, 1)
            for n, b in enumerate((32, 96)):
                pool.wait_ge(setup.k_ones, n + 1)
                nc.gpsimd.memset(RA.K[b:b + 32, :, :, :].bitcast(F32), 1.0).then_inc(setup.k_ones, 1)
            pool.wait_ge(setup.k_ones, 3)
            A0["pool"](pool, -3, 1)
            pool.wait_ge(setup.w_lo, 2)
            nc.gpsimd.memset(RA.v[:, :, :, :, HD:2 * HD], 1.0)
            pool.drain().then_inc(setup.hi1, 1)
            pool.wait_ge(setup.const_cp, 3)
            run_attention(pool, A0, "pool", F0, t0=-2)
            end_of_phase(pool, 1)
            run_feed_forward(pool, F0, "pool", A1, ones_beside_v)
            end_of_phase(pool, 2)
            run_attention(pool, A1, "pool", F1, t0=1 - A1["ahead"])
            end_of_phase(pool, 3)
            run_feed_forward(pool, F1, "pool")
            end_of_phase(pool, 4)

        @block.scalar
        def _(act):
            A0["act"](act, -3, 1)
            for n, part in enumerate((slice(0, NC * W0), slice(NC * W0, NW0))):
                act.wait_ge((setup.w_raw, setup.wo_raw)[n], 16)
                nc.scalar.copy(wat_hi[:, part], raw0[:, part]).then_inc(setup.w_hi, 1)
            act.wait_ge(setup.hi1, 1)
            run_attention(act, A0, "act", F0, t0=-2)
            end_of_phase(act, 1)
            run_feed_forward(act, F0, "act", A1)
            end_of_phase(act, 2)
            act.wait_ge(setup.hi1, 2)
            run_attention(act, A1, "act", F1)
            end_of_phase(act, 3)
            run_feed_forward(act, F1, "act")
            end_of_phase(act, 4)

        @block.vector
        def _(dve):
            dve.wait_ge(setup.const, 80)
            nc.vector.tensor_copy(identb[:, :], ident[:, :]).then_inc(setup.const_cp, 1)
            nc.vector.tensor_copy(maskb[:, :, :], wstage[:, 0:P].rearrange("p (o n) -> p o n", o=1)
                                  .to_broadcast([P, 4, P])).then_inc(setup.const_cp, 1)
            nc.vector.memset(ones[:, :].bitcast(F32), 1.0).then_inc(setup.const_cp, 1)
            A0["dve"](dve, -3, 1)
            for n, part in enumerate((slice(0, NC * W0), slice(NC * W0, NW0))):
                dve.wait_ge(setup.w_hi, n + 1)
                nc.vector.tensor_tensor(wat_lo[:, part], raw0[:, part], wat_hi[:, part].bitcast(F32),
                                        ALU.subtract).then_inc(setup.w_lo, 1)
            run_attention(dve, A0, "dve", F0, t0=-2)
            end_of_phase(dve, 1)
            nc.vector.memset(rawo[0:64, E:4 * E], 0.0).then_inc(setup.sum1, 1)
            nc.vector.memset(RA.mT.bitcast(F32), 0.0)
            dve.drain().then_inc(setup.sum1, 1)
            run_feed_forward(dve, F0, "dve", A1, prepare_layer1)
            end_of_phase(dve, 2)
            run_attention(dve, A1, "dve", F1, t0=1 - A1["ahead"])
            end_of_phase(dve, 3)
            run_feed_forward(dve, F1, "dve")
            end_of_phase(dve, 4)

        @block.tensor
        def _(pe):
            pe.wait_ge(setup.const_cp, 3)
            A0["pe"](pe, -3, 1)
            pe.wait_ge(setup.w_lo, 1)
            A0["pe"](pe, -2, 0)
            pe.wait_ge(setup.w_lo, 2)
            run_attention(pe, A0, "pe", F0, t0=-1)
            end_of_phase(pe, 1)
            run_feed_forward(pe, F0, "pe", A1)
            end_of_phase(pe, 2)
            pe.wait_ge(setup.lo1, 4)
            run_attention(pe, A1, "pe", F1)
            end_of_phase(pe, 3)
            run_feed_forward(pe, F1, "pe")
            end_of_phase(pe, 4)


def constants():
    f = np.float32
    inv = (f(1.0) / np.power(f(10000.0), np.arange(0, HD, 2, dtype=f) / f(HD))).astype(f)
    ang = (np.arange(T, dtype=f)[:, None] * inv[None, :]).astype(f)
    c, s = np.cos(ang).astype(f), np.sin(ang).astype(f)
    cos = np.concatenate([c, c], 1).reshape(NT, P, HD).transpose(1, 0, 2)
    sin = np.concatenate([-s, s], 1).reshape(NT, P, HD).transpose(1, 0, 2)
    ident = np.eye(P, dtype=f)
    mask = np.where(np.arange(P)[None, :] > np.arange(P)[:, None], f(MASK), f(0.0)).astype(f)
    tri = np.broadcast_to(np.tril(np.ones((NEXP, NEXP), f), -1), (P, NEXP, NEXP))
    sel = np.zeros((64, INTER1), f)
    for e in range(NEXP):
        sel[e, e * HID:(e + 1) * HID] = 1.0
        sel[32 + e, e * HID:(e + 1) * HID] = 1.0
    sel = sel.reshape(64, INTER1 // P, P)
    pick = np.zeros((64, 4, P), f)
    for h in range(4):
        pick[h, h] = pick[32 + h, h] = 1.0
    return {k: np.ascontiguousarray(v) for k, v in
            dict(c_cos=cos, c_sin=sin, c_ident=ident, c_mask=mask, c_tri=tri, c_sel=sel, c_pick=pick).items()}


def kernel(**inputs):
    import concourse.bacc as bacc
    from concourse.bass_utils import run_bass_kernel_spmd as run

    i = {k: np.asarray(v) for k, v in inputs.items()}
    perm = np.concatenate([np.arange(0, HD, 2), np.arange(1, HD, 2)])

    def heads(w):
        return w.reshape(w.shape[0], -1, HD)[:, :, perm].reshape(w.shape[0], -1)

    def by_partition(w):
        k, n = w.shape
        return w.reshape(k // P, P, n).transpose(1, 0, 2).reshape(P, -1)

    w1 = i["L1_ffn_W1"].reshape(INTER1, E).T
    w2 = i["L1_ffn_W2"].reshape(INTER1, E).T
    w3 = i["L1_ffn_W3"].transpose(0, 2, 1).reshape(INTER1, E)
    arrays = dict(
        x_in=i["L0_attn_x"],
        wqkv0=np.concatenate([i["L0_attn_wq"], i["L0_attn_wk"], i["L0_attn_wv"]], 1),
        wo0=i["L0_attn_wo"],
        w_ff0=np.concatenate([by_partition(i["L0_ffn_w_gate_up"].T), by_partition(i["L0_ffn_w_down"].T)], 1),
        wq1=heads(i["L1_attn_Wq"]),
        wkv1=np.concatenate([heads(i["L1_attn_Wk"]), i["L1_attn_Wv"]], 1),
        bq1=heads(i["L1_attn_bq"][None, :]),
        bkv1=np.concatenate([heads(i["L1_attn_bk"][None, :]), i["L1_attn_bv"][None, :]], 1),
        wo1=i["L1_attn_Wo"],
        bo1=i["L1_attn_bo"][None, :],
        w_moe=np.concatenate([by_partition(np.concatenate([w1, w2], 1)), by_partition(w3)], 1),
        w_gate=i["L1_ffn_Wg"].T,
        **constants(),
    )
    arrays = {k: np.ascontiguousarray(v) for k, v in arrays.items()}
    nc = bacc.Bacc("TRN2", target_bir_lowering=False, num_devices=1)
    args = [nc.dram_tensor(k, v.shape, mybir.dt.from_np(v.dtype), kind="ExternalInput").ap()
            for k, v in arrays.items()]
    out = nc.dram_tensor("out", (NSEQ, T, E), F32, kind="ExternalOutput").ap()
    build(nc, *args, out)
    r = run(nc, [arrays], core_ids=[0])
    return r.results[0]["out"]
```
